# Optimizing a Trainium2 kernel written in Bass

```python
import numpy as np
import jax
import jax.numpy as jnp

def _softmax(x, axis=-1):
    return jax.nn.softmax(x, axis=axis)

def _gelu(x):
    return jax.nn.gelu(x, approximate=True)

def _silu(x):
    return jax.nn.silu(x)

def _sigmoid(x):
    return jax.nn.sigmoid(x)

def _layernorm(x, axis=-1, eps=1e-05):
    m = jnp.mean(x, axis=axis, keepdims=True)
    v = jnp.var(x, axis=axis, keepdims=True)
    return (x - m) / jnp.sqrt(v + eps)

def _scatter_add(tgt, idx, src, axis=0):
    return tgt.at[idx].add(src)

def _segment_sum(src, seg, n):
    return jax.ops.segment_sum(src, seg, n)
kernel_name = 'mk_gnn_ffn_d1_gnn_r8_016430'

def setup_inputs(seed: int=0):
    np.random.seed(seed)
    _w = jnp.asarray

    def _rec_inputs():
        import jax
        import jax.numpy as jnp
        _gk = jax.random.key(seed)
        x = -0.0002117 + 1 * jax.random.normal(jax.random.fold_in(_gk, 1), (12500, 256), jnp.float32)
        _s = jax.random.randint(jax.random.fold_in(_gk, 2), (100000,), 0, 12500, jnp.int32)
        _d = jax.random.randint(jax.random.fold_in(_gk, 3), (100000,), 0, 12500, jnp.int32)
        _loop = jnp.arange(12500, dtype=jnp.int32)
        src = jnp.concatenate([_s, _d, _loop])
        dst = jnp.concatenate([_d, _s, _loop])
        _o = jnp.argsort(dst, stable=True)
        src = src[_o]
        dst = dst[_o]
        edge_weight = jax.random.uniform(jax.random.fold_in(_gk, 13), (212500,), jnp.float32, 0.0, 1)
        return (x, src, dst, edge_weight)
    x, src, dst, edge_weight = _rec_inputs()

    def _L0_gnn_setup():
        import jax, jax.numpy as jnp
        import numpy as np
        N = 12500
        E = 400000
        D = 256
        key = jax.random.key(seed)
        ks = jax.random.split(key, 6)
        x = jax.random.normal(ks[0], (N, D), dtype=jnp.float32)
        row = jax.random.randint(ks[1], (E,), 0, N, dtype=jnp.int32)
        col = jax.random.randint(ks[2], (E,), 0, N, dtype=jnp.int32)
        values = jax.random.uniform(ks[3], (E,), dtype=jnp.float32)
        out_norm = jax.random.uniform(ks[4], (N, 1), dtype=jnp.float32)
        in_norm = jax.random.uniform(ks[5], (N, 1), dtype=jnp.float32)
        return {'x': x, 'row': row, 'col': col, 'values': values, 'out_norm': out_norm, 'in_norm': in_norm}
    _L0_gnn_all = _L0_gnn_setup()
    _L0_gnn_in = {k: v for k, v in _L0_gnn_all.items() if k in ()}
    del _L0_gnn_all

    def _L0_ffn_setup():
        import jax, jax.numpy as jnp
        import numpy as np
        B, N, D = (16, 512, 256)
        NUM_EXPERTS, TOP_K, HEADS = (4, 2, 4)
        N_EDGES = 131072
        LN_EPS = 1e-05

        def _layernorm(x, g, b):
            mu = x.mean(-1, keepdims=True)
            var = ((x - mu) ** 2).mean(-1, keepdims=True)
            return (x - mu) * jax.lax.rsqrt(var + LN_EPS) * g + b

        def _forward(x, edge_index, W_gat, att_src, att_dst, b_gat, ln_gamma, ln_beta, W1, b1, W2, b2):
            Bc, Nc, Dc = x.shape
            M = Bc * Nc
            x_flat = x.reshape(M, Dc)
            h = (x_flat @ W_gat).reshape(M, HEADS, NUM_EXPERTS)
            loops = jnp.arange(M, dtype=edge_index.dtype)
            src = jnp.concatenate([edge_index[0], loops])
            dst = jnp.concatenate([edge_index[1], loops])
            a_src = (h * att_src).sum(-1)
            a_dst = (h * att_dst).sum(-1)
            e = jax.nn.leaky_relu(a_src[src] + a_dst[dst], negative_slope=0.2)
            e_max = jax.ops.segment_max(e, dst, num_segments=M)
            ee = jnp.exp(e - e_max[dst])
            denom = jax.ops.segment_sum(ee, dst, num_segments=M)
            alpha = ee / (denom[dst] + 1e-16)
            msg = h[src] * alpha[:, :, None]
            agg = jax.ops.segment_sum(msg, dst, num_segments=M).reshape(M, HEADS * NUM_EXPERTS) + b_gat
            scores = _layernorm(agg, ln_gamma, ln_beta).reshape(M, HEADS, NUM_EXPERTS).mean(1)
            scores = scores.reshape(Bc, Nc, NUM_EXPERTS)
            topk_s, topk_i = jax.lax.top_k(scores, TOP_K)
            w = jax.nn.softmax(topk_s, axis=-1)
            out = jnp.zeros_like(x)
            for ei in range(NUM_EXPERTS):
                g = jnp.where(topk_i == ei, w, 0.0).sum(-1)
                hh = jax.nn.gelu(x @ W1[ei] + b1[ei], approximate=False)
                out = out + g[..., None] * (hh @ W2[ei] + b2[ei])
            return out
        key = jax.random.key(seed)
        ks = jax.random.split(key, 8)
        s = 0.05
        return {'x': jax.random.normal(ks[0], (B, N, D), jnp.float32), 'W_gat': jax.random.normal(ks[1], (D, HEADS * NUM_EXPERTS), jnp.float32) * s, 'att_src': jax.random.normal(ks[2], (HEADS, NUM_EXPERTS), jnp.float32) * s, 'att_dst': jax.random.normal(ks[3], (HEADS, NUM_EXPERTS), jnp.float32) * s, 'b_gat': jnp.zeros((HEADS * NUM_EXPERTS,), jnp.float32), 'ln_gamma': jnp.ones((HEADS * NUM_EXPERTS,), jnp.float32), 'ln_beta': jnp.zeros((HEADS * NUM_EXPERTS,), jnp.float32), 'W1': jax.random.normal(ks[4], (NUM_EXPERTS, D, 2 * D), jnp.float32) * s, 'b1': jnp.zeros((NUM_EXPERTS, 2 * D), jnp.float32), 'W2': jax.random.normal(ks[5], (NUM_EXPERTS, 2 * D, D), jnp.float32) * s, 'b2': jnp.zeros((NUM_EXPERTS, D), jnp.float32), 'edge_index': jax.random.randint(ks[6], (2, N_EDGES), 0, B * N, jnp.int32)}
    _L0_ffn_all = _L0_ffn_setup()
    _L0_ffn_in = {k: v for k, v in _L0_ffn_all.items() if k in ('W_gat', 'att_src', 'att_dst', 'b_gat', 'ln_gamma', 'ln_beta', 'W1', 'b1', 'W2', 'b2', 'edge_index')}
    del _L0_ffn_all
    return {'x': x, 'src': src, 'dst': dst, 'edge_weight': edge_weight, 'L0_ffn_W_gat': _L0_ffn_in['W_gat'], 'L0_ffn_att_src': _L0_ffn_in['att_src'], 'L0_ffn_att_dst': _L0_ffn_in['att_dst'], 'L0_ffn_b_gat': _L0_ffn_in['b_gat'], 'L0_ffn_ln_gamma': _L0_ffn_in['ln_gamma'], 'L0_ffn_ln_beta': _L0_ffn_in['ln_beta'], 'L0_ffn_W1': _L0_ffn_in['W1'], 'L0_ffn_b1': _L0_ffn_in['b1'], 'L0_ffn_W2': _L0_ffn_in['W2'], 'L0_ffn_b2': _L0_ffn_in['b2'], 'L0_ffn_edge_index': _L0_ffn_in['edge_index']}

def reference(x, src, dst, edge_weight, L0_ffn_W_gat, L0_ffn_att_src, L0_ffn_att_dst, L0_ffn_b_gat, L0_ffn_ln_gamma, L0_ffn_ln_beta, L0_ffn_W1, L0_ffn_b1, L0_ffn_W2, L0_ffn_b2, L0_ffn_edge_index):
    import jax
    import jax.numpy as jnp

    def _L0_gnn_ref(x, row, col, values, out_norm, in_norm):
        import jax, jax.numpy as jnp
        import numpy as np
        N = 12500
        E = 400000
        D = 256
        xs = out_norm * x
        msg = xs[col] * values[:, None]
        agg = jax.ops.segment_sum(msg, row, num_segments=N)
        return in_norm * agg

    def _L0_ffn_ref(x, W_gat, att_src, att_dst, b_gat, ln_gamma, ln_beta, W1, b1, W2, b2, edge_index):
        import jax, jax.numpy as jnp
        import numpy as np
        B, N, D = (16, 512, 256)
        NUM_EXPERTS, TOP_K, HEADS = (4, 2, 4)
        N_EDGES = 131072
        LN_EPS = 1e-05

        def _layernorm(x, g, b):
            mu = x.mean(-1, keepdims=True)
            var = ((x - mu) ** 2).mean(-1, keepdims=True)
            return (x - mu) * jax.lax.rsqrt(var + LN_EPS) * g + b

        def _forward(x, edge_index, W_gat, att_src, att_dst, b_gat, ln_gamma, ln_beta, W1, b1, W2, b2):
            Bc, Nc, Dc = x.shape
            M = Bc * Nc
            x_flat = x.reshape(M, Dc)
            h = (x_flat @ W_gat).reshape(M, HEADS, NUM_EXPERTS)
            loops = jnp.arange(M, dtype=edge_index.dtype)
            src = jnp.concatenate([edge_index[0], loops])
            dst = jnp.concatenate([edge_index[1], loops])
            a_src = (h * att_src).sum(-1)
            a_dst = (h * att_dst).sum(-1)
            e = jax.nn.leaky_relu(a_src[src] + a_dst[dst], negative_slope=0.2)
            e_max = jax.ops.segment_max(e, dst, num_segments=M)
            ee = jnp.exp(e - e_max[dst])
            denom = jax.ops.segment_sum(ee, dst, num_segments=M)
            alpha = ee / (denom[dst] + 1e-16)
            msg = h[src] * alpha[:, :, None]
            agg = jax.ops.segment_sum(msg, dst, num_segments=M).reshape(M, HEADS * NUM_EXPERTS) + b_gat
            scores = _layernorm(agg, ln_gamma, ln_beta).reshape(M, HEADS, NUM_EXPERTS).mean(1)
            scores = scores.reshape(Bc, Nc, NUM_EXPERTS)
            topk_s, topk_i = jax.lax.top_k(scores, TOP_K)
            w = jax.nn.softmax(topk_s, axis=-1)
            out = jnp.zeros_like(x)
            for ei in range(NUM_EXPERTS):
                g = jnp.where(topk_i == ei, w, 0.0).sum(-1)
                hh = jax.nn.gelu(x @ W1[ei] + b1[ei], approximate=False)
                out = out + g[..., None] * (hh @ W2[ei] + b2[ei])
            return out
        return _forward(x, edge_index, W_gat, att_src, att_dst, b_gat, ln_gamma, ln_beta, W1, b1, W2, b2)
    deg = jnp.maximum(jax.ops.segment_sum(jnp.ones(dst.shape, jnp.float32), dst, num_segments=12500), 1.0)
    deg_isqrt = deg ** (-0.5)
    x = x + _L0_gnn_ref(_layernorm(x, axis=-1), src, dst, edge_weight, deg_isqrt[:, None], deg_isqrt[:, None])
    x = x + _L0_ffn_ref(_layernorm(x, axis=-1)[None], L0_ffn_W_gat, L0_ffn_att_src, L0_ffn_att_dst, L0_ffn_b_gat, L0_ffn_ln_gamma, L0_ffn_ln_beta, L0_ffn_W1, L0_ffn_b1, L0_ffn_W2, L0_ffn_b2, L0_ffn_edge_index)[0]
    return x

_drawn_inputs = setup_inputs


def setup_inputs(seed=0):
    import zlib

    import numpy as np

    out = dict(_drawn_inputs(seed))
    spreads = {'L0_ffn_b_gat': (0.0, 0.1),
     'L0_ffn_ln_gamma': (1.0, 0.2),
     'L0_ffn_ln_beta': (0.0, 0.1),
     'L0_ffn_b1': (0.0, 0.1),
     'L0_ffn_b2': (0.0, 0.1)}
    factors = {}
    for name, (base, spread) in spreads.items():
        noise = np.random.default_rng([zlib.crc32(name.encode()), seed]).standard_normal(out[name].shape)
        drawn = base * np.exp(spread * noise) if base else spread * noise
        out[name] = jnp.asarray(drawn.astype(out[name].dtype))
    for name, factor in factors.items():
        out[name] = (out[name] * factor).astype(out[name].dtype)
    return out
```

```python
import concourse.bass as bass
from concourse import mybir
from contextlib import ExitStack

F32 = mybir.dt.float32
BF16 = mybir.dt.bfloat16
I32 = mybir.dt.int32
ALU = mybir.AluOpType
ACT = mybir.ActivationFunctionType
AX = mybir.AxisListType

P = 128
LOG_P = 7
N = 12500
D = 256
NT = -(-N // P)
NP = NT * P
LAST = N - (NT - 1) * P
HEADS, EXPERTS = 4, 4
HE = HEADS * EXPERTS
FF = 512
LN_EPS = 1e-5
GROUP = 8
TG = 7
SORT_COLS = 16
SORT_EDGES = SORT_COLS * P
NO_EDGE = -1.0e30
TAB = HE + HEADS


class EdgeList:

    def __init__(self, name, edges, cols, words):
        self.name, self.edges, self.cols, self.words = name, edges, cols, words
        self.buckets = NT + (cols * P > edges)
        most = (cols * P + self.buckets * (P - 1)) // P
        self.chunks = -(-most // (2 * GROUP)) * 2 * GROUP
        self.steps = cols // SORT_COLS
        assert cols % (2 * SORT_COLS) == 0 and cols % P == 0 and cols * P >= edges


def wait(eng, sem, value):
    if not isinstance(value, int) or value > 0:
        eng.wait_ge(sem, value)


def peeled(eng, steps, body):
    body(0)
    if steps > 1:
        with eng.Fori(1, steps) as i:
            body(i)


class Chain:

    def __init__(self, eng, sem):
        self.eng, self.sem, self.count, self.loop = eng, sem, 0, 0

    def step(self, ins):
        ins.then_inc(self.sem, 1)
        self.count += 1
        self.eng.wait_ge(self.sem, self.loop + self.count)

    def put(self, ins):
        ins.then_inc(self.sem, 1)
        self.count += 1

    def settle(self):
        self.eng.wait_ge(self.sem, self.loop + self.count)

    def peeled(self, steps, body):
        start = self.count
        body(0)
        per = self.count - start
        if steps > 1:
            with self.eng.Fori(1, steps) as i:
                self.loop = i * per - per
                body(i)
                assert self.count - start == 2 * per
        self.count, self.loop = start + per * steps, 0


def build(nc, x, src, dst, edge_weight, W_gat, att_src, att_dst, b_gat, ln_gamma, ln_beta,
          W1, b1, W2, b2, edge_index, out, stage="all"):
    gnn = EdgeList("gnn", src.shape[0], 1664, 3)
    gat = EdgeList("gat", edge_index.shape[1], 1024, 2)
    top = ExitStack()
    with top:
        def keep(name, shape, dt):
            return top.enter_context(nc.sbuf_tensor(name, shape, dt))

        def dram(name, shape, dt):
            return nc.dram_tensor(name, shape, dt, kind="Internal").ap()

        xs_d = dram("xs_d", (NP, D), F32)
        x1_d = dram("x1_d", (NP, D), F32)
        ut_d = [dram(f"ut_d{k}", (P, NP), F32) for k in range(2)]
        tab_d = dram("tab_d", (NP + 1, TAB), F32)
        bucket_d = {s.name: dram(f"bucket_{s.name}", (s.cols, P), BF16) for s in (gnn, gat)}
        rec_d = {s.name: dram(f"rec_{s.name}", (P * s.chunks, s.words), F32) for s in (gnn, gat)}

        pidx = keep("pidx", [P, 1], F32)
        iota_i = keep("iota_i", [P, P], I32)
        pidx_i = keep("pidx_i", [P, 1], I32)
        iota_f = keep("iota_f", [P, P], F32)
        iota_b = keep("iota_b", [P, P], BF16)
        ident = keep("ident", [P, P], F32)
        ident_b = keep("ident_b", [P, P], BF16)
        later = keep("later", [P, P], F32)
        ones_b = keep("ones_b", [P, 1], BF16)
        ones_f = keep("ones_f", [P, 1], F32)
        dis = keep("dis", [P, NT], F32)
        chunk_tile = {s.name: keep(f"chunk_tile_{s.name}", [1, s.chunks], I32) for s in (gnn, gat)}

        constants(nc, pidx, pidx_i, iota_i, iota_f, iota_b, ident, ident_b, later, ones_b, ones_f)
        C = dict(pidx=pidx, iota_f=iota_f, iota_b=iota_b, ident=ident, ident_b=ident_b, later=later,
                 ones_b=ones_b, ones_f=ones_f)
        degrees(nc, gnn, dst, dis, C)
        scaled_layernorm(nc, x, xs_d, dis)
        edge_sort(nc, gnn, src, dst, edge_weight, bucket_d["gnn"], rec_d["gnn"], chunk_tile["gnn"], C)
        edge_sort(nc, gat, edge_index[1], edge_index[0], None, bucket_d["gat"], rec_d["gat"],
                  chunk_tile["gat"], C)
        neighbour_sum(nc, gnn, x, xs_d, rec_d["gnn"], chunk_tile["gnn"], dis, x1_d, C)
        if stage == "x1":
            copy_out(nc, x1_d, out)
            return
        nodes = dict(T=keep("T", [P, NT, 2 * HEADS], F32),
                     own=keep("own", [P, NT, TAB], F32),
                     asd=keep("asd", [P, NT, HEADS], F32),
                     top=keep("top", [P, NT, HEADS], F32),
                     gate=keep("gate", [P, NT, EXPERTS], F32))
        router_table(nc, x1_d, ut_d, W_gat, att_src, att_dst, tab_d, nodes, C)
        attention(nc, gat, tab_d, rec_d["gat"], chunk_tile["gat"], nodes, b_gat, ln_gamma, ln_beta, C)
        if stage == "gate":
            with nc.semaphore("gate_out") as gate_out, nc.Block() as block:
                @block.sync
                def _(sp):
                    sp.dma_start(out, nodes["gate"][:, :, :].rearrange("p a b -> p (a b)")).then_inc(gate_out, 16)
                    sp.wait_ge(gate_out, 16)
            return
        experts(nc, x1_d, ut_d, W1, b1, W2, b2, nodes["gate"], out, C)


def copy_out(nc, x1_d, out):
    with nc.semaphore("copied") as copied, nc.Block() as block:
        @block.sync
        def _(sp):
            sp.dma_start(out, x1_d[0:N, :]).then_inc(copied, 16)
            sp.wait_ge(copied, 16)


def constants(nc, pidx, pidx_i, iota_i, iota_f, iota_b, ident, ident_b, later, ones_b, ones_f):
    with nc.semaphore("counted") as counted, nc.semaphore("const_chain") as chain_sem, nc.Block() as block:
        @block.gpsimd
        def _(pool):
            pool.iota(iota_i[:], pattern=[[1, P]], base=0, channel_multiplier=0).then_inc(counted, 1)
            pool.iota(pidx_i[:], pattern=[[0, 1]], base=0, channel_multiplier=1).then_inc(counted, 1)

        @block.vector
        def _(dve):
            chain = Chain(dve, chain_sem)
            dve.memset(ones_b[:], 1.0)
            dve.memset(ones_f[:], 1.0)
            dve.wait_ge(counted, 2)
            chain.put(dve.tensor_copy(iota_f[:], iota_i[:]))
            chain.put(dve.tensor_copy(iota_b[:], iota_i[:]))
            chain.put(dve.tensor_copy(pidx[:], pidx_i[:]))
            chain.settle()
            dve.tensor_scalar(ident[:], iota_f[:], pidx[:, 0:1], None, ALU.is_equal)
            dve.tensor_scalar(ident_b[:], iota_f[:], pidx[:, 0:1], None, ALU.is_equal)
            dve.tensor_scalar(later[:], iota_f[:], pidx[:, 0:1], None, ALU.is_gt)


def load_edges(eng, s, tile, array, sem):
    full = s.edges // s.cols
    if full == P:
        eng.dma_start(tile[:, :], array.rearrange("(p c) -> p c", p=P)).then_inc(sem, 16)
        return 16
    assert full == P - 1
    eng.dma_start(tile[0:full, :], array[0:full * s.cols].rearrange("(p c) -> p c", p=full)).then_inc(sem, 16)
    rest = s.edges - full * s.cols
    eng.dma_start(tile[full:P, 0:rest], array[full * s.cols:s.edges].rearrange("(p c) -> p c", p=1)).then_inc(sem, 16)
    return 32


def degrees(nc, s, dst, dis, C):
    steps = s.cols // GROUP
    with ExitStack() as ctx:
        sb = lambda n, sh, dt: ctx.enter_context(nc.sbuf_tensor(n, sh, dt))
        sem = lambda n: ctx.enter_context(nc.semaphore(n))
        key = sb("deg_key", [P, s.cols], I32)
        digit = sb("deg_digit", [P, s.cols], I32)
        hi = sb("deg_hi", [P, s.cols], BF16)
        lo = sb("deg_lo", [P, s.cols], BF16)
        one_hi = sb("deg_one_hi", [P, 2, GROUP, NT], BF16)
        one_lo = sb("deg_one_lo", [P, 2, GROUP, P], BF16)
        zeros = sb("deg_zeros", [P, P], BF16)
        deg = sb("deg_deg", [P, NT], F32)
        root = sb("deg_root", [P, NT], F32)
        hist = ctx.enter_context(nc.psum_tensor("deg_hist", [P, NT], F32))
        filled, loaded, chain_sem = sem("deg_filled"), sem("deg_loaded"), sem("deg_chain")
        coded, counted, total, rooted, clipped = (sem("deg_coded"), sem("deg_counted"), sem("deg_total"),
                                                  sem("deg_rooted"), sem("deg_clipped"))
        block = ctx.enter_context(nc.Block())

        @block.sync
        def _(sp):
            sp.wait_ge(filled, 1)
            load_edges(sp, s, key, dst, loaded)

        @block.vector
        def _(dve):
            chain = Chain(dve, chain_sem)
            dve.memset(key[:], NP).then_inc(filled, 1)
            dve.memset(zeros[:], 0.0).then_inc(filled, 1)
            dve.wait_ge(loaded, 32)
            chain.step(dve.tensor_scalar(digit[:], key[:], LOG_P, None, ALU.logical_shift_right))
            chain.step(dve.tensor_copy(hi[:], digit[:]))
            chain.step(dve.tensor_scalar(digit[:], key[:], P - 1, None, ALU.bitwise_and))
            chain.step(dve.tensor_copy(lo[:], digit[:]))

            def body(i):
                for slot in range(2):
                    wait(dve, counted, 2 * i + slot - 1)
                    cols = bass.ds(i * 2 * GROUP + slot * GROUP, GROUP)
                    dve.tensor_tensor(one_hi[:, slot], C["iota_b"][:, 0:NT].unsqueeze(1).to_broadcast([P, GROUP, NT]),
                                      hi[:, cols].unsqueeze(2).to_broadcast([P, GROUP, NT]),
                                      ALU.is_equal).then_inc(coded, 1)
                    dve.tensor_tensor(one_lo[:, slot], C["iota_b"][:, :].unsqueeze(1).to_broadcast([P, GROUP, P]),
                                      lo[:, cols].unsqueeze(2).to_broadcast([P, GROUP, P]),
                                      ALU.is_equal).then_inc(coded, 1)
            peeled(dve, steps // 2, body)
            dve.wait_ge(total, 1)
            chain.step(dve.tensor_scalar(deg[:], hist[:], 1.0, None, ALU.max))
            dve.sem_inc(clipped, 1)
            dve.wait_ge(rooted, 1)
            dve.reciprocal(dis[:], root[:])

        @block.tensor
        def _(pe):
            pe.wait_ge(filled, 2)
            pe.matmul(hist[:], zeros[:], zeros[:, 0:NT], start=True, stop=False)

            def body(i):
                for slot in range(2):
                    pe.wait_ge(coded, i * 4 + slot * 2 + 2)
                    for g in range(GROUP):
                        last = pe.matmul(hist[:], one_lo[:, slot, g], one_hi[:, slot, g], start=False, stop=False)
                    last.then_inc(counted, 1)
            peeled(pe, steps // 2, body)
            pe.matmul(hist[:], zeros[:], zeros[:, 0:NT], start=False, stop=True).then_inc(total, 1)

        @block.scalar
        def _(act):
            act.wait_ge(clipped, 1)
            act.activation(root[:], deg[:], ACT.Sqrt).then_inc(rooted, 1)


def layernorm_stats(dve, chain, tiles, stats, mv, k0=0):
    for k in range(tiles.shape[1]):
        chain.put(dve.bn_stats(stats[:, k], tiles[:, k]))
    chain.settle()
    dve.nop(nofuse=True)
    for k in range(tiles.shape[1]):
        chain.put(dve.bn_aggr(mv[:, k], stats[:, k]))
    chain.settle()


def node_rows(array, i):
    return array[bass.ds(i * TG * P, TG * P), :].rearrange("(t p) f -> p t f", p=P)


def load_nodes(sp, tile, x, i, last, sem):
    if not last:
        sp.dma_start(tile, node_rows(x, i)).then_inc(sem, 32)
    else:
        base = i * TG * P
        whole = base + (TG - 1) * P
        sp.dma_start(tile[:, 0:TG - 1], x[base:whole, :].rearrange("(t p) f -> p t f", p=P)).then_inc(sem, 16)
        sp.dma_start(tile[0:LAST, TG - 1], x[whole:N, :]).then_inc(sem, 16)


def scaled_layernorm(nc, x, xs_d, dis):
    steps = NT // TG
    with ExitStack() as ctx:
        sb = lambda n, sh, dt: ctx.enter_context(nc.sbuf_tensor(n, sh, dt))
        sem = lambda n: ctx.enter_context(nc.semaphore(n))
        xin = sb("sl_x", [P, 2, TG, D], F32)
        xout = sb("sl_out", [P, 2, TG, D], F32)
        stats = sb("sl_stats", [P, TG, 6], F32)
        mv = sb("sl_mv", [P, TG, 2], F32)
        var = sb("sl_var", [P, TG], F32)
        root = sb("sl_root", [P, TG], F32)
        scale = sb("sl_scale", [P, TG], F32)
        loaded = [sem("sl_loaded0"), sem("sl_loaded1")]
        stored = [sem("sl_stored0"), sem("sl_stored1")]
        chain_sem, ready, rooted, normed, cleared = (sem("sl_chain"), sem("sl_var_ready"), sem("sl_rooted"),
                                                     sem("sl_normed"), sem("sl_cleared"))
        block = ctx.enter_context(nc.Block())

        @block.sync
        def _(sp):
            def one(i, slot, last=False):
                step = i * 2 + slot
                wait(sp, normed, TG * (step - 1))
                load_nodes(sp, xin[:, slot], x, step, last, loaded[slot])

            def body(i):
                one(i, 0)
                one(i, 1)
            peeled(sp, steps // 2 - 1, body)
            one(steps // 2 - 1, 0)
            sp.wait_ge(cleared, 1)
            one(steps // 2 - 1, 1, last=True)

        @block.vector
        def _(dve):
            chain = Chain(dve, chain_sem)

            def one(i, slot):
                step = i * 2 + slot
                dve.wait_ge(loaded[slot], i * 32 + 32)
                layernorm_stats(dve, chain, xin[:, slot], stats, mv)
                chain.put(dve.tensor_scalar(var[:], mv[:, :, 1], LN_EPS, None, ALU.add))
                chain.settle()
                dve.tensor_copy(var[:], var[:]).then_inc(ready, 1)
                dve.wait_ge(rooted, step + 1)
                chain.step(dve.reciprocal(scale[:], root[:]))
                chain.step(dve.tensor_tensor(scale[:], scale[:], dis[:, bass.ds(step * TG, TG)], ALU.mult))
                wait(dve, stored[slot], 16 * i)
                for k in range(TG):
                    dve.tensor_scalar(xout[:, slot, k], xin[:, slot, k], mv[:, k, 0:1], scale[:, k:k + 1],
                                      ALU.subtract, ALU.mult).then_inc(normed, 1)
                dve.wait_ge(normed, TG * step + TG)

            def body(i):
                one(i, 0)
                one(i, 1)
            chain.peeled(steps // 2 - 1, body)
            one(steps // 2 - 1, 0)
            dve.memset(xin[:, 1, TG - 1], 0.0).then_inc(cleared, 1)
            one(steps // 2 - 1, 1)

        @block.scalar
        def _(act):
            def body(i):
                for slot in range(2):
                    act.wait_ge(ready, i * 2 + slot + 1)
                    act.activation(root[:], var[:], ACT.Sqrt).then_inc(rooted, 1)
                    act.wait_ge(normed, TG * (i * 2 + slot + 1))
                    act.dma_start(node_rows(xs_d, i * 2 + slot), xout[:, slot]).then_inc(stored[slot], 16)
            peeled(act, steps // 2, body)
            for slot in range(2):
                act.wait_ge(stored[slot], 16 * (steps // 2))


def edge_sort(nc, s, key_a, other_a, weight_a, bucket_d, rec_d, chunk_tile, C):
    B, W, NC = s.buckets, s.words, s.chunks
    blocks = s.cols // P
    with ExitStack() as ctx:
        sb = lambda n, sh, dt: ctx.enter_context(nc.sbuf_tensor(f"{s.name}_{n}", sh, dt))
        ps = lambda n, sh, dt: ctx.enter_context(nc.psum_tensor(f"{s.name}_{n}", sh, dt))
        sem = lambda n: ctx.enter_context(nc.semaphore(f"{s.name}_{n}"))
        fields = sb("fields", [P, s.cols, W], F32)
        empty = sb("empty", [P, NC, W], F32)
        tmp = ExitStack()
        key = tmp.enter_context(nc.sbuf_tensor(f"{s.name}_key", [P, s.cols], I32))
        other = tmp.enter_context(nc.sbuf_tensor(f"{s.name}_other", [P, s.cols], I32))
        weight = tmp.enter_context(nc.sbuf_tensor(f"{s.name}_weight", [P, s.cols], F32)) if weight_a is not None else None
        digit = tmp.enter_context(nc.sbuf_tensor(f"{s.name}_digit", [P, s.cols], I32))
        hi = tmp.enter_context(nc.sbuf_tensor(f"{s.name}_hi", [P, s.cols], F32))
        hi_t = tmp.enter_context(nc.sbuf_tensor(f"{s.name}_hi_t", [P, blocks, P], BF16))

        with ExitStack() as c1:
            sem1 = lambda n: c1.enter_context(nc.semaphore(f"{s.name}_{n}"))
            pt = c1.enter_context(nc.psum_tensor(f"{s.name}_pt", [P, 2, 512], F32))
            filled, loaded, chain_sem, split, turned, taken, saved, blank = (
                sem1("filled"), sem1("loaded"), sem1("chain1"), sem1("split"), sem1("turned"), sem1("taken"),
                sem1("saved"), sem1("blank"))
            block = c1.enter_context(nc.Block())

            @block.sync
            def _(sp):
                sp.wait_ge(filled, 3)
                load_edges(sp, s, key, key_a, loaded)
                load_edges(sp, s, other, other_a, loaded)
                if weight is not None:
                    load_edges(sp, s, weight, weight_a, loaded)
                sp.wait_ge(blank, 1)
                sp.dma_start(rec_d.rearrange("(p c) w -> p (c w)", p=P),
                             empty[:, :, :].rearrange("p c w -> p (c w)")).then_inc(saved, 16)
                sp.wait_ge(taken, blocks)
                sp.dma_start(bucket_d.rearrange("(b t) p -> t b p", t=P), hi_t[:]).then_inc(saved, 16)
                sp.wait_ge(saved, 32)

            @block.vector
            def _(dve):
                chain = Chain(dve, chain_sem)
                dve.memset(key[:], NP).then_inc(filled, 1)
                dve.memset(other[:], 0).then_inc(filled, 1)
                if weight is not None:
                    dve.memset(weight[:], 0.0).then_inc(filled, 1)
                    chain.step(dve.memset(empty[:], 0.0))
                else:
                    chain.step(dve.memset(empty[:], 0.0))
                    chain.step(dve.memset(empty[:, :, 0], float(NP)))
                    dve.memset(digit[:], 0).then_inc(filled, 1)
                dve.memset(pt[:, 0, 0:1], 0.0).then_inc(blank, 1)
                per = 16 if s.edges == s.cols * P else 32
                dve.wait_ge(loaded, per * W)
                dve.wait_ge(filled, 3)
                chain.step(dve.tensor_scalar(digit[:], key[:], LOG_P, None, ALU.logical_shift_right))
                dve.tensor_copy(hi[:], digit[:]).then_inc(split, 1)
                dve.wait_ge(split, 1)
                chain.step(dve.tensor_scalar(digit[:], key[:], P - 1, None, ALU.bitwise_and))
                dve.tensor_copy(fields[:, :, 1], digit[:])
                dve.tensor_copy(fields[:, :, 0], other[:])
                if weight is not None:
                    dve.tensor_copy(fields[:, :, 2], weight[:])
                for b in range(blocks):
                    dve.wait_ge(turned, b + 1)
                    dve.tensor_copy(hi_t[:, b], pt[:, b % 2, 0:P]).then_inc(taken, 1)

            @block.tensor
            def _(pe):
                pe.wait_ge(blank, 1)
                pe.wait_ge(split, 1)
                for b in range(blocks):
                    wait(pe, taken, b - 1)
                    pe.transpose(pt[:, b % 2, 0:P], hi[:, b * P:(b + 1) * P], C["ident"][:]).then_inc(turned, 1)
        tmp.close()

        keys = sb("keys", [P, 2, SORT_EDGES], BF16)
        match = sb("match", [P, 2, SORT_EDGES], BF16)
        run = sb("run", [P, 2, SORT_EDGES], F32)
        slots = sb("slots", [P, 2, SORT_EDGES], F32)
        count = sb("count", [P, 4], F32)
        small_i = sb("small_i", [P, 2], I32)
        need_f = sb("need_f", [P, 1], F32)
        first_f = sb("first_f", [P, 1], F32)
        end_f = sb("end_f", [P, 1], F32)
        chunk_no_i = sb("chunk_no_i", [P, NC], I32)
        past = sb("past", [P, NC], BF16)
        place = sb("place", [P, SORT_COLS], I32)
        lane = sb("lane", [P, SORT_COLS], I32)
        index = sb("index", [P, 2, SORT_COLS], I32)
        record = sb("record", [P, 2, SORT_COLS, W], F32)
        first_ps = ps("first_ps", [P, 1], F32)
        tile_ps = ps("tile_ps", [1, 512], F32)
        pos_ps = ps("pos_ps", [P, 2, 512], F32)
        keys_in = [sem("keys_in0"), sem("keys_in1")]
        keys_used, chain_sem, chunk_no = sem("keys_used"), sem("chain2"), sem("chunk_no")
        needed, started, pasted, tiled, tiles_read = (sem("needed"), sem("started"), sem("pasted"), sem("tiled"),
                                                      sem("tiles_read"))
        masked, summed, placed, staged = sem("masked"), sem("summed"), sem("placed"), sem("staged")
        scattered = [sem("scattered0"), sem("scattered1")]
        block = ctx.enter_context(nc.Block())
        flat = bucket_d.rearrange("c p -> (c p)")

        @block.sync
        def _(sp):
            def sweep(base):
                def body(i):
                    for slot in range(2):
                        step = i * 2 + slot
                        wait(sp, keys_used, base + step - 1)
                        sp.dma_start(keys[0:B, slot], flat[bass.ds(step * SORT_EDGES, SORT_EDGES)]
                                     .partition_broadcast(B)).then_inc(keys_in[slot], 16)
                return body
            peeled(sp, s.steps // 2, sweep(0))
            for slot in range(2):
                sp.wait_ge(keys_used, s.steps - 1 + slot)
                sp.dma_start(keys[0:B, slot], flat[slot * SORT_EDGES:(slot + 1) * SORT_EDGES]
                             .partition_broadcast(B)).then_inc(keys_in[slot], 16)
            with sp.Fori(1, s.steps // 2) as i:
                sweep(s.steps)(i)

        @block.gpsimd
        def _(pool):
            pool.iota(chunk_no_i[:], pattern=[[1, NC]], base=0, channel_multiplier=0).then_inc(chunk_no, 1)

            def body(i):
                for slot in range(2):
                    pool.wait_ge(placed, 2 * i + slot + 1)
                    pool.wait_ge(staged, 2 * i + slot + 1)
                    pool.nop(nofuse=True)
                    for c in range(SORT_COLS):
                        pool.indirect_dma_start(rec_d, bass.IndirectOffsetOnAxis(ap=index[:, slot, c:c + 1], axis=0),
                                                record[:, slot, c], None).then_inc(scattered[slot], 16)
            peeled(pool, s.steps // 2, body)
            for slot in range(2):
                pool.wait_ge(scattered[slot], 16 * SORT_COLS * (s.steps // 2))

        @block.scalar
        def _(act):
            def body(i):
                for slot in range(2):
                    wait(act, scattered[slot], 16 * SORT_COLS * i)
                    act.activation(record[:, slot], fields[:, bass.ds((i * 2 + slot) * SORT_COLS, SORT_COLS), :],
                                   ACT.Copy).then_inc(staged, 1)
            peeled(act, s.steps // 2, body)

        @block.tensor
        def _(pe):
            pe.wait_ge(needed, 1)
            pe.matmul(first_ps[0:B, :], C["later"][0:B, 0:B], need_f[0:B, :], start=True, stop=True).then_inc(started, 1)
            pe.wait_ge(pasted, 1)
            for n, c in enumerate(range(0, NC, 512)):
                w = min(512, NC - c)
                wait(pe, tiles_read, n)
                pe.matmul(tile_ps[:, 0:w], C["ones_b"][0:B, :], past[0:B, c:c + w], start=True, stop=True).then_inc(tiled, 1)

            def body(i):
                for slot in range(2):
                    pe.wait_ge(masked, 2 * i + slot + 1)
                    for c in range(SORT_COLS):
                        last = pe.matmul(pos_ps[:, slot, c:c + 1], slots[0:B, slot, c * P:(c + 1) * P],
                                         C["ones_f"][0:B, :], start=True, stop=True)
                    last.then_inc(summed, 1)
            peeled(pe, s.steps // 2, body)

        @block.vector
        def _(dve):
            chain = Chain(dve, chain_sem)
            for k in range(2):
                chain.put(dve.memset(count[:, 2 * k:2 * k + 2], 0.0))
            chain.settle()

            def counts(i):
                for slot in range(2):
                    dve.wait_ge(keys_in[slot], i * 16 + 16)
                    dve.tensor_scalar(match[0:B, slot], keys[0:B, slot], C["pidx"][0:B, 0:1], None, ALU.is_equal,
                                      ALU.add, accum_out=count[0:B, slot:slot + 1]).then_inc(keys_used, 1)
                    dve.wait_ge(keys_used, 2 * i + slot + 1)
                    chain.step(dve.tensor_tensor(count[0:B, 2:3], count[0:B, 2:3], count[0:B, slot:slot + 1], ALU.add))
            chain.peeled(s.steps // 2, counts)
            chain.step(dve.tensor_scalar(small_i[0:B, 0:1], count[0:B, 2:3], float(P - 1), None, ALU.add))
            chain.step(dve.tensor_scalar(small_i[0:B, 1:2], small_i[0:B, 0:1], LOG_P, None, ALU.logical_shift_right))
            dve.tensor_copy(need_f[0:B, :], small_i[0:B, 1:2]).then_inc(needed, 1)
            dve.wait_ge(started, 1)
            chain.put(dve.tensor_scalar(run[0:B, 1, SORT_EDGES - 1:SORT_EDGES], first_ps[0:B, :], float(P), -1.0,
                                        ALU.mult, ALU.add))
            chain.step(dve.tensor_tensor(end_f[0:B, :], first_ps[0:B, :], need_f[0:B, :], ALU.add))
            dve.wait_ge(chunk_no, 1)
            dve.tensor_scalar(past[0:B, :], chunk_no_i[0:B, :], end_f[0:B, 0:1], None, ALU.is_ge).then_inc(pasted, 1)
            for n, c in enumerate(range(0, NC, 512)):
                w = min(512, NC - c)
                dve.wait_ge(tiled, n + 1)
                dve.tensor_scalar(chunk_tile[:, c:c + w], tile_ps[:, 0:w], float(NT - 1), None,
                                  ALU.min).then_inc(tiles_read, 1)

            def ranks(i):
                for slot in range(2):
                    dve.wait_ge(keys_in[slot], i * 16 + 16 + 16 * (s.steps // 2))
                    dve.tensor_scalar(match[0:B, slot], keys[0:B, slot], C["pidx"][0:B, 0:1], None,
                                      ALU.is_equal).then_inc(keys_used, 1)
                    dve.wait_ge(keys_used, s.steps + 2 * i + slot + 1)
                    chain.step(dve.tensor_tensor_scan(run[0:B, slot], match[0:B, slot], match[0:B, slot],
                                                      run[0:B, 1 - slot, SORT_EDGES - 1:SORT_EDGES], ALU.add, ALU.max))
                    wait(dve, summed, 2 * i + slot - 1)
                    dve.tensor_tensor(slots[0:B, slot], run[0:B, slot], match[0:B, slot], ALU.mult).then_inc(masked, 1)
                    dve.wait_ge(summed, 2 * i + slot + 1)
                    chain.step(dve.tensor_copy(place[:], pos_ps[:, slot, 0:SORT_COLS]))
                    chain.step(dve.tensor_scalar(lane[:], place[:], P - 1, None, ALU.bitwise_and))
                    chain.step(dve.tensor_scalar(place[:], place[:], LOG_P, None, ALU.logical_shift_right))
                    wait(dve, scattered[slot], 16 * SORT_COLS * i)
                    dve.scalar_tensor_tensor(out=index[:, slot], in0=lane[:], scalar=float(NC), in1=place[:],
                                             op0=ALU.mult, op1=ALU.add).then_inc(placed, 1)
                    dve.wait_ge(placed, 2 * i + slot + 1)
            chain.peeled(s.steps // 2, ranks)


def neighbour_sum(nc, s, x, xs_d, rec_d, chunk_tile, dis, x1_d, C):
    NC, W = s.chunks, s.words
    pairs = NC // (2 * GROUP)
    with ExitStack() as ctx:
        sb = lambda n, sh, dt: ctx.enter_context(nc.sbuf_tensor(f"ns_{n}", sh, dt))
        sem = lambda n: ctx.enter_context(nc.semaphore(f"ns_{n}"))
        rec = sb("rec", [P, NC, W], F32)
        agg = sb("agg", [P, NT, D], F32)
        got = sb("got", [P, 2, GROUP, D], F32)
        spread = sb("spread", [P, 2, GROUP, P], F32)
        index = sb("index", [P, 2, GROUP], I32)
        field = sb("field", [P, 2, GROUP, 2], F32)
        part = ctx.enter_context(nc.psum_tensor("ns_part", [P, 4, 512], F32))
        rec_in, cleared, indexed, added, spreads, multiplied, chain_sem = (
            sem("rec_in"), sem("cleared"), sem("indexed"), sem("added"), sem("spreads"), sem("multiplied"), sem("chain"))
        gathered = [sem("gathered0"), sem("gathered1")]
        xin = sb("xin", [P, 2, TG, D], F32)
        x_in = [sem("x_in0"), sem("x_in1")]
        x_out = [sem("x_out0"), sem("x_out1")]
        summed = sem("summed")
        block = ctx.enter_context(nc.Block())
        steps = NT // TG

        @block.sync
        def _(sp):
            sp.dma_start(rec[:, :, :].rearrange("p c w -> p (c w)"),
                         rec_d.rearrange("(p c) w -> p (c w)", p=P)).then_inc(rec_in, 16)
            sp.wait_ge(cleared, 2)
            def one(i, slot, last=False):
                if isinstance(i, int) and i == 0:
                    pass
                else:
                    sp.wait_ge(x_out[slot], 16 * i)
                load_nodes(sp, xin[:, slot], x, i * 2 + slot, last, x_in[slot])

            def body(i):
                one(i, 0)
                one(i, 1)
            peeled(sp, steps // 2 - 1, body)
            one(steps // 2 - 1, 0)
            one(steps // 2 - 1, 1, last=True)

        @block.gpsimd
        def _(pool):
            def body(i):
                for slot in range(2):
                    wait(pool, multiplied, GROUP * (2 * i + slot - 1))
                    pool.wait_ge(indexed, 2 * (2 * i + slot + 1))
                    pool.nop(nofuse=True)
                    for g in range(GROUP):
                        pool.indirect_dma_start(got[:, slot, g], None, xs_d,
                                                bass.IndirectOffsetOnAxis(ap=index[:, slot, g:g + 1], axis=0)
                                                ).then_inc(gathered[slot], 16)
            peeled(pool, pairs, body)

        @block.scalar
        def _(act):
            act.wait_ge(rec_in, 16)

            def body(i):
                for slot in range(2):
                    chunks = bass.ds((i * 2 + slot) * GROUP, GROUP)
                    wait(act, gathered[slot], 16 * GROUP * i)
                    act.activation(index[:, slot], rec[:, chunks, 0], ACT.Copy).then_inc(indexed, 1)
                    wait(act, spreads, GROUP * (2 * i + slot - 1))
                    act.activation(field[:, slot], rec[:, chunks, 1:3], ACT.Copy).then_inc(indexed, 1)
            peeled(act, pairs, body)
            def store(i):
                for slot in range(2):
                    act.wait_ge(summed, TG * (2 * i + slot + 1))
                    act.dma_start(node_rows(x1_d, i * 2 + slot), xin[:, slot]).then_inc(x_out[slot], 16)
            peeled(act, steps // 2, store)
            for slot in range(2):
                act.wait_ge(x_out[slot], 16 * (steps // 2))

        @block.tensor
        def _(pe):
            def body(i):
                for slot in range(2):
                    pe.wait_ge(gathered[slot], 16 * GROUP * (i + 1))
                    for g in range(GROUP):
                        done = (i * 2 + slot) * GROUP + g
                        pe.wait_ge(spreads, done + 1)
                        wait(pe, added, done - 3)
                        pe.matmul(part[:, g % 4, 0:D], spread[:, slot, g], got[:, slot, g],
                                  start=True, stop=True).then_inc(multiplied, 1)
            peeled(pe, pairs, body)

        @block.vector
        def _(dve):
            dve.memset(xin[:, 1, TG - 1], 0.0).then_inc(cleared, 1)
            dve.memset(agg[:], 0.0).then_inc(cleared, 1)

            def body(i):
                for slot in range(2):
                    first = (i * 2 + slot) * GROUP
                    dve.wait_ge(indexed, 2 * (2 * i + slot + 1))
                    wait(dve, multiplied, first - GROUP)
                    for g in range(GROUP):
                        dve.tensor_scalar(spread[:, slot, g], C["iota_f"][:], field[:, slot, g, 0:1],
                                          field[:, slot, g, 1:2], ALU.is_equal, ALU.mult).then_inc(spreads, 1)
                    for g in range(GROUP):
                        tile = dve.value_load(chunk_tile[0:1, bass.ds(first + g, 1)], min_val=0, max_val=NT - 1)
                        dve.wait_ge(multiplied, first + g + 1)
                        wait(dve, added, first + g)
                        at = agg[:, bass.ds(tile, 1), :].rearrange("p a f -> p (a f)")
                        dve.tensor_tensor(at, at, part[:, g % 4, 0:D], ALU.add).then_inc(added, 1)
            dve.wait_ge(cleared, 2)
            peeled(dve, pairs, body)
            dve.wait_ge(added, NC)

            def final(i):
                for slot in range(2):
                    dve.wait_ge(x_in[slot], 32 * (i + 1))
                    for k in range(TG):
                        tile = (i * 2 + slot) * TG + k
                        dve.scalar_tensor_tensor(
                            out=xin[:, slot, k], in0=agg[:, bass.ds(tile, 1), :].rearrange("p a f -> p (a f)"),
                            scalar=dis[:, bass.ds(tile, 1)], in1=xin[:, slot, k],
                            op0=ALU.mult, op1=ALU.add).then_inc(summed, 1)
            peeled(dve, steps // 2, final)

def router_table(nc, x1_d, ut_d, W_gat, att_src, att_dst, tab_d, nodes, C):
    steps = NT // TG
    with ExitStack() as ctx:
        sb = lambda n, sh, dt: ctx.enter_context(nc.sbuf_tensor(f"rt_{n}", sh, dt))
        sem = lambda n: ctx.enter_context(nc.semaphore(f"rt_{n}"))
        xin = sb("x", [P, 2, TG, D], F32)
        u = sb("u", [P, 2, TG, D], F32)
        ut = sb("ut", [P, 2, TG, 2, P], F32)
        wg = sb("wg", [P, 2, HE], F32)
        att = sb("att", [P, 2, HE], F32)
        stats = sb("stats", [P, TG, 6], F32)
        mv = sb("mv", [P, TG, 2], F32)
        var = sb("var", [P, TG], F32)
        root = sb("root", [P, TG], F32)
        scale = sb("scale", [P, TG], F32)
        prod = sb("prod", [P, NT, HE], F32)
        blank = sb("blank", [1, TAB], F32)
        turned = ctx.enter_context(nc.psum_tensor("rt_turned", [P, 16, P], F32))
        h_ps = ctx.enter_context(nc.psum_tensor("rt_h", [P, TG, HE], F32))
        weights_in = sem("weights_in")
        x_in = [sem("x_in0"), sem("x_in1")]
        ut_out = [sem("ut_out0"), sem("ut_out1")]
        chain_sem, var_ready, rooted, normed, transposed, ut_ready, h_ready, h_taken, table_ready, table_out, blanked = (
            sem("chain"), sem("var_ready"), sem("rooted"), sem("normed"), sem("transposed"), sem("ut_ready"),
            sem("h_ready"), sem("h_taken"), sem("table_ready"), sem("table_out"), sem("blanked"))
        block = ctx.enter_context(nc.Block())
        own = nodes["own"]

        @block.sync
        def _(sp):
            sp.dma_start(wg[:], W_gat.rearrange("(k p) n -> p k n", p=P)).then_inc(weights_in, 16)
            sp.dma_start(att[:, 0], att_src.rearrange("h e -> (h e)").partition_broadcast(P)).then_inc(weights_in, 16)
            sp.dma_start(att[:, 1], att_dst.rearrange("h e -> (h e)").partition_broadcast(P)).then_inc(weights_in, 16)

            def body(i):
                for slot in range(2):
                    wait(sp, normed, TG * (2 * i + slot - 1))
                    sp.dma_start(xin[:, slot], node_rows(x1_d, i * 2 + slot)).then_inc(x_in[slot], 16)
            peeled(sp, steps // 2, body)
            sp.wait_ge(table_ready, 3)
            sp.dma_start(tab_d[0:NP, :].rearrange("(t p) f -> p t f", p=P), own[:]).then_inc(table_out, 16)
            sp.wait_ge(blanked, 2)
            sp.dma_start(tab_d[NP:NP + 1, :], blank[:]).then_inc(table_out, 16)
            sp.wait_ge(table_out, 32)

        @block.vector
        def _(dve):
            chain = Chain(dve, chain_sem)
            dve.memset(blank[:, 0:HE], 0.0).then_inc(blanked, 1)
            dve.memset(blank[:, HE:TAB], NO_EDGE).then_inc(blanked, 1)

            def body(i):
                for slot in range(2):
                    step = i * 2 + slot
                    dve.wait_ge(x_in[slot], i * 16 + 16)
                    layernorm_stats(dve, chain, xin[:, slot], stats, mv)
                    dve.tensor_scalar(var[:], mv[:, :, 1], LN_EPS, None, ALU.add).then_inc(var_ready, 1)
                    dve.wait_ge(rooted, step + 1)
                    chain.step(dve.reciprocal(scale[:], root[:]))
                    wait(dve, transposed, step - 1)
                    for k in range(TG):
                        dve.tensor_scalar(u[:, slot, k], xin[:, slot, k], mv[:, k, 0:1], scale[:, k:k + 1],
                                          ALU.subtract, ALU.mult).then_inc(normed, 1)
                    dve.wait_ge(normed, TG * step + TG)
                    dve.wait_ge(h_ready, step + 1)
                    dve.tensor_copy(own[:, bass.ds(step * TG, TG), 0:HE], h_ps[:]).then_inc(h_taken, 1)
            chain.peeled(steps // 2, body)
            dve.wait_ge(h_taken, steps)
            dve.wait_ge(weights_in, 48)
            for k, target in ((0, own[:, :, HE:TAB]), (1, nodes["asd"][:])):
                chain.step(dve.tensor_tensor(prod[:], own[:, :, 0:HE],
                                             att[:, k].unsqueeze(1).to_broadcast([P, NT, HE]), ALU.mult))
                dve.tensor_reduce(target, prod[:, :, :].rearrange("p t (h e) -> p t h e", h=HEADS), AX.X,
                                  ALU.add).then_inc(table_ready, 1)
                dve.wait_ge(table_ready, k + 1)
            dve.tensor_copy(nodes["top"][:], own[:, :, HE:TAB]).then_inc(table_ready, 1)

        @block.tensor
        def _(pe):
            pe.wait_ge(weights_in, 48)

            def body(i):
                for slot in range(2):
                    step = i * 2 + slot
                    pe.wait_ge(normed, TG * step + TG)
                    wait(pe, ut_ready, step)
                    for k in range(TG):
                        for half in range(2):
                            last = pe.transpose(turned[:, 2 * k + half], u[:, slot, k, half * P:(half + 1) * P],
                                                C["ident"][:])
                    last.then_inc(transposed, 1)
                    pe.wait_ge(ut_ready, step + 1)
                    wait(pe, h_taken, step)
                    for k in range(TG):
                        for half in range(2):
                            last = pe.matmul(h_ps[:, k], ut[:, slot, k, half], wg[:, half],
                                             start=(half == 0), stop=(half == 1))
                    last.then_inc(h_ready, 1)
            peeled(pe, steps // 2, body)

        @block.scalar
        def _(act):
            def body(i):
                for slot in range(2):
                    step = i * 2 + slot
                    act.wait_ge(var_ready, step + 1)
                    act.activation(root[:], var[:], ACT.Sqrt).then_inc(rooted, 1)
                    act.wait_ge(transposed, step + 1)
                    wait(act, h_ready, step - 1)
                    wait(act, ut_out[slot], 32 * i)
                    act.activation(ut[:, slot].rearrange("p k h q -> p (k h) q"), turned[:, 0:2 * TG],
                                   ACT.Copy).then_inc(ut_ready, 1)
                    act.wait_ge(ut_ready, step + 1)
                    for half in range(2):
                        act.dma_start(ut_d[half][:, bass.ds(step * TG * P, TG * P)].rearrange("p (k q) -> p k q", q=P),
                                      ut[:, slot, :, half]).then_inc(ut_out[slot], 16)
            peeled(act, steps // 2, body)
            for slot in range(2):
                act.wait_ge(ut_out[slot], 32 * (steps // 2))


def attention(nc, s, tab_d, rec_d, chunk_tile, nodes, b_gat, ln_gamma, ln_beta, C):
    NC = s.chunks
    pairs = NC // (2 * GROUP)
    HALF = GROUP // 2
    top_, T, own, asd = nodes["top"], nodes["T"], nodes["own"], nodes["asd"]
    with ExitStack() as outer:
        rec = outer.enter_context(nc.sbuf_tensor("at_rec", [P, NC, 2], F32))
        rows = outer.enter_context(nc.sbuf_tensor("at_rows", [P, NC, TAB], F32))

        with ExitStack() as ctx:
            sb = lambda n, sh, dt: ctx.enter_context(nc.sbuf_tensor(f"am_{n}", sh, dt))
            ps = lambda n, sh, dt: ctx.enter_context(nc.psum_tensor(f"am_{n}", sh, dt))
            sem = lambda n: ctx.enter_context(nc.semaphore(f"am_{n}"))
            got = sb("got", [P, 2, GROUP, TAB], F32)
            index = sb("index", [P, 2, GROUP], I32)
            row = sb("row", [P, 2, GROUP], F32)
            one = sb("one", [P, 2, GROUP, P], BF16)
            one_t = sb("one_t", [P, 2, GROUP * P], BF16)
            score_t = sb("score_t", [HEADS, 2, GROUP * P], F32)
            head = sb("head", [HEADS, HEADS, P], F32)
            other = sb("other", [P, P], BF16)
            most = sb("most", [P, HEADS, GROUP], F32)
            one_ps = ps("one_ps", [P, GROUP * P], BF16)
            score_ps = ps("score_ps", [HEADS, GROUP * P], F32)
            spread = ps("spread", [P, 2, 2, HALF, P], F32)
            rec_in, ready, chain_sem = sem("rec_in"), sem("ready"), sem("chain")
            indexed, coded, coded_t, copied_t, copied, spreads, reduced, topped = (
                sem("indexed"), sem("coded"), sem("coded_t"), sem("copied_t"), sem("copied"), sem("spreads"),
                sem("reduced"), sem("topped"))
            gathered = [sem("gathered0"), sem("gathered1")]
            block = ctx.enter_context(nc.Block())

            @block.sync
            def _(sp):
                sp.dma_start(rec[:, :, :].rearrange("p c w -> p (c w)"),
                             rec_d.rearrange("(p c) w -> p (c w)", p=P)).then_inc(rec_in, 16)

            @block.gpsimd
            def _(pool):
                def body(i):
                    for slot in range(2):
                        wait(pool, copied, 2 * i + slot - 1)
                        wait(pool, coded_t, 2 * i + slot - 1)
                        pool.wait_ge(indexed, 2 * (2 * i + slot + 1))
                        pool.nop(nofuse=True)
                        for g in range(GROUP):
                            pool.indirect_dma_start(got[:, slot, g], None, tab_d,
                                                    bass.IndirectOffsetOnAxis(ap=index[:, slot, g:g + 1], axis=0)
                                                    ).then_inc(gathered[slot], 16)
                peeled(pool, pairs, body)

            @block.scalar
            def _(act):
                act.wait_ge(rec_in, 16)

                def fields(step, slot, i):
                    chunks = bass.ds(step * GROUP, GROUP)
                    wait(act, gathered[slot], 16 * GROUP * i)
                    act.activation(index[:, slot], rec[:, chunks, 0], ACT.Copy).then_inc(indexed, 1)
                    wait(act, coded, step - 1)
                    act.activation(row[:, slot], rec[:, chunks, 1], ACT.Copy).then_inc(indexed, 1)

                def body(i):
                    for slot in range(2):
                        fields(i * 2 + slot, slot, i)
                    for slot in range(2):
                        step = i * 2 + slot
                        act.wait_ge(coded_t, step + 1)
                        wait(act, spreads, 4 * (step - 1))
                        act.activation(one_t[:, slot], one_ps[:], ACT.Copy).then_inc(copied_t, 1)
                        act.activation(score_t[:, slot], score_ps[:], ACT.Copy).then_inc(copied_t, 1)
                        act.activation(rows[:, bass.ds(step * GROUP, GROUP), :], got[:, slot], ACT.Copy).then_inc(copied, 1)
                peeled(act, pairs, body)

            @block.tensor
            def _(pe):
                pe.wait_ge(ready, 2)

                def body(i):
                    for slot in range(2):
                        step = i * 2 + slot
                        pe.wait_ge(gathered[slot], 16 * GROUP * (i + 1))
                        pe.wait_ge(coded, step + 1)
                        wait(pe, copied_t, 2 * step)
                        for g in range(GROUP):
                            pe.transpose(one_ps[:, g * P:(g + 1) * P], one[:, slot, g], C["ident_b"][:])
                        for g in range(GROUP):
                            last = pe.transpose(score_ps[:, g * P:(g + 1) * P], got[:, slot, g, HE:TAB], C["ident"][:])
                        last.then_inc(coded_t, 1)
                        pe.wait_ge(copied_t, 2 * step + 2)
                        for unit in range(4):
                            half, pair = unit // 2, unit % 2
                            wait(pe, reduced, 4 * step + unit - 1)
                            for h in range(2):
                                bank = spread[:, unit % 2, h].rearrange("p c q -> p (c q)")
                                cols = slice(half * HALF * P, (half + 1) * HALF * P)
                                pe.matmul(bank, head[:, pair * 2 + h], score_t[:, slot, cols], start=True, stop=False)
                                last = pe.matmul(bank, other[:], one_t[:, slot, cols], start=False, stop=True)
                            last.then_inc(spreads, 1)
                peeled(pe, pairs, body)

            @block.vector
            def _(dve):
                chain = Chain(dve, chain_sem)
                dve.tensor_scalar(other[:], C["ident"][:], -NO_EDGE, NO_EDGE, ALU.mult, ALU.add).then_inc(ready, 1)
                dve.tensor_copy(head[:], C["ident"][0:HEADS, 0:HEADS].unsqueeze(2).to_broadcast([HEADS, HEADS, P])
                                ).then_inc(ready, 1)

                def body(i):
                    for slot in range(2):
                        step = i * 2 + slot
                        dve.wait_ge(indexed, 2 * (step + 1))
                        wait(dve, coded_t, step - 1)
                        dve.tensor_tensor(one[:, slot], C["iota_b"][:, :].unsqueeze(1).to_broadcast([P, GROUP, P]),
                                          row[:, slot].unsqueeze(2).to_broadcast([P, GROUP, P]),
                                          ALU.is_equal).then_inc(coded, 1)
                    for slot in range(2):
                        step = i * 2 + slot
                        wait(dve, topped, GROUP * step)
                        for unit in range(4):
                            half, pair = unit // 2, unit % 2
                            dve.wait_ge(spreads, 4 * step + unit + 1)
                            dve.tensor_reduce(most[:, pair * 2:pair * 2 + 2, half * HALF:(half + 1) * HALF],
                                              spread[:, unit % 2], AX.X, ALU.max).then_inc(reduced, 1)
                        dve.wait_ge(reduced, 4 * step + 4)
                        for g in range(GROUP):
                            tile = dve.value_load(chunk_tile[0:1, bass.ds(step * GROUP + g, 1)], min_val=0,
                                                  max_val=NT - 1)
                            wait(dve, topped, GROUP * step + g)
                            at = top_[:, bass.ds(tile, 1), :].rearrange("p a f -> p (a f)")
                            dve.tensor_tensor(at, at, most[:, :, g], ALU.max).then_inc(topped, 1)
                peeled(dve, pairs, body)

        with ExitStack() as ctx:
            sb = lambda n, sh, dt: ctx.enter_context(nc.sbuf_tensor(f"as_{n}", sh, dt))
            ps = lambda n, sh, dt: ctx.enter_context(nc.psum_tensor(f"as_{n}", sh, dt))
            sem = lambda n: ctx.enter_context(nc.semaphore(f"as_{n}"))
            one = sb("one", [P, 2, GROUP, P], F32)
            one_t = sb("one_t", [P, 2, GROUP, P], F32)
            z = sb("z", [P, GROUP, HEADS], F32)
            zz = sb("zz", [P, GROUP, HEADS], F32)
            msg = sb("msg", [P, 2, GROUP, TAB], F32)
            acc = sb("acc", [P, NT, TAB], F32)
            self_z = sb("self_z", [P, NT, HEADS], F32)
            vec = sb("vec", [P, 3, HE], F32)
            t16 = sb("t16", [P, NT, HE], F32)
            t1 = sb("t1", [P, 2, NT], F32)
            score = sb("score", [P, NT, EXPERTS], F32)
            beaten = sb("beaten", [P, NT, EXPERTS], F32)
            win = sb("win", [P, NT], F32)
            one_ps = ps("one_ps", [P, GROUP, P], F32)
            edge_ps = ps("edge_ps", [P, 2, GROUP, 64], F32)
            sum_ps = ps("sum_ps", [P, 2, GROUP, 64], F32)
            vec_in, chain_sem, maxed = sem("vec_in"), sem("chain"), sem("maxed")
            self_exp, coded, coded_t, copied_t, fetched, shifted, exped, messaged, summed, added = (
                sem("self_exp"), sem("coded"), sem("coded_t"), sem("copied_t"), sem("fetched"), sem("shifted"),
                sem("exped"), sem("messaged"), sem("summed"), sem("added"))
            varied, rooted, centred, gate_exp = sem("varied"), sem("rooted"), sem("centred"), sem("gate_exp")
            block = ctx.enter_context(nc.Block())
            heads = lambda ap: ap.rearrange("p t (h e) -> p t h e", h=HEADS)

            @block.sync
            def _(sp):
                for k, v in enumerate((b_gat, ln_gamma, ln_beta)):
                    sp.dma_start(vec[:, k], v.partition_broadcast(P)).then_inc(vec_in, 16)

            @block.scalar
            def _(act):
                act.wait_ge(maxed, 1)
                act.activation(acc[:, :, HE:TAB], self_z[:], ACT.Exp).then_inc(self_exp, 1)

                def body(i):
                    for slot in range(2):
                        step = i * 2 + slot
                        act.wait_ge(coded_t, step + 1)
                        wait(act, fetched, step - 1)
                        act.activation(one_t[:, slot], one_ps[:], ACT.Copy).then_inc(copied_t, 1)
                        act.wait_ge(shifted, step + 1)
                        wait(act, summed, step - 1)
                        act.activation(msg[:, slot, :, HE:TAB], zz[:], ACT.Exp).then_inc(exped, 1)
                peeled(act, pairs, body)
                act.wait_ge(varied, 1)
                act.activation(t1[:, 1], t1[:, 0], ACT.Sqrt).then_inc(rooted, 1)
                act.wait_ge(centred, 1)
                act.activation(score[:], score[:], ACT.Exp).then_inc(gate_exp, 1)

            @block.tensor
            def _(pe):
                pe.wait_ge(maxed, 1)

                def body(i):
                    for slot in range(2):
                        step = i * 2 + slot
                        pe.wait_ge(coded, step + 1)
                        wait(pe, copied_t, step)
                        for g in range(GROUP):
                            last = pe.transpose(one_ps[:, g], one[:, slot, g], C["ident"][:])
                        last.then_inc(coded_t, 1)
                        pe.wait_ge(copied_t, step + 1)
                        wait(pe, shifted, step - 1)
                        for g in range(GROUP):
                            tile = pe.value_load(chunk_tile[0:1, bass.ds(step * GROUP + g, 1)], min_val=0,
                                                 max_val=NT - 1)
                            last = pe.matmul(edge_ps[:, slot, g, 0:2 * HEADS], one_t[:, slot, g],
                                             T[:, bass.ds(tile, 1), :].rearrange("p a f -> p (a f)"),
                                             start=True, stop=True)
                        last.then_inc(fetched, 1)
                        pe.wait_ge(messaged, step + 1)
                        wait(pe, added, GROUP * (step - 1))
                        for g in range(GROUP):
                            last = pe.matmul(sum_ps[:, slot, g, 0:TAB], one[:, slot, g], msg[:, slot, g],
                                             start=True, stop=True)
                        last.then_inc(summed, 1)
                peeled(pe, pairs, body)

            @block.vector
            def _(dve):
                chain = Chain(dve, chain_sem)
                chain.put(dve.tensor_copy(T[:, :, 0:HEADS], asd[:]))
                chain.step(dve.tensor_tensor(self_z[:], top_[:], asd[:], ALU.add))
                chain.step(dve.scalar_tensor_tensor(out=T[:, :, HEADS:2 * HEADS], in0=self_z[:], scalar=0.2,
                                                    in1=self_z[:], op0=ALU.mult, op1=ALU.max))
                chain.step(dve.tensor_tensor(self_z[:], own[:, :, HE:TAB], asd[:], ALU.add))
                chain.step(dve.scalar_tensor_tensor(out=self_z[:], in0=self_z[:], scalar=0.2, in1=self_z[:],
                                                    op0=ALU.mult, op1=ALU.max))
                dve.tensor_tensor(self_z[:], self_z[:], T[:, :, HEADS:2 * HEADS], ALU.subtract).then_inc(maxed, 1)
                dve.wait_ge(self_exp, 1)
                chain.step(dve.tensor_tensor(heads(acc[:, :, 0:HE]), heads(own[:, :, 0:HE]),
                                             acc[:, :, HE:TAB].unsqueeze(3).to_broadcast([P, NT, HEADS, EXPERTS]),
                                             ALU.mult))

                def body(i):
                    for slot in range(2):
                        step = i * 2 + slot
                        chunks = bass.ds(step * GROUP, GROUP)
                        wait(dve, summed, step - 1)
                        dve.tensor_tensor(one[:, slot], C["iota_f"][:, :].unsqueeze(1).to_broadcast([P, GROUP, P]),
                                          rec[:, chunks, 1].unsqueeze(2).to_broadcast([P, GROUP, P]),
                                          ALU.is_equal).then_inc(coded, 1)
                        dve.wait_ge(fetched, step + 1)
                        chain.step(dve.tensor_tensor(z[:], rows[:, chunks, HE:TAB], edge_ps[:, slot, :, 0:HEADS], ALU.add))
                        chain.step(dve.scalar_tensor_tensor(out=z[:], in0=z[:], scalar=0.2, in1=z[:],
                                                            op0=ALU.mult, op1=ALU.max))
                        dve.tensor_tensor(zz[:], z[:], edge_ps[:, slot, :, HEADS:2 * HEADS],
                                          ALU.subtract).then_inc(shifted, 1)
                        dve.wait_ge(exped, step + 1)
                        dve.tensor_tensor(msg[:, slot, :, 0:HE].rearrange("p g (h e) -> p g h e", h=HEADS),
                                          rows[:, chunks, 0:HE].rearrange("p g (h e) -> p g h e", h=HEADS),
                                          msg[:, slot, :, HE:TAB].unsqueeze(3).to_broadcast([P, GROUP, HEADS, EXPERTS]),
                                          ALU.mult).then_inc(messaged, 1)
                        dve.wait_ge(summed, step + 1)
                        for g in range(GROUP):
                            tile = dve.value_load(chunk_tile[0:1, bass.ds(step * GROUP + g, 1)], min_val=0,
                                                  max_val=NT - 1)
                            wait(dve, added, GROUP * step + g)
                            at = acc[:, bass.ds(tile, 1), :].rearrange("p a f -> p (a f)")
                            dve.tensor_tensor(at, at, sum_ps[:, slot, g, 0:TAB], ALU.add).then_inc(added, 1)
                chain.peeled(pairs, body)
                dve.wait_ge(added, NC)
                tt, ts, red = dve.tensor_tensor, dve.tensor_scalar, dve.tensor_reduce
                wide = lambda ap: ap.unsqueeze(2).to_broadcast([P, NT, HE])
                row = lambda k: vec[:, k].unsqueeze(1).to_broadcast([P, NT, HE])
                dve.wait_ge(vec_in, 48)
                chain.step(ts(self_z[:], acc[:, :, HE:TAB], 1e-16, None, ALU.add))
                chain.step(dve.reciprocal(self_z[:], self_z[:]))
                chain.step(tt(heads(t16[:]), heads(acc[:, :, 0:HE]),
                              self_z[:].unsqueeze(3).to_broadcast([P, NT, HEADS, EXPERTS]), ALU.mult))
                chain.step(tt(t16[:], t16[:], row(0), ALU.add))
                chain.step(red(t1[:, 0], t16[:], AX.X, ALU.add))
                chain.step(ts(t1[:, 0], t1[:, 0], 1.0 / HE, None, ALU.mult))
                chain.step(tt(t16[:], t16[:], wide(t1[:, 0]), ALU.subtract))
                chain.step(tt(acc[:, :, 0:HE], t16[:], t16[:], ALU.mult))
                chain.step(red(t1[:, 0], acc[:, :, 0:HE], AX.X, ALU.add))
                ts(t1[:, 0], t1[:, 0], 1.0 / HE, LN_EPS, ALU.mult, ALU.add).then_inc(varied, 1)
                dve.wait_ge(rooted, 1)
                chain.step(dve.reciprocal(t1[:, 1], t1[:, 1]))
                chain.step(tt(t16[:], t16[:], wide(t1[:, 1]), ALU.mult))
                chain.step(tt(t16[:], t16[:], row(1), ALU.mult))
                chain.step(tt(t16[:], t16[:], row(2), ALU.add))
                chain.step(red(score[:], t16[:].rearrange("p t (h e) -> p t e h", h=HEADS), AX.X, ALU.add))
                chain.step(ts(score[:], score[:], 1.0 / HEADS, None, ALU.mult))
                chain.step(dve.memset(beaten[:], 0.0))
                for a in range(EXPERTS):
                    for b in range(a + 1, EXPERTS):
                        chain.step(tt(win[:], score[:, :, a], score[:, :, b], ALU.is_ge))
                        chain.put(tt(beaten[:, :, b], beaten[:, :, b], win[:], ALU.add))
                        chain.step(dve.scalar_tensor_tensor(out=beaten[:, :, a], in0=beaten[:, :, a], scalar=1.0,
                                                            in1=win[:], op0=ALU.add, op1=ALU.subtract))
                chain.put(ts(beaten[:], beaten[:], 1.5, None, ALU.is_lt))
                chain.step(red(t1[:, 0], score[:], AX.X, ALU.max))
                four = lambda ap: ap.unsqueeze(2).to_broadcast([P, NT, EXPERTS])
                tt(score[:], score[:], four(t1[:, 0]), ALU.subtract).then_inc(centred, 1)
                dve.wait_ge(gate_exp, 1)
                chain.step(tt(score[:], score[:], beaten[:], ALU.mult))
                chain.step(red(t1[:, 0], score[:], AX.X, ALU.add))
                chain.step(dve.reciprocal(t1[:, 0], t1[:, 0]))
                chain.step(tt(nodes["gate"][:], score[:], four(t1[:, 0]), ALU.mult))


def experts(nc, x1_d, ut_d, W1, b1, W2, b2, gate, out, C):
    FO = FF // P
    PAIR = 2
    TOK = PAIR * P
    steps = NT // PAIR
    with ExitStack() as ctx:
        sb = lambda n, sh, dt: ctx.enter_context(nc.sbuf_tensor(f"ex_{n}", sh, dt))
        ps = lambda n, sh, dt: ctx.enter_context(nc.psum_tensor(f"ex_{n}", sh, dt))
        sem = lambda n: ctx.enter_context(nc.semaphore(f"ex_{n}"))
        w1 = sb("w1", [P, EXPERTS, 2, FF], F32)
        w2 = sb("w2", [P, EXPERTS, FO, D], F32)
        b1c = sb("b1c", [P, EXPERTS * FO], F32)
        b2r = sb("b2r", [EXPERTS, D], F32)
        ut = sb("ut", [P, 2, 2, TOK], F32)
        res = sb("res", [P, 2, PAIR, D], F32)
        hid = sb("hid", [P, 2, FO, TOK], F32)
        gates = sb("gates", [P, 2, PAIR, EXPERTS], F32)
        gate_t = sb("gate_t", [EXPERTS, PAIR, P], F32)
        h_ps = ps("h_ps", [P, 4, 512], F32)
        y_ps = ps("y_ps", [P, 2, PAIR, D], F32)
        b_ps = ps("b_ps", [P, PAIR, D], F32)
        g_ps = ps("g_ps", [EXPERTS, PAIR, P], F32)
        w_in = sem("w_in")
        ut_in = [sem("ut_in0"), sem("ut_in1")]
        x_in = [sem("x_in0"), sem("x_in1")]
        stored = [sem("stored0"), sem("stored1")]
        picked = sem("picked")
        turned, taken, biased, hidden, active, mixed, combined = (sem("turned"), sem("taken"), sem("biased"),
                                                                  sem("hidden"), sem("active"), sem("mixed"),
                                                                  sem("combined"))
        block = ctx.enter_context(nc.Block())
        PER = PAIR * (EXPERTS + 1)

        def all_steps(eng, one):
            def body(i):
                one(i, 0)
                one(i, 1)
            peeled(eng, steps // 2, body)
            one(steps // 2, 0)

        @block.sync
        def _(sp):
            for e in range(EXPERTS):
                sp.dma_start(w1[:, e], W1[e].rearrange("(k p) n -> p k n", p=P)).then_inc(w_in, 16)
                sp.dma_start(w2[:, e], W2[e].rearrange("(f p) n -> p f n", p=P)).then_inc(w_in, 16)
            with nc.allow_non_contiguous_dma(reason="a bias per partition"):
                sp.dma_start(b1c[:], b1.rearrange("e (f p) -> p (e f)", p=P)).then_inc(w_in, 16)
            sp.dma_start(b2r[:], b2).then_inc(w_in, 16)

            def one(i, slot):
                step = i * 2 + slot
                wait(sp, mixed, EXPERTS * (step - 1))
                for half in range(2):
                    sp.dma_start(ut[:, slot, half], ut_d[half][:, bass.ds(step * TOK, TOK)]).then_inc(ut_in[slot], 16)
                wait(sp, stored[slot], 16 * i)
                sp.dma_start(res[:, slot], x1_d[bass.ds(step * TOK, TOK), :].rearrange("(t p) f -> p t f", p=P)
                             ).then_inc(x_in[slot], 16)
            all_steps(sp, one)

        @block.tensor
        def _(pe):
            pe.wait_ge(w_in, 16 * (2 * EXPERTS + 2))

            def first(step, slot, e):
                for f in range(FO):
                    wait(pe, active, step * 16 + e * FO + f - 3)
                    for half in range(2):
                        last = pe.matmul(h_ps[:, f, 0:TOK], w1[:, e, half, f * P:(f + 1) * P], ut[:, slot, half],
                                         start=(half == 0), stop=(half == 1))
                    last.then_inc(hidden, 1)

            def second(step, e):
                pe.wait_ge(active, step * 16 + (e + 1) * FO)
                wait(pe, combined, step * PER + PAIR * e if e >= 2 else (step - 1) * PER + PAIR * (e + 4))
                for t in range(PAIR):
                    for f in range(FO):
                        last = pe.matmul(y_ps[:, e % 2, t], hid[:, e % 2, f, t * P:(t + 1) * P], w2[:, e, f],
                                         start=(f == 0), stop=(f == FO - 1))
                last.then_inc(mixed, 1)

            def one(i, slot):
                step = i * 2 + slot
                pe.wait_ge(picked, step + 1)
                wait(pe, taken, step)
                for t in range(PAIR):
                    last = pe.transpose(g_ps[:, t], gates[:, slot, t], C["ident"][:])
                last.then_inc(turned, 1)
                pe.wait_ge(ut_in[slot], 32 * (i + 1))
                first(step, slot, 0)
                pe.wait_ge(taken, step + 1)
                wait(pe, combined, (step - 1) * PER + PAIR)
                for t in range(PAIR):
                    last = pe.matmul(b_ps[:, t], gate_t[:, t], b2r[:], start=True, stop=True)
                last.then_inc(biased, 1)
                for e in range(EXPERTS):
                    if e + 1 < EXPERTS:
                        first(step, slot, e + 1)
                    second(step, e)
            all_steps(pe, one)

        @block.scalar
        def _(act):
            def one(i, slot):
                step = i * 2 + slot
                for e in range(EXPERTS):
                    wait(act, mixed, step * EXPERTS + e - 1)
                    for f in range(FO):
                        act.wait_ge(hidden, step * 16 + e * FO + f + 1)
                        act.activation(hid[:, e % 2, f], h_ps[:, f, 0:TOK], ACT.Gelu,
                                       bias=b1c[:, e * FO + f:e * FO + f + 1]).then_inc(active, 1)
            act.wait_ge(w_in, 16 * (2 * EXPERTS + 2))
            all_steps(act, one)

        @block.vector
        def _(dve):
            def one(i, slot):
                step = i * 2 + slot
                wait(dve, turned, step - 1)
                wait(dve, combined, PER * (step - 1))
                dve.tensor_copy(gates[:, slot], gate[:, bass.ds(step * PAIR, PAIR), :]).then_inc(picked, 1)
                dve.wait_ge(picked, step + 1)
                dve.wait_ge(turned, step + 1)
                wait(dve, biased, step)
                dve.tensor_copy(gate_t[:], g_ps[:]).then_inc(taken, 1)
                dve.wait_ge(biased, step + 1)
                dve.wait_ge(x_in[slot], 16 * (i + 1))
                for t in range(PAIR):
                    dve.tensor_tensor(res[:, slot, t], res[:, slot, t], b_ps[:, t], ALU.add).then_inc(combined, 1)
                for e in range(EXPERTS):
                    dve.wait_ge(mixed, step * EXPERTS + e + 1)
                    for t in range(PAIR):
                        dve.wait_ge(combined, step * PER + PAIR * (e + 1) + t - 1)
                        dve.scalar_tensor_tensor(out=res[:, slot, t], in0=y_ps[:, e % 2, t], scalar=gates[:, slot, t, e:e + 1],
                                                 in1=res[:, slot, t], op0=ALU.mult, op1=ALU.add).then_inc(combined, 1)
            all_steps(dve, one)

        @block.gpsimd
        def _(pool):
            def one(i, slot, last=False):
                step = i * 2 + slot
                pool.wait_ge(combined, PER * (step + 1))
                pool.nop(nofuse=True)
                if not last:
                    pool.dma_start(out[bass.ds(step * TOK, TOK), :].rearrange("(t p) f -> p t f", p=P),
                                   res[:, slot]).then_inc(stored[slot], 16)
                else:
                    base = step * TOK
                    pool.dma_start(out[base:base + P, :], res[:, slot, 0]).then_inc(stored[slot], 16)
                    pool.dma_start(out[base + P:N, :], res[0:LAST, slot, 1]).then_inc(stored[slot], 16)

            def body(i):
                one(i, 0)
                one(i, 1)
            peeled(pool, steps // 2, body)
            one(steps // 2, 0, last=True)
            pool.wait_ge(stored[0], 16 * (steps // 2) + 32)
            pool.wait_ge(stored[1], 16 * (steps // 2))


_INS = ['x', 'src', 'dst', 'edge_weight', 'L0_ffn_W_gat', 'L0_ffn_att_src', 'L0_ffn_att_dst', 'L0_ffn_b_gat',
        'L0_ffn_ln_gamma', 'L0_ffn_ln_beta', 'L0_ffn_W1', 'L0_ffn_b1', 'L0_ffn_W2', 'L0_ffn_b2', 'L0_ffn_edge_index']
_OUTS = [((12500, 256), 'float32')]


def kernel(**inputs):
    import numpy as _np
    import concourse.bacc as _bacc
    from concourse import mybir as _mybir
    from concourse.bass_utils import run_bass_kernel_spmd as _run

    nc = _bacc.Bacc("TRN2", target_bir_lowering=False, num_devices=1)
    arrays, args = {}, []
    for name in _INS:
        a = _np.ascontiguousarray(inputs[name])
        arrays[f"in_{name}_dram"] = a
        args.append(nc.dram_tensor(f"in_{name}_dram", a.shape, _mybir.dt.from_np(a.dtype), kind="ExternalInput").ap())
    for i, (shape, dtype) in enumerate(_OUTS):
        dt = _mybir.dt.from_np(_np.dtype(dtype))
        args.append(nc.dram_tensor(f"out_{i}_dram", shape, dt, kind="ExternalOutput").ap())
    build(nc, *args)
    r = _run(nc, [arrays], core_ids=[0])
    return r.results[0]["out_0_dram"]
```

```python
import concourse.bass as bass
from concourse import mybir
from contextlib import ExitStack

F32 = mybir.dt.float32
BF16 = mybir.dt.bfloat16
I32 = mybir.dt.int32
ALU = mybir.AluOpType
ACT = mybir.ActivationFunctionType
AX = mybir.AxisListType

P = 128
LOG_P = 7
N = 12500
D = 256
NT = -(-N // P)
NP = NT * P
LAST = N - (NT - 1) * P
HEADS, EXPERTS = 4, 4
HE = HEADS * EXPERTS
FF = 512
LN_EPS = 1e-5
GROUP = 8
TG = 7
SORT_COLS = 16
SORT_EDGES = SORT_COLS * P
AHEAD = 2
SLOTS = 4
PARTS = 3
NO_EDGE = -2.0 ** 100
TAB = HE + HEADS
TABW = TAB + PARTS * HEADS // 2


class EdgeList:

    def __init__(self, name, edges, cols, words):
        self.name, self.edges, self.cols, self.words = name, edges, cols, words
        self.buckets = NT + (cols * P > edges)
        most = (cols * P + self.buckets * (P - 1)) // P
        self.chunks = -(-most // GROUP) * GROUP
        self.steps = cols // SORT_COLS
        assert cols % (2 * SORT_COLS) == 0 and cols % P == 0 and cols * P >= edges


def wait(eng, sem, value):
    if not isinstance(value, int) or value > 0:
        eng.wait_ge(sem, value)


def peeled(eng, steps, body):
    body(0)
    if steps > 1:
        with eng.Fori(1, steps) as i:
            body(i)


def run_steps(eng, steps, body, lag=0, unroll=4):
    rounds = steps // unroll
    for k in range(unroll):
        body(k, k, 0)
    with eng.Fori(1, rounds) as i:
        for k in range(unroll):
            body(i * unroll + k, k, i)
    for step in range(rounds * unroll, steps + lag):
        body(step, step % unroll, step // unroll)


def due(step, steps):
    return not isinstance(step, int) or 0 <= step < steps


def tiles_of(nc, eng, engine, chunk_tile, step):
    _, tiles = nc.values_load_multi_w_load_instructions(
        chunk_tile[0:1, bass.ds(step * GROUP, GROUP)], engines=(engine,), min_val=0, max_val=NT - 1,
        skip_runtime_bounds_check_because="chunk_tile is made as min(a count, NT - 1)")
    return tiles


class Chain:

    def __init__(self, eng, sem):
        self.eng, self.sem, self.count, self.loop = eng, sem, 0, 0

    def step(self, ins):
        ins.then_inc(self.sem, 1)
        self.count += 1
        self.eng.wait_ge(self.sem, self.loop + self.count)

    def put(self, ins):
        ins.then_inc(self.sem, 1)
        self.count += 1

    def settle(self):
        self.eng.wait_ge(self.sem, self.loop + self.count)

    def peeled(self, steps, body):
        start = self.count
        body(0)
        per = self.count - start
        if steps > 1:
            with self.eng.Fori(1, steps) as i:
                self.loop = i * per - per
                body(i)
                assert self.count - start == 2 * per
        self.count, self.loop = start + per * steps, 0

    def run(self, steps, body, unroll=4):
        start = self.count
        for k in range(unroll):
            body(k, k, 0)
        per, rounds = self.count - start, steps // unroll
        with self.eng.Fori(1, rounds) as i:
            self.loop = i * per - per
            for k in range(unroll):
                body(i * unroll + k, k, i)
            assert self.count - start == 2 * per
        self.count, self.loop = start + per * rounds, 0
        for step in range(rounds * unroll, steps):
            body(step, step % unroll, step // unroll)


def build(nc, x, src, dst, edge_weight, W_gat, att_src, att_dst, b_gat, ln_gamma, ln_beta,
          W1, b1, W2, b2, edge_index, out, stage="all"):
    gnn = EdgeList("gnn", src.shape[0], 1664, 3)
    gat = EdgeList("gat", edge_index.shape[1], 1024, 2)
    top = ExitStack()
    with top:
        def keep(name, shape, dt):
            return top.enter_context(nc.sbuf_tensor(name, shape, dt))

        def dram(name, shape, dt):
            return nc.dram_tensor(name, shape, dt, kind="Internal").ap()

        xs_d = dram("xs_d", (NP, D), F32)
        x1_d = dram("x1_d", (NP, D), F32)
        ut_d = [dram(f"ut_d{k}", (P, NP), F32) for k in range(2)]
        tab_d = dram("tab_d", (NP + 1, TABW), F32)
        bucket_d = {s.name: dram(f"bucket_{s.name}", (s.cols, P), BF16) for s in (gnn, gat)}
        rec_d = {s.name: dram(f"rec_{s.name}", (P * s.chunks, s.words), F32) for s in (gnn, gat)}

        pidx = keep("pidx", [P, 1], F32)
        iota_i = keep("iota_i", [P, P], I32)
        pidx_i = keep("pidx_i", [P, 1], I32)
        iota_f = keep("iota_f", [P, P], F32)
        iota_b = keep("iota_b", [P, P], BF16)
        ident = keep("ident", [P, P], F32)
        ident_b = keep("ident_b", [P, P], BF16)
        later = keep("later", [P, P], F32)
        ones_b = keep("ones_b", [P, 1], BF16)
        ones_f = keep("ones_f", [P, 1], F32)
        dis = keep("dis", [P, NT], F32)
        chunk_tile = {s.name: keep(f"chunk_tile_{s.name}", [1, s.chunks], I32) for s in (gnn, gat)}

        constants(nc, pidx, pidx_i, iota_i, iota_f, iota_b, ident, ident_b, later, ones_b, ones_f)
        C = dict(pidx=pidx, iota_f=iota_f, iota_b=iota_b, ident=ident, ident_b=ident_b, later=later,
                 ones_b=ones_b, ones_f=ones_f)
        degrees(nc, gnn, dst, dis, C)
        scaled_layernorm(nc, x, xs_d, dis)
        edge_sort(nc, gnn, src, dst, edge_weight, bucket_d["gnn"], rec_d["gnn"], chunk_tile["gnn"], C)
        edge_sort(nc, gat, edge_index[1], edge_index[0], None, bucket_d["gat"], rec_d["gat"],
                  chunk_tile["gat"], C)
        neighbour_sum(nc, gnn, x, xs_d, rec_d["gnn"], chunk_tile["gnn"], dis, x1_d, C)
        if stage == "x1":
            copy_out(nc, x1_d, out)
            return
        nodes = dict(T=keep("T", [P, NT, 2 * HEADS], F32),
                     own=keep("own", [P, NT, TABW], F32),
                     asd=keep("asd", [P, NT, HEADS], F32),
                     top=keep("top", [P, NT, HEADS], F32),
                     gate=keep("gate", [P, NT, EXPERTS], F32))
        router_table(nc, x1_d, ut_d, W_gat, att_src, att_dst, tab_d, nodes, C)
        attention(nc, gat, tab_d, rec_d["gat"], chunk_tile["gat"], nodes, b_gat, ln_gamma, ln_beta, C)
        if stage == "gate":
            with nc.semaphore("gate_out") as gate_out, nc.Block() as block:
                @block.sync
                def _(sp):
                    sp.dma_start(out, nodes["gate"][:, :, :].rearrange("p a b -> p (a b)")).then_inc(gate_out, 16)
                    sp.wait_ge(gate_out, 16)
            return
        experts(nc, x1_d, ut_d, W1, b1, W2, b2, nodes["gate"], out, C)


def copy_out(nc, x1_d, out):
    with nc.semaphore("copied") as copied, nc.Block() as block:
        @block.sync
        def _(sp):
            sp.dma_start(out, x1_d[0:N, :]).then_inc(copied, 16)
            sp.wait_ge(copied, 16)


def constants(nc, pidx, pidx_i, iota_i, iota_f, iota_b, ident, ident_b, later, ones_b, ones_f):
    with nc.semaphore("counted") as counted, nc.semaphore("const_chain") as chain_sem, nc.Block() as block:
        @block.gpsimd
        def _(pool):
            pool.iota(iota_i[:], pattern=[[1, P]], base=0, channel_multiplier=0).then_inc(counted, 1)
            pool.iota(pidx_i[:], pattern=[[0, 1]], base=0, channel_multiplier=1).then_inc(counted, 1)

        @block.vector
        def _(dve):
            chain = Chain(dve, chain_sem)
            dve.memset(ones_b[:], 1.0)
            dve.memset(ones_f[:], 1.0)
            dve.wait_ge(counted, 2)
            chain.put(dve.tensor_copy(iota_f[:], iota_i[:]))
            chain.put(dve.tensor_copy(iota_b[:], iota_i[:]))
            chain.put(dve.tensor_copy(pidx[:], pidx_i[:]))
            chain.settle()
            dve.tensor_scalar(ident[:], iota_f[:], pidx[:, 0:1], None, ALU.is_equal)
            dve.tensor_scalar(ident_b[:], iota_f[:], pidx[:, 0:1], None, ALU.is_equal)
            dve.tensor_scalar(later[:], iota_f[:], pidx[:, 0:1], None, ALU.is_gt)


def load_edges(eng, s, tile, array, sem):
    full = s.edges // s.cols
    if full == P:
        eng.dma_start(tile[:, :], array.rearrange("(p c) -> p c", p=P)).then_inc(sem, 16)
        return 16
    assert full == P - 1
    eng.dma_start(tile[0:full, :], array[0:full * s.cols].rearrange("(p c) -> p c", p=full)).then_inc(sem, 16)
    rest = s.edges - full * s.cols
    eng.dma_start(tile[full:P, 0:rest], array[full * s.cols:s.edges].rearrange("(p c) -> p c", p=1)).then_inc(sem, 16)
    return 32


def degrees(nc, s, dst, dis, C):
    steps = s.cols // GROUP
    with ExitStack() as ctx:
        sb = lambda n, sh, dt: ctx.enter_context(nc.sbuf_tensor(n, sh, dt))
        sem = lambda n: ctx.enter_context(nc.semaphore(n))
        key = sb("deg_key", [P, s.cols], I32)
        digit = sb("deg_digit", [P, s.cols], I32)
        hi = sb("deg_hi", [P, s.cols], BF16)
        lo = sb("deg_lo", [P, s.cols], BF16)
        one_hi = sb("deg_one_hi", [P, 2, GROUP, NT], BF16)
        one_lo = sb("deg_one_lo", [P, 2, GROUP, P], BF16)
        zeros = sb("deg_zeros", [P, P], BF16)
        deg = sb("deg_deg", [P, NT], F32)
        root = sb("deg_root", [P, NT], F32)
        hist = ctx.enter_context(nc.psum_tensor("deg_hist", [P, NT], F32))
        filled, loaded, chain_sem = sem("deg_filled"), sem("deg_loaded"), sem("deg_chain")
        coded, counted, total, rooted, clipped = (sem("deg_coded"), sem("deg_counted"), sem("deg_total"),
                                                  sem("deg_rooted"), sem("deg_clipped"))
        block = ctx.enter_context(nc.Block())

        @block.sync
        def _(sp):
            sp.wait_ge(filled, 1)
            load_edges(sp, s, key, dst, loaded)

        @block.vector
        def _(dve):
            chain = Chain(dve, chain_sem)
            dve.memset(key[:], NP).then_inc(filled, 1)
            dve.memset(zeros[:], 0.0).then_inc(filled, 1)
            dve.wait_ge(loaded, 32)
            chain.step(dve.tensor_scalar(digit[:], key[:], LOG_P, None, ALU.logical_shift_right))
            chain.step(dve.tensor_copy(hi[:], digit[:]))
            chain.step(dve.tensor_scalar(digit[:], key[:], P - 1, None, ALU.bitwise_and))
            chain.step(dve.tensor_copy(lo[:], digit[:]))

            def body(i):
                for slot in range(2):
                    wait(dve, counted, 2 * i + slot - 1)
                    cols = bass.ds(i * 2 * GROUP + slot * GROUP, GROUP)
                    dve.tensor_tensor(one_hi[:, slot], C["iota_b"][:, 0:NT].unsqueeze(1).to_broadcast([P, GROUP, NT]),
                                      hi[:, cols].unsqueeze(2).to_broadcast([P, GROUP, NT]),
                                      ALU.is_equal).then_inc(coded, 1)
                    dve.tensor_tensor(one_lo[:, slot], C["iota_b"][:, :].unsqueeze(1).to_broadcast([P, GROUP, P]),
                                      lo[:, cols].unsqueeze(2).to_broadcast([P, GROUP, P]),
                                      ALU.is_equal).then_inc(coded, 1)
            peeled(dve, steps // 2, body)
            dve.wait_ge(total, 1)
            chain.step(dve.tensor_scalar(deg[:], hist[:], 1.0, None, ALU.max))
            dve.sem_inc(clipped, 1)
            dve.wait_ge(rooted, 1)
            dve.reciprocal(dis[:], root[:])

        @block.tensor
        def _(pe):
            pe.wait_ge(filled, 2)
            pe.matmul(hist[:], zeros[:], zeros[:, 0:NT], start=True, stop=False)

            def body(i):
                for slot in range(2):
                    pe.wait_ge(coded, i * 4 + slot * 2 + 2)
                    for g in range(GROUP):
                        last = pe.matmul(hist[:], one_lo[:, slot, g], one_hi[:, slot, g], start=False, stop=False)
                    last.then_inc(counted, 1)
            peeled(pe, steps // 2, body)
            pe.matmul(hist[:], zeros[:], zeros[:, 0:NT], start=False, stop=True).then_inc(total, 1)

        @block.scalar
        def _(act):
            act.wait_ge(clipped, 1)
            act.activation(root[:], deg[:], ACT.Sqrt).then_inc(rooted, 1)


def layernorm_stats(dve, chain, tiles, stats, mv, k0=0):
    for k in range(tiles.shape[1]):
        chain.put(dve.bn_stats(stats[:, k], tiles[:, k]))
    chain.settle()
    dve.nop(nofuse=True)
    for k in range(tiles.shape[1]):
        chain.put(dve.bn_aggr(mv[:, k], stats[:, k]))
    chain.settle()


def node_rows(array, i):
    return array[bass.ds(i * TG * P, TG * P), :].rearrange("(t p) f -> p t f", p=P)


def load_nodes(sp, tile, x, i, last, sem):
    if not last:
        sp.dma_start(tile, node_rows(x, i)).then_inc(sem, 32)
    else:
        base = i * TG * P
        whole = base + (TG - 1) * P
        sp.dma_start(tile[:, 0:TG - 1], x[base:whole, :].rearrange("(t p) f -> p t f", p=P)).then_inc(sem, 16)
        sp.dma_start(tile[0:LAST, TG - 1], x[whole:N, :]).then_inc(sem, 16)


def scaled_layernorm(nc, x, xs_d, dis):
    steps = NT // TG
    with ExitStack() as ctx:
        sb = lambda n, sh, dt: ctx.enter_context(nc.sbuf_tensor(n, sh, dt))
        sem = lambda n: ctx.enter_context(nc.semaphore(n))
        xin = sb("sl_x", [P, 2, TG, D], F32)
        xout = sb("sl_out", [P, 2, TG, D], F32)
        stats = sb("sl_stats", [P, TG, 6], F32)
        mv = sb("sl_mv", [P, TG, 2], F32)
        var = sb("sl_var", [P, TG], F32)
        root = sb("sl_root", [P, TG], F32)
        scale = sb("sl_scale", [P, TG], F32)
        loaded = [sem("sl_loaded0"), sem("sl_loaded1")]
        stored = [sem("sl_stored0"), sem("sl_stored1")]
        chain_sem, ready, rooted, normed, cleared = (sem("sl_chain"), sem("sl_var_ready"), sem("sl_rooted"),
                                                     sem("sl_normed"), sem("sl_cleared"))
        block = ctx.enter_context(nc.Block())

        @block.sync
        def _(sp):
            def one(i, slot, last=False):
                step = i * 2 + slot
                wait(sp, normed, TG * (step - 1))
                load_nodes(sp, xin[:, slot], x, step, last, loaded[slot])

            def body(i):
                one(i, 0)
                one(i, 1)
            peeled(sp, steps // 2 - 1, body)
            one(steps // 2 - 1, 0)
            sp.wait_ge(cleared, 1)
            one(steps // 2 - 1, 1, last=True)

        @block.vector
        def _(dve):
            chain = Chain(dve, chain_sem)

            def one(i, slot):
                step = i * 2 + slot
                dve.wait_ge(loaded[slot], i * 32 + 32)
                layernorm_stats(dve, chain, xin[:, slot], stats, mv)
                chain.put(dve.tensor_scalar(var[:], mv[:, :, 1], LN_EPS, None, ALU.add))
                chain.settle()
                dve.tensor_copy(var[:], var[:]).then_inc(ready, 1)
                dve.wait_ge(rooted, step + 1)
                chain.step(dve.reciprocal(scale[:], root[:]))
                chain.step(dve.tensor_tensor(scale[:], scale[:], dis[:, bass.ds(step * TG, TG)], ALU.mult))
                wait(dve, stored[slot], 16 * i)
                for k in range(TG):
                    dve.tensor_scalar(xout[:, slot, k], xin[:, slot, k], mv[:, k, 0:1], scale[:, k:k + 1],
                                      ALU.subtract, ALU.mult).then_inc(normed, 1)
                dve.wait_ge(normed, TG * step + TG)

            def body(i):
                one(i, 0)
                one(i, 1)
            chain.peeled(steps // 2 - 1, body)
            one(steps // 2 - 1, 0)
            dve.memset(xin[:, 1, TG - 1], 0.0).then_inc(cleared, 1)
            one(steps // 2 - 1, 1)

        @block.scalar
        def _(act):
            def body(i):
                for slot in range(2):
                    act.wait_ge(ready, i * 2 + slot + 1)
                    act.activation(root[:], var[:], ACT.Sqrt).then_inc(rooted, 1)
                    act.wait_ge(normed, TG * (i * 2 + slot + 1))
                    act.dma_start(node_rows(xs_d, i * 2 + slot), xout[:, slot]).then_inc(stored[slot], 16)
            peeled(act, steps // 2, body)
            for slot in range(2):
                act.wait_ge(stored[slot], 16 * (steps // 2))


def edge_sort(nc, s, key_a, other_a, weight_a, bucket_d, rec_d, chunk_tile, C):
    B, W, NC = s.buckets, s.words, s.chunks
    blocks = s.cols // P
    with ExitStack() as ctx:
        sb = lambda n, sh, dt: ctx.enter_context(nc.sbuf_tensor(f"{s.name}_{n}", sh, dt))
        ps = lambda n, sh, dt: ctx.enter_context(nc.psum_tensor(f"{s.name}_{n}", sh, dt))
        sem = lambda n: ctx.enter_context(nc.semaphore(f"{s.name}_{n}"))
        fields = sb("fields", [P, s.cols, W], F32)
        empty = sb("empty", [P, NC, W], F32)
        tmp = ExitStack()
        key = tmp.enter_context(nc.sbuf_tensor(f"{s.name}_key", [P, s.cols], I32))
        other = tmp.enter_context(nc.sbuf_tensor(f"{s.name}_other", [P, s.cols], I32))
        weight = tmp.enter_context(nc.sbuf_tensor(f"{s.name}_weight", [P, s.cols], F32)) if weight_a is not None else None
        digit = tmp.enter_context(nc.sbuf_tensor(f"{s.name}_digit", [P, s.cols], I32))
        hi = tmp.enter_context(nc.sbuf_tensor(f"{s.name}_hi", [P, s.cols], F32))
        hi_t = tmp.enter_context(nc.sbuf_tensor(f"{s.name}_hi_t", [P, blocks, P], BF16))

        with ExitStack() as c1:
            sem1 = lambda n: c1.enter_context(nc.semaphore(f"{s.name}_{n}"))
            pt = c1.enter_context(nc.psum_tensor(f"{s.name}_pt", [P, 2, 512], F32))
            filled, loaded, chain_sem, split, turned, taken, saved, blank = (
                sem1("filled"), sem1("loaded"), sem1("chain1"), sem1("split"), sem1("turned"), sem1("taken"),
                sem1("saved"), sem1("blank"))
            block = c1.enter_context(nc.Block())

            @block.sync
            def _(sp):
                sp.wait_ge(filled, 3)
                load_edges(sp, s, key, key_a, loaded)
                load_edges(sp, s, other, other_a, loaded)
                if weight is not None:
                    load_edges(sp, s, weight, weight_a, loaded)
                sp.wait_ge(blank, 1)
                sp.dma_start(rec_d.rearrange("(p c) w -> p (c w)", p=P),
                             empty[:, :, :].rearrange("p c w -> p (c w)")).then_inc(saved, 16)
                sp.wait_ge(taken, blocks)
                sp.dma_start(bucket_d.rearrange("(b t) p -> t b p", t=P), hi_t[:]).then_inc(saved, 16)
                sp.wait_ge(saved, 32)

            @block.vector
            def _(dve):
                chain = Chain(dve, chain_sem)
                dve.memset(key[:], NP).then_inc(filled, 1)
                dve.memset(other[:], 0).then_inc(filled, 1)
                if weight is not None:
                    dve.memset(weight[:], 0.0).then_inc(filled, 1)
                    chain.step(dve.memset(empty[:], 0.0))
                else:
                    chain.step(dve.memset(empty[:], 0.0))
                    chain.step(dve.memset(empty[:, :, 0], float(NP)))
                    dve.memset(digit[:], 0).then_inc(filled, 1)
                dve.memset(pt[:, 0, 0:1], 0.0).then_inc(blank, 1)
                per = 16 if s.edges == s.cols * P else 32
                dve.wait_ge(loaded, per * W)
                dve.wait_ge(filled, 3)
                chain.step(dve.tensor_scalar(digit[:], key[:], LOG_P, None, ALU.logical_shift_right))
                dve.tensor_copy(hi[:], digit[:]).then_inc(split, 1)
                dve.wait_ge(split, 1)
                chain.step(dve.tensor_scalar(digit[:], key[:], P - 1, None, ALU.bitwise_and))
                dve.tensor_copy(fields[:, :, 1], digit[:])
                dve.tensor_copy(fields[:, :, 0], other[:])
                if weight is not None:
                    dve.tensor_copy(fields[:, :, 2], weight[:])
                for b in range(blocks):
                    dve.wait_ge(turned, b + 1)
                    dve.tensor_copy(hi_t[:, b], pt[:, b % 2, 0:P]).then_inc(taken, 1)

            @block.tensor
            def _(pe):
                pe.wait_ge(blank, 1)
                pe.wait_ge(split, 1)
                for b in range(blocks):
                    wait(pe, taken, b - 1)
                    pe.transpose(pt[:, b % 2, 0:P], hi[:, b * P:(b + 1) * P], C["ident"][:]).then_inc(turned, 1)
        tmp.close()

        keys = sb("keys", [P, 2, SORT_EDGES], BF16)
        match = sb("match", [P, 2, SORT_EDGES], BF16)
        run = sb("run", [P, 2, SORT_EDGES], F32)
        slots = sb("slots", [P, 2, SORT_EDGES], F32)
        count = sb("count", [P, 4], F32)
        small_i = sb("small_i", [P, 2], I32)
        need_f = sb("need_f", [P, 1], F32)
        first_f = sb("first_f", [P, 1], F32)
        end_f = sb("end_f", [P, 1], F32)
        chunk_no_i = sb("chunk_no_i", [P, NC], I32)
        past = sb("past", [P, NC], BF16)
        place = sb("place", [P, SORT_COLS], I32)
        lane = sb("lane", [P, SORT_COLS], I32)
        index = sb("index", [P, 2, SORT_COLS], I32)
        record = sb("record", [P, 2, SORT_COLS, W], F32)
        first_ps = ps("first_ps", [P, 1], F32)
        tile_ps = ps("tile_ps", [1, 512], F32)
        pos_ps = ps("pos_ps", [P, 2, 512], F32)
        keys_in = [sem("keys_in0"), sem("keys_in1")]
        keys_used, chain_sem, chunk_no = sem("keys_used"), sem("chain2"), sem("chunk_no")
        needed, started, pasted, tiled, tiles_read = (sem("needed"), sem("started"), sem("pasted"), sem("tiled"),
                                                      sem("tiles_read"))
        masked, summed, placed, staged = sem("masked"), sem("summed"), sem("placed"), sem("staged")
        scattered = [sem("scattered0"), sem("scattered1")]
        block = ctx.enter_context(nc.Block())
        flat = bucket_d.rearrange("c p -> (c p)")

        @block.sync
        def _(sp):
            def sweep(base):
                def body(i):
                    for slot in range(2):
                        step = i * 2 + slot
                        wait(sp, keys_used, base + step - 1)
                        sp.dma_start(keys[0:B, slot], flat[bass.ds(step * SORT_EDGES, SORT_EDGES)]
                                     .partition_broadcast(B)).then_inc(keys_in[slot], 16)
                return body
            peeled(sp, s.steps // 2, sweep(0))
            for slot in range(2):
                sp.wait_ge(keys_used, s.steps - 1 + slot)
                sp.dma_start(keys[0:B, slot], flat[slot * SORT_EDGES:(slot + 1) * SORT_EDGES]
                             .partition_broadcast(B)).then_inc(keys_in[slot], 16)
            with sp.Fori(1, s.steps // 2) as i:
                sweep(s.steps)(i)

        @block.gpsimd
        def _(pool):
            pool.iota(chunk_no_i[:], pattern=[[1, NC]], base=0, channel_multiplier=0).then_inc(chunk_no, 1)

            def body(i):
                for slot in range(2):
                    pool.wait_ge(placed, 2 * i + slot + 1)
                    pool.wait_ge(staged, 2 * i + slot + 1)
                    pool.nop(nofuse=True)
                    for c in range(SORT_COLS):
                        pool.indirect_dma_start(rec_d, bass.IndirectOffsetOnAxis(ap=index[:, slot, c:c + 1], axis=0),
                                                record[:, slot, c], None).then_inc(scattered[slot], 16)
            peeled(pool, s.steps // 2, body)
            for slot in range(2):
                pool.wait_ge(scattered[slot], 16 * SORT_COLS * (s.steps // 2))

        @block.scalar
        def _(act):
            def body(i):
                for slot in range(2):
                    wait(act, scattered[slot], 16 * SORT_COLS * i)
                    act.activation(record[:, slot], fields[:, bass.ds((i * 2 + slot) * SORT_COLS, SORT_COLS), :],
                                   ACT.Copy).then_inc(staged, 1)
            peeled(act, s.steps // 2, body)

        @block.tensor
        def _(pe):
            pe.wait_ge(needed, 1)
            pe.matmul(first_ps[0:B, :], C["later"][0:B, 0:B], need_f[0:B, :], start=True, stop=True).then_inc(started, 1)
            pe.wait_ge(pasted, 1)
            for n, c in enumerate(range(0, NC, 512)):
                w = min(512, NC - c)
                wait(pe, tiles_read, n)
                pe.matmul(tile_ps[:, 0:w], C["ones_b"][0:B, :], past[0:B, c:c + w], start=True, stop=True).then_inc(tiled, 1)

            def body(i):
                for slot in range(2):
                    pe.wait_ge(masked, 2 * i + slot + 1)
                    for c in range(SORT_COLS):
                        last = pe.matmul(pos_ps[:, slot, c:c + 1], slots[0:B, slot, c * P:(c + 1) * P],
                                         C["ones_f"][0:B, :], start=True, stop=True)
                    last.then_inc(summed, 1)
            peeled(pe, s.steps // 2, body)

        @block.vector
        def _(dve):
            chain = Chain(dve, chain_sem)
            for k in range(2):
                chain.put(dve.memset(count[:, 2 * k:2 * k + 2], 0.0))
            chain.settle()

            def counts(i):
                for slot in range(2):
                    dve.wait_ge(keys_in[slot], i * 16 + 16)
                    dve.tensor_scalar(match[0:B, slot], keys[0:B, slot], C["pidx"][0:B, 0:1], None, ALU.is_equal,
                                      ALU.add, accum_out=count[0:B, slot:slot + 1]).then_inc(keys_used, 1)
                    dve.wait_ge(keys_used, 2 * i + slot + 1)
                    chain.step(dve.tensor_tensor(count[0:B, 2:3], count[0:B, 2:3], count[0:B, slot:slot + 1], ALU.add))
            chain.peeled(s.steps // 2, counts)
            chain.step(dve.tensor_scalar(small_i[0:B, 0:1], count[0:B, 2:3], float(P - 1), None, ALU.add))
            chain.step(dve.tensor_scalar(small_i[0:B, 1:2], small_i[0:B, 0:1], LOG_P, None, ALU.logical_shift_right))
            dve.tensor_copy(need_f[0:B, :], small_i[0:B, 1:2]).then_inc(needed, 1)
            dve.wait_ge(started, 1)
            chain.put(dve.tensor_scalar(run[0:B, 1, SORT_EDGES - 1:SORT_EDGES], first_ps[0:B, :], float(P), -1.0,
                                        ALU.mult, ALU.add))
            chain.step(dve.tensor_tensor(end_f[0:B, :], first_ps[0:B, :], need_f[0:B, :], ALU.add))
            dve.wait_ge(chunk_no, 1)
            dve.tensor_scalar(past[0:B, :], chunk_no_i[0:B, :], end_f[0:B, 0:1], None, ALU.is_ge).then_inc(pasted, 1)
            for n, c in enumerate(range(0, NC, 512)):
                w = min(512, NC - c)
                dve.wait_ge(tiled, n + 1)
                dve.tensor_scalar(chunk_tile[:, c:c + w], tile_ps[:, 0:w], float(NT - 1), None,
                                  ALU.min).then_inc(tiles_read, 1)

            def ranks(i):
                for slot in range(2):
                    dve.wait_ge(keys_in[slot], i * 16 + 16 + 16 * (s.steps // 2))
                    dve.tensor_scalar(match[0:B, slot], keys[0:B, slot], C["pidx"][0:B, 0:1], None,
                                      ALU.is_equal).then_inc(keys_used, 1)
                    dve.wait_ge(keys_used, s.steps + 2 * i + slot + 1)
                    chain.step(dve.tensor_tensor_scan(run[0:B, slot], match[0:B, slot], match[0:B, slot],
                                                      run[0:B, 1 - slot, SORT_EDGES - 1:SORT_EDGES], ALU.add, ALU.max))
                    wait(dve, summed, 2 * i + slot - 1)
                    dve.tensor_tensor(slots[0:B, slot], run[0:B, slot], match[0:B, slot], ALU.mult).then_inc(masked, 1)
                    dve.wait_ge(summed, 2 * i + slot + 1)
                    chain.step(dve.tensor_copy(place[:], pos_ps[:, slot, 0:SORT_COLS]))
                    chain.step(dve.tensor_scalar(lane[:], place[:], P - 1, None, ALU.bitwise_and))
                    chain.step(dve.tensor_scalar(place[:], place[:], LOG_P, None, ALU.logical_shift_right))
                    wait(dve, scattered[slot], 16 * SORT_COLS * i)
                    dve.scalar_tensor_tensor(out=index[:, slot], in0=lane[:], scalar=float(NC), in1=place[:],
                                             op0=ALU.mult, op1=ALU.add).then_inc(placed, 1)
                    dve.wait_ge(placed, 2 * i + slot + 1)
            chain.peeled(s.steps // 2, ranks)


def neighbour_sum(nc, s, x, xs_d, rec_d, chunk_tile, dis, x1_d, C):
    NC, W = s.chunks, s.words
    groups = NC // GROUP
    BANKS = 8
    with ExitStack() as ctx:
        sb = lambda n, sh, dt: ctx.enter_context(nc.sbuf_tensor(f"ns_{n}", sh, dt))
        sem = lambda n: ctx.enter_context(nc.semaphore(f"ns_{n}"))
        rec = sb("rec", [P, NC + AHEAD * GROUP, W], F32)
        agg = sb("agg", [P, NT, D], F32)
        got = sb("got", [P, SLOTS, GROUP, D], F32)
        spread = sb("spread", [P, 2, GROUP, P], F32)
        index = sb("index", [P, SLOTS, GROUP], I32)
        field = sb("field", [P, SLOTS, GROUP, 2], F32)
        part = ctx.enter_context(nc.psum_tensor("ns_part", [P, BANKS, 512], F32))
        rec_in, cleared, indexed, added, spreads, multiplied = (
            sem("rec_in"), sem("cleared"), sem("indexed"), sem("added"), sem("spreads"), sem("multiplied"))
        gathered = [sem(f"gathered{k}") for k in range(SLOTS)]
        xin = sb("xin", [P, 2, TG, D], F32)
        x_in = [sem("x_in0"), sem("x_in1")]
        x_out = [sem("x_out0"), sem("x_out1")]
        summed = sem("summed")
        block = ctx.enter_context(nc.Block())
        steps = NT // TG

        @block.sync
        def _(sp):
            sp.dma_start(rec[:, 0:NC, :].rearrange("p c w -> p (c w)"),
                         rec_d.rearrange("(p c) w -> p (c w)", p=P)).then_inc(rec_in, 16)
            sp.wait_ge(cleared, 2)

            def one(i, slot, last=False):
                wait(sp, x_out[slot], 16 * i)
                load_nodes(sp, xin[:, slot], x, i * 2 + slot, last, x_in[slot])

            def body(i):
                one(i, 0)
                one(i, 1)
            peeled(sp, steps // 2 - 1, body)
            one(steps // 2 - 1, 0)
            one(steps // 2 - 1, 1, last=True)

        @block.gpsimd
        def _(pool):
            def body(step, slot, i):
                wait(pool, multiplied, GROUP * (step - SLOTS + 1))
                pool.wait_ge(indexed, 2 * (step + 1))
                pool.nop(nofuse=True)
                for g in range(GROUP):
                    pool.indirect_dma_start(got[:, slot, g], None, xs_d,
                                            bass.IndirectOffsetOnAxis(ap=index[:, slot, g:g + 1], axis=0)
                                            ).then_inc(gathered[slot], 16)
            run_steps(pool, groups, body)

        @block.scalar
        def _(act):
            act.wait_ge(rec_in, 16)
            act.wait_ge(cleared, 1)

            def fields(step, slot, i):
                chunks = bass.ds(step * GROUP, GROUP)
                wait(act, gathered[slot], 16 * GROUP * i)
                act.activation(index[:, slot], rec[:, chunks, 0], ACT.Copy).then_inc(indexed, 1)
                wait(act, spreads, GROUP * (step - SLOTS + 1))
                act.activation(field[:, slot], rec[:, chunks, 1:3], ACT.Copy).then_inc(indexed, 1)
            run_steps(act, groups, fields)

            def store(i):
                for slot in range(2):
                    act.wait_ge(summed, TG * (2 * i + slot + 1))
                    act.dma_start(node_rows(x1_d, i * 2 + slot), xin[:, slot]).then_inc(x_out[slot], 16)
            peeled(act, steps // 2, store)
            for slot in range(2):
                act.wait_ge(x_out[slot], 16 * (steps // 2))

        @block.tensor
        def _(pe):
            def body(step, slot, i):
                pe.wait_ge(gathered[slot], 16 * GROUP * (i + 1))
                for g in range(GROUP):
                    done = step * GROUP + g
                    pe.wait_ge(spreads, done + 1)
                    wait(pe, added, done + 1 - BANKS)
                    pe.matmul(part[:, g, 0:D], spread[:, slot % 2, g], got[:, slot, g],
                              start=True, stop=True).then_inc(multiplied, 1)
            run_steps(pe, groups, body)

        @block.vector
        def _(dve):
            dve.memset(rec[:, NC:, :], 0.0).then_inc(cleared, 1)
            dve.memset(xin[:, 1, TG - 1], 0.0).then_inc(cleared, 1)
            dve.memset(agg[:], 0.0).then_inc(cleared, 1)
            dve.wait_ge(cleared, 3)

            def body(step, slot, i):
                if due(step, groups):
                    dve.wait_ge(indexed, 2 * (step + 1))
                    wait(dve, multiplied, GROUP * (step - 1))
                    for g in range(GROUP):
                        dve.tensor_scalar(spread[:, slot % 2, g], C["iota_f"][:], field[:, slot, g, 0:1],
                                          field[:, slot, g, 1:2], ALU.is_equal, ALU.mult).then_inc(spreads, 1)
                if due(step - 1, groups):
                    tiles = tiles_of(nc, dve, mybir.EngineType.DVE, chunk_tile, step - 1)
                    for g in range(GROUP):
                        dve.wait_ge(multiplied, (step - 1) * GROUP + g + 1)
                        wait(dve, added, (step - 1) * GROUP + g)
                        at = agg[:, bass.ds(tiles[g], 1), :].rearrange("p a f -> p (a f)")
                        dve.tensor_tensor(at, at, part[:, g, 0:D], ALU.add).then_inc(added, 1)
            run_steps(dve, groups, body, lag=1)
            dve.wait_ge(added, NC)

            def final(i):
                for slot in range(2):
                    dve.wait_ge(x_in[slot], 32 * (i + 1))
                    for k in range(TG):
                        tile = (i * 2 + slot) * TG + k
                        dve.scalar_tensor_tensor(
                            out=xin[:, slot, k], in0=agg[:, bass.ds(tile, 1), :].rearrange("p a f -> p (a f)"),
                            scalar=dis[:, bass.ds(tile, 1)], in1=xin[:, slot, k],
                            op0=ALU.mult, op1=ALU.add).then_inc(summed, 1)
            peeled(dve, steps // 2, final)


def split(dve, chain, parts, whole, left):
    w = whole.shape[-1]
    part = [parts[:, :, k * w:(k + 1) * w] for k in range(PARTS)]
    chain.step(dve.tensor_copy(part[0], whole))
    chain.step(dve.tensor_tensor(left, whole, part[0], ALU.subtract))
    chain.step(dve.tensor_copy(part[1], left))
    chain.step(dve.tensor_tensor(left, left, part[1], ALU.subtract))
    chain.step(dve.tensor_copy(part[2], left))


def router_table(nc, x1_d, ut_d, W_gat, att_src, att_dst, tab_d, nodes, C):
    steps = NT // TG
    with ExitStack() as ctx:
        sb = lambda n, sh, dt: ctx.enter_context(nc.sbuf_tensor(f"rt_{n}", sh, dt))
        sem = lambda n: ctx.enter_context(nc.semaphore(f"rt_{n}"))
        xin = sb("x", [P, 2, TG, D], F32)
        u = sb("u", [P, 2, TG, D], F32)
        ut = sb("ut", [P, 2, TG, 2, P], F32)
        wg = sb("wg", [P, 2, HE], F32)
        att = sb("att", [P, 2, HE], F32)
        stats = sb("stats", [P, TG, 6], F32)
        mv = sb("mv", [P, TG, 2], F32)
        var = sb("var", [P, TG], F32)
        root = sb("root", [P, TG], F32)
        scale = sb("scale", [P, TG], F32)
        prod = sb("prod", [P, NT, HE], F32)
        left = sb("left", [P, NT, HEADS], F32)
        blank = sb("blank", [1, TABW], F32)
        turned = ctx.enter_context(nc.psum_tensor("rt_turned", [P, 16, P], F32))
        h_ps = ctx.enter_context(nc.psum_tensor("rt_h", [P, TG, HE], F32))
        weights_in = sem("weights_in")
        x_in = [sem("x_in0"), sem("x_in1")]
        ut_out = [sem("ut_out0"), sem("ut_out1")]
        chain_sem, var_ready, rooted, normed, transposed, ut_ready, h_ready, h_taken, table_ready, table_out, blanked = (
            sem("chain"), sem("var_ready"), sem("rooted"), sem("normed"), sem("transposed"), sem("ut_ready"),
            sem("h_ready"), sem("h_taken"), sem("table_ready"), sem("table_out"), sem("blanked"))
        block = ctx.enter_context(nc.Block())
        own = nodes["own"]

        @block.sync
        def _(sp):
            sp.dma_start(wg[:], W_gat.rearrange("(k p) n -> p k n", p=P)).then_inc(weights_in, 16)
            sp.dma_start(att[:, 0], att_src.rearrange("h e -> (h e)").partition_broadcast(P)).then_inc(weights_in, 16)
            sp.dma_start(att[:, 1], att_dst.rearrange("h e -> (h e)").partition_broadcast(P)).then_inc(weights_in, 16)

            def body(i):
                for slot in range(2):
                    wait(sp, normed, TG * (2 * i + slot - 1))
                    sp.dma_start(xin[:, slot], node_rows(x1_d, i * 2 + slot)).then_inc(x_in[slot], 16)
            peeled(sp, steps // 2, body)
            sp.wait_ge(table_ready, 4)
            sp.dma_start(tab_d[0:NP, :].rearrange("(t p) f -> p t f", p=P), own[:]).then_inc(table_out, 16)
            sp.wait_ge(blanked, 4)
            sp.dma_start(tab_d[NP:NP + 1, :], blank[:]).then_inc(table_out, 16)
            sp.wait_ge(table_out, 32)

        @block.vector
        def _(dve):
            chain = Chain(dve, chain_sem)
            dve.memset(blank[:, 0:HE], 0.0).then_inc(blanked, 1)
            dve.memset(blank[:, HE:TAB], NO_EDGE).then_inc(blanked, 1)
            blank_parts = blank[:, TAB:TABW].bitcast(BF16)
            dve.memset(blank_parts[:, 0:HEADS], NO_EDGE).then_inc(blanked, 1)
            dve.memset(blank_parts[:, HEADS:], 0.0).then_inc(blanked, 1)

            def body(i):
                for slot in range(2):
                    step = i * 2 + slot
                    dve.wait_ge(x_in[slot], i * 16 + 16)
                    layernorm_stats(dve, chain, xin[:, slot], stats, mv)
                    dve.tensor_scalar(var[:], mv[:, :, 1], LN_EPS, None, ALU.add).then_inc(var_ready, 1)
                    dve.wait_ge(rooted, step + 1)
                    chain.step(dve.reciprocal(scale[:], root[:]))
                    wait(dve, transposed, step - 1)
                    for k in range(TG):
                        dve.tensor_scalar(u[:, slot, k], xin[:, slot, k], mv[:, k, 0:1], scale[:, k:k + 1],
                                          ALU.subtract, ALU.mult).then_inc(normed, 1)
                    dve.wait_ge(normed, TG * step + TG)
                    dve.wait_ge(h_ready, step + 1)
                    dve.tensor_copy(own[:, bass.ds(step * TG, TG), 0:HE], h_ps[:]).then_inc(h_taken, 1)
            chain.peeled(steps // 2, body)
            dve.wait_ge(h_taken, steps)
            dve.wait_ge(weights_in, 48)
            for k, target in ((0, own[:, :, HE:TAB]), (1, nodes["asd"][:])):
                chain.step(dve.tensor_tensor(prod[:], own[:, :, 0:HE],
                                             att[:, k].unsqueeze(1).to_broadcast([P, NT, HE]), ALU.mult))
                dve.tensor_reduce(target, prod[:, :, :].rearrange("p t (h e) -> p t h e", h=HEADS), AX.X,
                                  ALU.add).then_inc(table_ready, 1)
                dve.wait_ge(table_ready, k + 1)
            dve.tensor_copy(nodes["top"][:], own[:, :, HE:TAB]).then_inc(table_ready, 1)
            split(dve, chain, own[:, :, TAB:TABW].bitcast(BF16), own[:, :, HE:TAB], left[:])
            dve.sem_inc(table_ready, 1)

        @block.tensor
        def _(pe):
            pe.wait_ge(weights_in, 48)

            def body(i):
                for slot in range(2):
                    step = i * 2 + slot
                    pe.wait_ge(normed, TG * step + TG)
                    wait(pe, ut_ready, step)
                    for k in range(TG):
                        for half in range(2):
                            last = pe.transpose(turned[:, 2 * k + half], u[:, slot, k, half * P:(half + 1) * P],
                                                C["ident"][:])
                    last.then_inc(transposed, 1)
                    pe.wait_ge(ut_ready, step + 1)
                    wait(pe, h_taken, step)
                    for k in range(TG):
                        for half in range(2):
                            last = pe.matmul(h_ps[:, k], ut[:, slot, k, half], wg[:, half],
                                             start=(half == 0), stop=(half == 1))
                    last.then_inc(h_ready, 1)
            peeled(pe, steps // 2, body)

        @block.scalar
        def _(act):
            def body(i):
                for slot in range(2):
                    step = i * 2 + slot
                    act.wait_ge(var_ready, step + 1)
                    act.activation(root[:], var[:], ACT.Sqrt).then_inc(rooted, 1)
                    act.wait_ge(transposed, step + 1)
                    wait(act, h_ready, step - 1)
                    wait(act, ut_out[slot], 32 * i)
                    act.activation(ut[:, slot].rearrange("p k h q -> p (k h) q"), turned[:, 0:2 * TG],
                                   ACT.Copy).then_inc(ut_ready, 1)
                    act.wait_ge(ut_ready, step + 1)
                    for half in range(2):
                        act.dma_start(ut_d[half][:, bass.ds(step * TG * P, TG * P)].rearrange("p (k q) -> p k q", q=P),
                                      ut[:, slot, :, half]).then_inc(ut_out[slot], 16)
            peeled(act, steps // 2, body)
            for slot in range(2):
                act.wait_ge(ut_out[slot], 32 * (steps // 2))


def attention(nc, s, tab_d, rec_d, chunk_tile, nodes, b_gat, ln_gamma, ln_beta, C):
    NC = s.chunks
    groups = NC // GROUP
    HALF = GROUP // 2
    KEYS = 2 * HEADS
    top_, T, own, asd = nodes["top"], nodes["T"], nodes["own"], nodes["asd"]
    with ExitStack() as outer:
        rec = outer.enter_context(nc.sbuf_tensor("at_rec", [P, NC + AHEAD * GROUP, 2], F32))
        rows = outer.enter_context(nc.sbuf_tensor("at_rows", [P, NC, TAB], F32))

        with ExitStack() as ctx:
            sb = lambda n, sh, dt: ctx.enter_context(nc.sbuf_tensor(f"am_{n}", sh, dt))
            ps = lambda n, sh, dt: ctx.enter_context(nc.psum_tensor(f"am_{n}", sh, dt))
            sem = lambda n: ctx.enter_context(nc.semaphore(f"am_{n}"))
            got = sb("got", [P, SLOTS, GROUP, TABW], F32)
            index = sb("index", [P, SLOTS, GROUP], I32)
            row = sb("row", [P, SLOTS, GROUP], F32)
            one = sb("one", [P, 2, GROUP, P], BF16)
            one_t = sb("one_t", [P, 2, GROUP * P], BF16)
            score_t = sb("score_t", [PARTS * HEADS, 2, GROUP * P], BF16)
            head = sb("head", [PARTS * HEADS, HEADS, P], BF16)
            pick = sb("pick", [PARTS * HEADS, 2, PARTS * HEADS], F32)
            other = sb("other", [P, P], BF16)
            most = sb("most", [P, HEADS, GROUP], F32)
            one_ps = ps("one_ps", [P, 2, GROUP * P], BF16)
            score_ps = ps("score_ps", [PARTS * HEADS, 2, GROUP * P], BF16)
            spread = ps("spread", [P, 2, 2, HALF, P], F32)
            rec_in, ready, cleared, chain_sem = sem("rec_in"), sem("ready"), sem("cleared"), sem("chain")
            indexed, coded, coded_t, copied_t, copied, spreads, reduced, topped = (
                sem("indexed"), sem("coded"), sem("coded_t"), sem("copied_t"), sem("copied"), sem("spreads"),
                sem("reduced"), sem("topped"))
            gathered = [sem(f"gathered{k}") for k in range(SLOTS)]
            block = ctx.enter_context(nc.Block())

            @block.sync
            def _(sp):
                sp.dma_start(rec[:, 0:NC, :].rearrange("p c w -> p (c w)"),
                             rec_d.rearrange("(p c) w -> p (c w)", p=P)).then_inc(rec_in, 16)

            @block.gpsimd
            def _(pool):
                def body(step, slot, i):
                    wait(pool, copied, step - SLOTS + 1)
                    wait(pool, coded_t, step - SLOTS + 1)
                    pool.wait_ge(indexed, 2 * (step + 1))
                    pool.nop(nofuse=True)
                    for g in range(GROUP):
                        pool.indirect_dma_start(got[:, slot, g], None, tab_d,
                                                bass.IndirectOffsetOnAxis(ap=index[:, slot, g:g + 1], axis=0)
                                                ).then_inc(gathered[slot], 16)
                run_steps(pool, groups, body)

            @block.scalar
            def _(act):
                act.wait_ge(rec_in, 16)
                act.wait_ge(cleared, 1)

                def fields(step, slot, i):
                    chunks = bass.ds(step * GROUP, GROUP)
                    wait(act, gathered[slot], 16 * GROUP * i)
                    act.activation(index[:, slot], rec[:, chunks, 0], ACT.Copy).then_inc(indexed, 1)
                    wait(act, coded, step - SLOTS + 1)
                    act.activation(row[:, slot], rec[:, chunks, 1], ACT.Copy).then_inc(indexed, 1)

                def body(step, slot, i):
                    fields(step + AHEAD, (slot + AHEAD) % SLOTS, i + (slot + AHEAD) // SLOTS)
                    act.wait_ge(coded_t, step + 1)
                    wait(act, spreads, 4 * (step - 1))
                    act.activation(one_t[:, slot % 2], one_ps[:, slot % 2], ACT.Copy).then_inc(copied_t, 1)
                    act.activation(score_t[:, slot % 2], score_ps[:, slot % 2], ACT.Copy).then_inc(copied_t, 1)
                    act.activation(rows[:, bass.ds(step * GROUP, GROUP), :], got[:, slot, :, 0:TAB],
                                   ACT.Copy).then_inc(copied, 1)
                for k in range(AHEAD):
                    fields(k, k, 0)
                run_steps(act, groups, body)

            @block.tensor
            def _(pe):
                pe.wait_ge(ready, 2)

                def body(step, slot, i):
                    if due(step, groups):
                        pe.wait_ge(gathered[slot], 16 * GROUP * (i + 1))
                        pe.wait_ge(coded, step + 1)
                        wait(pe, copied_t, 2 * (step - 1))
                        for g in range(GROUP):
                            pe.transpose(one_ps[:, slot % 2, g * P:(g + 1) * P], one[:, slot % 2, g], C["ident_b"][:])
                        for g in range(GROUP):
                            last = pe.transpose(score_ps[:, slot % 2, g * P:(g + 1) * P],
                                                got[:, slot, g, TAB:TABW].bitcast(BF16), C["ident_b"][:])
                        last.then_inc(coded_t, 1)
                    if due(step - 1, groups):
                        before = (slot + 1) % 2
                        pe.wait_ge(copied_t, 2 * step)
                        for unit in range(4):
                            half, pair = unit // 2, unit % 2
                            wait(pe, reduced, 4 * (step - 1) + unit - 1)
                            for h in range(2):
                                bank = spread[:, unit % 2, h].rearrange("p c q -> p (c q)")
                                cols = slice(half * HALF * P, (half + 1) * HALF * P)
                                pe.matmul(bank, head[:, pair * 2 + h], score_t[:, before, cols], start=True, stop=False)
                                last = pe.matmul(bank, other[:], one_t[:, before, cols], start=False, stop=True)
                            last.then_inc(spreads, 1)
                run_steps(pe, groups, body, lag=1)

            @block.vector
            def _(dve):
                chain = Chain(dve, chain_sem)
                K = PARTS * HEADS
                dve.memset(rec[:, NC:, :], 0.0).then_inc(cleared, 1)
                dve.tensor_scalar(other[:], C["ident"][:], -NO_EDGE, NO_EDGE, ALU.mult, ALU.add).then_inc(ready, 1)
                chain.step(dve.tensor_tensor(pick[:, 0, 0:HEADS], C["ident"][0:K, 0:HEADS], C["ident"][0:K, HEADS:2 * HEADS], ALU.add))
                chain.step(dve.tensor_tensor(pick[:, 1, 0:HEADS], pick[:, 0, 0:HEADS], C["ident"][0:K, 2 * HEADS:3 * HEADS], ALU.add))
                dve.tensor_copy(head[:], pick[:, 1, 0:HEADS].unsqueeze(2).to_broadcast([K, HEADS, P])).then_inc(ready, 1)

                def body(step, slot, i):
                    if due(step, groups):
                        dve.wait_ge(indexed, 2 * (step + 1))
                        wait(dve, coded_t, step - 1)
                        dve.tensor_tensor(one[:, slot % 2], C["iota_b"][:, :].unsqueeze(1).to_broadcast([P, GROUP, P]),
                                          row[:, slot].unsqueeze(2).to_broadcast([P, GROUP, P]),
                                          ALU.is_equal).then_inc(coded, 1)
                    if due(step - 1, groups):
                        wait(dve, topped, GROUP * (step - 1))
                        for unit in range(4):
                            half, pair = unit // 2, unit % 2
                            dve.wait_ge(spreads, 4 * (step - 1) + unit + 1)
                            dve.tensor_reduce(most[:, pair * 2:pair * 2 + 2, half * HALF:(half + 1) * HALF],
                                              spread[:, unit % 2], AX.X, ALU.max).then_inc(reduced, 1)
                        tiles = tiles_of(nc, dve, mybir.EngineType.DVE, chunk_tile, step - 1)
                        dve.wait_ge(reduced, 4 * step)
                        for g in range(GROUP):
                            wait(dve, topped, GROUP * (step - 1) + g)
                            at = top_[:, bass.ds(tiles[g], 1), :].rearrange("p a f -> p (a f)")
                            dve.tensor_tensor(at, at, most[:, :, g], ALU.max).then_inc(topped, 1)
                run_steps(dve, groups, body, lag=1)

        with ExitStack() as ctx:
            sb = lambda n, sh, dt: ctx.enter_context(nc.sbuf_tensor(f"as_{n}", sh, dt))
            ps = lambda n, sh, dt: ctx.enter_context(nc.psum_tensor(f"as_{n}", sh, dt))
            sem = lambda n: ctx.enter_context(nc.semaphore(f"as_{n}"))
            one = sb("one", [P, SLOTS, GROUP, P], F32)
            one_t = sb("one_t", [P, 2, GROUP, P], BF16)
            T_parts = sb("T_parts", [P, NT, PARTS * KEYS], BF16)
            T_left = sb("T_left", [P, NT, KEYS], F32)
            keys = sb("keys", [P, GROUP, KEYS], F32)
            z = sb("z", [P, GROUP, HEADS], F32)
            zz = sb("zz", [P, 2, GROUP, HEADS], F32)
            msg = sb("msg", [P, 2, GROUP, TAB], F32)
            acc = sb("acc", [P, NT, TAB], F32)
            self_z = sb("self_z", [P, NT, HEADS], F32)
            vec = sb("vec", [P, 3, HE], F32)
            t16 = sb("t16", [P, NT, HE], F32)
            t1 = sb("t1", [P, 2, NT], F32)
            score = sb("score", [P, NT, EXPERTS], F32)
            beaten = sb("beaten", [P, NT, EXPERTS], F32)
            win = sb("win", [P, NT], F32)
            one_ps = ps("one_ps", [P, 2, GROUP, P], F32)
            edge_ps = ps("edge_ps", [P, 2, GROUP, 64], F32)
            sum_ps = ps("sum_ps", [P, 2, GROUP, 64], F32)
            vec_in, chain_sem, maxed = sem("vec_in"), sem("chain"), sem("maxed")
            self_exp, coded, coded_t, copied_t, fetched, read, shifted, exped, messaged, summed, added = (
                sem("self_exp"), sem("coded"), sem("coded_t"), sem("copied_t"), sem("fetched"), sem("read"),
                sem("shifted"), sem("exped"), sem("messaged"), sem("summed"), sem("added"))
            chained = sem("chained")
            varied, rooted, centred, gate_exp = sem("varied"), sem("rooted"), sem("centred"), sem("gate_exp")
            block = ctx.enter_context(nc.Block())
            heads = lambda ap: ap.rearrange("p t (h e) -> p t h e", h=HEADS)

            @block.sync
            def _(sp):
                for k, v in enumerate((b_gat, ln_gamma, ln_beta)):
                    sp.dma_start(vec[:, k], v.partition_broadcast(P)).then_inc(vec_in, 16)

            @block.scalar
            def _(act):
                act.wait_ge(maxed, 1)
                act.activation(acc[:, :, HE:TAB], self_z[:], ACT.Exp).then_inc(self_exp, 1)

                def body(step, slot, i):
                    if due(step, groups):
                        act.wait_ge(coded_t, step + 1)
                        wait(act, fetched, step - 1)
                        act.activation(one_t[:, slot % 2], one_ps[:, slot % 2], ACT.Copy).then_inc(copied_t, 1)
                    if due(step - 1, groups):
                        act.wait_ge(shifted, step)
                        wait(act, summed, step - 2)
                        before = (slot + 1) % 2
                        act.activation(msg[:, before, :, HE:TAB], zz[:, before], ACT.Exp).then_inc(exped, 1)
                run_steps(act, groups, body, lag=1)
                act.wait_ge(varied, 1)
                act.activation(t1[:, 1], t1[:, 0], ACT.Sqrt).then_inc(rooted, 1)
                act.wait_ge(centred, 1)
                act.activation(score[:], score[:], ACT.Exp).then_inc(gate_exp, 1)

            @block.tensor
            def _(pe):
                pe.wait_ge(maxed, 1)

                def body(step, slot, i):
                    if due(step, groups):
                        pe.wait_ge(coded, step + 1)
                        wait(pe, copied_t, step - 1)
                        for g in range(GROUP):
                            last = pe.transpose(one_ps[:, slot % 2, g], one[:, slot, g], C["ident"][:])
                        last.then_inc(coded_t, 1)
                    if due(step - 1, groups):
                        before = (slot + 1) % 2
                        tiles = tiles_of(nc, pe, mybir.EngineType.PE, chunk_tile, step - 1)
                        pe.wait_ge(copied_t, step)
                        wait(pe, read, step - 2)
                        for g in range(GROUP):
                            last = pe.matmul(edge_ps[:, before, g, 0:PARTS * KEYS], one_t[:, before, g],
                                             T_parts[:, bass.ds(tiles[g], 1), :].rearrange("p a f -> p (a f)"),
                                             start=True, stop=True)
                        last.then_inc(fetched, 1)
                    if due(step - 2, groups):
                        pe.wait_ge(messaged, step - 1)
                        wait(pe, added, GROUP * (step - 3))
                        for g in range(GROUP):
                            last = pe.matmul(sum_ps[:, slot % 2, g, 0:TAB], one[:, (slot + 2) % SLOTS, g],
                                             msg[:, slot % 2, g], start=True, stop=True)
                        last.then_inc(summed, 1)
                run_steps(pe, groups, body, lag=2)

            @block.vector
            def _(dve):
                chain = Chain(dve, chain_sem)
                chain.put(dve.tensor_copy(T[:, :, 0:HEADS], asd[:]))
                chain.step(dve.tensor_tensor(self_z[:], top_[:], asd[:], ALU.add))
                chain.step(dve.scalar_tensor_tensor(out=T[:, :, HEADS:KEYS], in0=self_z[:], scalar=0.2,
                                                    in1=self_z[:], op0=ALU.mult, op1=ALU.max))
                split(dve, chain, T_parts[:], T[:], T_left[:])
                chain.step(dve.tensor_tensor(self_z[:], own[:, :, HE:TAB], asd[:], ALU.add))
                chain.step(dve.scalar_tensor_tensor(out=self_z[:], in0=self_z[:], scalar=0.2, in1=self_z[:],
                                                    op0=ALU.mult, op1=ALU.max))
                dve.tensor_tensor(self_z[:], self_z[:], T[:, :, HEADS:KEYS], ALU.subtract).then_inc(maxed, 1)
                dve.wait_ge(self_exp, 1)
                chain.step(dve.tensor_tensor(heads(acc[:, :, 0:HE]), heads(own[:, :, 0:HE]),
                                             acc[:, :, HE:TAB].unsqueeze(3).to_broadcast([P, NT, HEADS, EXPERTS]),
                                             ALU.mult))

                def body(step, slot, i):
                    if due(step, groups):
                        wait(dve, summed, step - SLOTS + 1)
                        dve.tensor_tensor(one[:, slot], C["iota_f"][:, :].unsqueeze(1).to_broadcast([P, GROUP, P]),
                                          rec[:, bass.ds(step * GROUP, GROUP), 1].unsqueeze(2).to_broadcast([P, GROUP, P]),
                                          ALU.is_equal).then_inc(coded, 1)
                    if due(step - 2, groups):
                        chunks = bass.ds((step - 2) * GROUP, GROUP)
                        dve.wait_ge(exped, step - 1)
                        dve.tensor_tensor(msg[:, slot % 2, :, 0:HE].rearrange("p g (h e) -> p g h e", h=HEADS),
                                          rows[:, chunks, 0:HE].rearrange("p g (h e) -> p g h e", h=HEADS),
                                          msg[:, slot % 2, :, HE:TAB].unsqueeze(3).to_broadcast([P, GROUP, HEADS, EXPERTS]),
                                          ALU.mult).then_inc(messaged, 1)
                    if due(step - 1, groups):
                        chunks = bass.ds((step - 1) * GROUP, GROUP)
                        before = (slot + 1) % 2
                        parts = [edge_ps[:, before, :, k * KEYS:(k + 1) * KEYS] for k in range(PARTS)]
                        dve.wait_ge(fetched, step)
                        wait(dve, shifted, step - 1)
                        dve.tensor_copy(keys[:], parts[0]).then_inc(chained, 1)
                        dve.wait_ge(chained, 4 * (step - 1) + 1)
                        dve.tensor_tensor(keys[:], keys[:], parts[1], ALU.add).then_inc(chained, 1)
                        dve.wait_ge(chained, 4 * (step - 1) + 2)
                        dve.tensor_tensor(keys[:], keys[:], parts[2], ALU.add).then_inc(read, 1)
                        dve.wait_ge(read, step)
                        dve.tensor_tensor(z[:], rows[:, chunks, HE:TAB], keys[:, :, 0:HEADS], ALU.add).then_inc(chained, 1)
                        dve.wait_ge(chained, 4 * (step - 1) + 3)
                        dve.scalar_tensor_tensor(out=z[:], in0=z[:], scalar=0.2, in1=z[:],
                                                 op0=ALU.mult, op1=ALU.max).then_inc(chained, 1)
                        dve.wait_ge(chained, 4 * (step - 1) + 4)
                        dve.tensor_tensor(zz[:, before], z[:], keys[:, :, HEADS:KEYS], ALU.subtract).then_inc(shifted, 1)
                    if due(step - 3, groups):
                        tiles = tiles_of(nc, dve, mybir.EngineType.DVE, chunk_tile, step - 3)
                        dve.wait_ge(summed, step - 2)
                        for g in range(GROUP):
                            wait(dve, added, GROUP * (step - 3) + g)
                            at = acc[:, bass.ds(tiles[g], 1), :].rearrange("p a f -> p (a f)")
                            dve.tensor_tensor(at, at, sum_ps[:, (slot + 1) % 2, g, 0:TAB], ALU.add).then_inc(added, 1)
                run_steps(dve, groups, body, lag=3)
                dve.wait_ge(added, NC)
                tt, ts, red = dve.tensor_tensor, dve.tensor_scalar, dve.tensor_reduce
                wide = lambda ap: ap.unsqueeze(2).to_broadcast([P, NT, HE])
                row = lambda k: vec[:, k].unsqueeze(1).to_broadcast([P, NT, HE])
                dve.wait_ge(vec_in, 48)
                chain.step(ts(self_z[:], acc[:, :, HE:TAB], 1e-16, None, ALU.add))
                chain.step(dve.reciprocal(self_z[:], self_z[:]))
                chain.step(tt(heads(t16[:]), heads(acc[:, :, 0:HE]),
                              self_z[:].unsqueeze(3).to_broadcast([P, NT, HEADS, EXPERTS]), ALU.mult))
                chain.step(tt(t16[:], t16[:], row(0), ALU.add))
                chain.step(red(t1[:, 0], t16[:], AX.X, ALU.add))
                chain.step(ts(t1[:, 0], t1[:, 0], 1.0 / HE, None, ALU.mult))
                chain.step(tt(t16[:], t16[:], wide(t1[:, 0]), ALU.subtract))
                chain.step(tt(acc[:, :, 0:HE], t16[:], t16[:], ALU.mult))
                chain.step(red(t1[:, 0], acc[:, :, 0:HE], AX.X, ALU.add))
                ts(t1[:, 0], t1[:, 0], 1.0 / HE, LN_EPS, ALU.mult, ALU.add).then_inc(varied, 1)
                dve.wait_ge(rooted, 1)
                chain.step(dve.reciprocal(t1[:, 1], t1[:, 1]))
                chain.step(tt(t16[:], t16[:], wide(t1[:, 1]), ALU.mult))
                chain.step(tt(t16[:], t16[:], row(1), ALU.mult))
                chain.step(tt(t16[:], t16[:], row(2), ALU.add))
                chain.step(red(score[:], t16[:].rearrange("p t (h e) -> p t e h", h=HEADS), AX.X, ALU.add))
                chain.step(ts(score[:], score[:], 1.0 / HEADS, None, ALU.mult))
                chain.step(dve.memset(beaten[:], 0.0))
                for a in range(EXPERTS):
                    for b in range(a + 1, EXPERTS):
                        chain.step(tt(win[:], score[:, :, a], score[:, :, b], ALU.is_ge))
                        chain.put(tt(beaten[:, :, b], beaten[:, :, b], win[:], ALU.add))
                        chain.step(dve.scalar_tensor_tensor(out=beaten[:, :, a], in0=beaten[:, :, a], scalar=1.0,
                                                            in1=win[:], op0=ALU.add, op1=ALU.subtract))
                chain.put(ts(beaten[:], beaten[:], 1.5, None, ALU.is_lt))
                chain.step(red(t1[:, 0], score[:], AX.X, ALU.max))
                four = lambda ap: ap.unsqueeze(2).to_broadcast([P, NT, EXPERTS])
                tt(score[:], score[:], four(t1[:, 0]), ALU.subtract).then_inc(centred, 1)
                dve.wait_ge(gate_exp, 1)
                chain.step(tt(score[:], score[:], beaten[:], ALU.mult))
                chain.step(red(t1[:, 0], score[:], AX.X, ALU.add))
                chain.step(dve.reciprocal(t1[:, 0], t1[:, 0]))
                chain.step(tt(nodes["gate"][:], score[:], four(t1[:, 0]), ALU.mult))


def experts(nc, x1_d, ut_d, W1, b1, W2, b2, gate, out, C):
    FO = FF // P
    PAIR = 2
    TOK = PAIR * P
    steps = NT // PAIR
    with ExitStack() as ctx:
        sb = lambda n, sh, dt: ctx.enter_context(nc.sbuf_tensor(f"ex_{n}", sh, dt))
        ps = lambda n, sh, dt: ctx.enter_context(nc.psum_tensor(f"ex_{n}", sh, dt))
        sem = lambda n: ctx.enter_context(nc.semaphore(f"ex_{n}"))
        w1 = sb("w1", [P, EXPERTS, 2, FF], F32)
        w2 = sb("w2", [P, EXPERTS, FO, D], F32)
        b1c = sb("b1c", [P, EXPERTS * FO], F32)
        b2r = sb("b2r", [EXPERTS, D], F32)
        ut = sb("ut", [P, 2, 2, TOK], F32)
        res = sb("res", [P, 2, PAIR, D], F32)
        hid = sb("hid", [P, 2, FO, TOK], F32)
        gates = sb("gates", [P, 2, PAIR, EXPERTS], F32)
        gate_t = sb("gate_t", [EXPERTS, PAIR, P], F32)
        h_ps = ps("h_ps", [P, 4, 512], F32)
        y_ps = ps("y_ps", [P, 2, PAIR, D], F32)
        b_ps = ps("b_ps", [P, PAIR, D], F32)
        g_ps = ps("g_ps", [EXPERTS, PAIR, P], F32)
        w_in = sem("w_in")
        ut_in = [sem("ut_in0"), sem("ut_in1")]
        x_in = [sem("x_in0"), sem("x_in1")]
        stored = [sem("stored0"), sem("stored1")]
        picked = sem("picked")
        turned, taken, biased, hidden, active, mixed, combined = (sem("turned"), sem("taken"), sem("biased"),
                                                                  sem("hidden"), sem("active"), sem("mixed"),
                                                                  sem("combined"))
        block = ctx.enter_context(nc.Block())
        PER = PAIR * (EXPERTS + 1)

        def all_steps(eng, one):
            def body(i):
                one(i, 0)
                one(i, 1)
            peeled(eng, steps // 2, body)
            one(steps // 2, 0)

        @block.sync
        def _(sp):
            for e in range(EXPERTS):
                sp.dma_start(w1[:, e], W1[e].rearrange("(k p) n -> p k n", p=P)).then_inc(w_in, 16)
                sp.dma_start(w2[:, e], W2[e].rearrange("(f p) n -> p f n", p=P)).then_inc(w_in, 16)
            with nc.allow_non_contiguous_dma(reason="a bias per partition"):
                sp.dma_start(b1c[:], b1.rearrange("e (f p) -> p (e f)", p=P)).then_inc(w_in, 16)
            sp.dma_start(b2r[:], b2).then_inc(w_in, 16)

            def one(i, slot):
                step = i * 2 + slot
                wait(sp, mixed, EXPERTS * (step - 1))
                for half in range(2):
                    sp.dma_start(ut[:, slot, half], ut_d[half][:, bass.ds(step * TOK, TOK)]).then_inc(ut_in[slot], 16)
                wait(sp, stored[slot], 16 * i)
                sp.dma_start(res[:, slot], x1_d[bass.ds(step * TOK, TOK), :].rearrange("(t p) f -> p t f", p=P)
                             ).then_inc(x_in[slot], 16)
            all_steps(sp, one)

        @block.tensor
        def _(pe):
            pe.wait_ge(w_in, 16 * (2 * EXPERTS + 2))

            def first(step, slot, e):
                for f in range(FO):
                    wait(pe, active, step * 16 + e * FO + f - 3)
                    for half in range(2):
                        last = pe.matmul(h_ps[:, f, 0:TOK], w1[:, e, half, f * P:(f + 1) * P], ut[:, slot, half],
                                         start=(half == 0), stop=(half == 1))
                    last.then_inc(hidden, 1)

            def second(step, e):
                pe.wait_ge(active, step * 16 + (e + 1) * FO)
                wait(pe, combined, step * PER + PAIR * e if e >= 2 else (step - 1) * PER + PAIR * (e + 4))
                for t in range(PAIR):
                    for f in range(FO):
                        last = pe.matmul(y_ps[:, e % 2, t], hid[:, e % 2, f, t * P:(t + 1) * P], w2[:, e, f],
                                         start=(f == 0), stop=(f == FO - 1))
                last.then_inc(mixed, 1)

            def one(i, slot):
                step = i * 2 + slot
                pe.wait_ge(picked, step + 1)
                wait(pe, taken, step)
                for t in range(PAIR):
                    last = pe.transpose(g_ps[:, t], gates[:, slot, t], C["ident"][:])
                last.then_inc(turned, 1)
                pe.wait_ge(ut_in[slot], 32 * (i + 1))
                first(step, slot, 0)
                pe.wait_ge(taken, step + 1)
                wait(pe, combined, (step - 1) * PER + PAIR)
                for t in range(PAIR):
                    last = pe.matmul(b_ps[:, t], gate_t[:, t], b2r[:], start=True, stop=True)
                last.then_inc(biased, 1)
                for e in range(EXPERTS):
                    if e + 1 < EXPERTS:
                        first(step, slot, e + 1)
                    second(step, e)
            all_steps(pe, one)

        @block.scalar
        def _(act):
            def one(i, slot):
                step = i * 2 + slot
                for e in range(EXPERTS):
                    wait(act, mixed, step * EXPERTS + e - 1)
                    for f in range(FO):
                        act.wait_ge(hidden, step * 16 + e * FO + f + 1)
                        act.activation(hid[:, e % 2, f], h_ps[:, f, 0:TOK], ACT.Gelu,
                                       bias=b1c[:, e * FO + f:e * FO + f + 1]).then_inc(active, 1)
            act.wait_ge(w_in, 16 * (2 * EXPERTS + 2))
            all_steps(act, one)

        @block.vector
        def _(dve):
            def one(i, slot):
                step = i * 2 + slot
                wait(dve, turned, step - 1)
                wait(dve, combined, PER * (step - 1))
                dve.tensor_copy(gates[:, slot], gate[:, bass.ds(step * PAIR, PAIR), :]).then_inc(picked, 1)
                dve.wait_ge(picked, step + 1)
                dve.wait_ge(turned, step + 1)
                wait(dve, biased, step)
                dve.tensor_copy(gate_t[:], g_ps[:]).then_inc(taken, 1)
                dve.wait_ge(biased, step + 1)
                dve.wait_ge(x_in[slot], 16 * (i + 1))
                for t in range(PAIR):
                    dve.tensor_tensor(res[:, slot, t], res[:, slot, t], b_ps[:, t], ALU.add).then_inc(combined, 1)
                for e in range(EXPERTS):
                    dve.wait_ge(mixed, step * EXPERTS + e + 1)
                    for t in range(PAIR):
                        dve.wait_ge(combined, step * PER + PAIR * (e + 1) + t - 1)
                        dve.scalar_tensor_tensor(out=res[:, slot, t], in0=y_ps[:, e % 2, t], scalar=gates[:, slot, t, e:e + 1],
                                                 in1=res[:, slot, t], op0=ALU.mult, op1=ALU.add).then_inc(combined, 1)
            all_steps(dve, one)

        @block.gpsimd
        def _(pool):
            def one(i, slot, last=False):
                step = i * 2 + slot
                pool.wait_ge(combined, PER * (step + 1))
                pool.nop(nofuse=True)
                if not last:
                    pool.dma_start(out[bass.ds(step * TOK, TOK), :].rearrange("(t p) f -> p t f", p=P),
                                   res[:, slot]).then_inc(stored[slot], 16)
                else:
                    base = step * TOK
                    pool.dma_start(out[base:base + P, :], res[:, slot, 0]).then_inc(stored[slot], 16)
                    pool.dma_start(out[base + P:N, :], res[0:LAST, slot, 1]).then_inc(stored[slot], 16)

            def body(i):
                one(i, 0)
                one(i, 1)
            peeled(pool, steps // 2, body)
            one(steps // 2, 0, last=True)
            pool.wait_ge(stored[0], 16 * (steps // 2) + 32)
            pool.wait_ge(stored[1], 16 * (steps // 2))


_INS = ['x', 'src', 'dst', 'edge_weight', 'L0_ffn_W_gat', 'L0_ffn_att_src', 'L0_ffn_att_dst', 'L0_ffn_b_gat',
        'L0_ffn_ln_gamma', 'L0_ffn_ln_beta', 'L0_ffn_W1', 'L0_ffn_b1', 'L0_ffn_W2', 'L0_ffn_b2', 'L0_ffn_edge_index']
_OUTS = [((12500, 256), 'float32')]


def kernel(**inputs):
    import numpy as _np
    import concourse.bacc as _bacc
    from concourse import mybir as _mybir
    from concourse.bass_utils import run_bass_kernel_spmd as _run

    nc = _bacc.Bacc("TRN2", target_bir_lowering=False, num_devices=1)
    arrays, args = {}, []
    for name in _INS:
        a = _np.ascontiguousarray(inputs[name])
        arrays[f"in_{name}_dram"] = a
        args.append(nc.dram_tensor(f"in_{name}_dram", a.shape, _mybir.dt.from_np(a.dtype), kind="ExternalInput").ap())
    for i, (shape, dtype) in enumerate(_OUTS):
        dt = _mybir.dt.from_np(_np.dtype(dtype))
        args.append(nc.dram_tensor(f"out_{i}_dram", shape, dt, kind="ExternalOutput").ap())
    build(nc, *args)
    r = _run(nc, [arrays], core_ids=[0])
    return r.results[0]["out_0_dram"]
```

```python
import concourse.bass as bass
from concourse import mybir
from contextlib import ExitStack

F32 = mybir.dt.float32
BF16 = mybir.dt.bfloat16
I32 = mybir.dt.int32
ALU = mybir.AluOpType
ACT = mybir.ActivationFunctionType
AX = mybir.AxisListType

P = 128
LOG_P = 7
N = 12500
D = 256
NT = -(-N // P)
NP = NT * P
LAST = N - (NT - 1) * P
HEADS, EXPERTS = 4, 4
HE = HEADS * EXPERTS
FF = 512
LN_EPS = 1e-5
GROUP = 8
TG = 7
SORT_COLS = 16
SORT_EDGES = SORT_COLS * P
AHEAD = 2
SLOTS = 4
PARTS = 3
NO_EDGE = -2.0 ** 100
TAB = HE + HEADS
TABW = TAB + PARTS * HEADS // 2


class EdgeList:

    def __init__(self, name, edges, cols, words):
        self.name, self.edges, self.cols, self.words = name, edges, cols, words
        self.buckets = NT + (cols * P > edges)
        most = (cols * P + self.buckets * (P - 1)) // P
        self.chunks = -(-most // GROUP) * GROUP
        self.steps = cols // SORT_COLS
        assert cols % (2 * SORT_COLS) == 0 and cols % P == 0 and cols * P >= edges


def wait(eng, sem, value):
    if not isinstance(value, int) or value > 0:
        eng.wait_ge(sem, value)


def peeled(eng, steps, body):
    body(0)
    if steps > 1:
        with eng.Fori(1, steps) as i:
            body(i)


def run_steps(eng, steps, body, lag=0, unroll=4):
    rounds = steps // unroll
    for k in range(unroll):
        body(k, k, 0)
    with eng.Fori(1, rounds) as i:
        for k in range(unroll):
            body(i * unroll + k, k, i)
    for step in range(rounds * unroll, steps + lag):
        body(step, step % unroll, step // unroll)


def due(step, steps):
    return not isinstance(step, int) or 0 <= step < steps


def tiles_of(nc, eng, engine, chunk_tile, step):
    _, tiles = nc.values_load_multi_w_load_instructions(
        chunk_tile[0:1, bass.ds(step * GROUP, GROUP)], engines=(engine,), min_val=0, max_val=NT - 1,
        skip_runtime_bounds_check_because="chunk_tile is made as min(a count, NT - 1)")
    return tiles


class Chain:

    def __init__(self, eng, sem):
        self.eng, self.sem, self.count, self.loop = eng, sem, 0, 0

    def on(self, eng):
        self.eng = eng
        return self

    def step(self, ins):
        ins.then_inc(self.sem, 1)
        self.count += 1
        self.eng.wait_ge(self.sem, self.loop + self.count)

    def put(self, ins):
        ins.then_inc(self.sem, 1)
        self.count += 1

    def settle(self):
        self.eng.wait_ge(self.sem, self.loop + self.count)

    def peeled(self, steps, body):
        start = self.count
        body(0)
        self.per = per = self.count - start
        if steps > 1:
            with self.eng.Fori(1, steps) as i:
                self.loop = i * per - per
                body(i)
                assert self.count - start == 2 * per
        self.count, self.loop = start + per * steps, 0

    def rest(self, first, steps, body):
        start = self.count
        with self.eng.Fori(first, steps) as i:
            per = self.per
            self.loop = i * per - first * per
            body(i)
            assert self.count - start == per
        self.count, self.loop = start + per * (steps - first), 0

    def run(self, steps, body, unroll=4):
        start = self.count
        for k in range(unroll):
            body(k, k, 0)
        per, rounds = self.count - start, steps // unroll
        with self.eng.Fori(1, rounds) as i:
            self.loop = i * per - per
            for k in range(unroll):
                body(i * unroll + k, k, i)
            assert self.count - start == 2 * per
        self.count, self.loop = start + per * rounds, 0
        for step in range(rounds * unroll, steps):
            body(step, step % unroll, step // unroll)


def build(nc, x, src, dst, edge_weight, W_gat, att_src, att_dst, b_gat, ln_gamma, ln_beta,
          W1, b1, W2, b2, edge_index, out):
    gnn = EdgeList("gnn", src.shape[0], 1664, 3)
    gat = EdgeList("gat", edge_index.shape[1], 1024, 2)
    top = ExitStack()
    with top:
        def keep(name, shape, dt):
            return top.enter_context(nc.sbuf_tensor(name, shape, dt))

        def dram(name, shape, dt):
            return nc.dram_tensor(name, shape, dt, kind="Internal").ap()

        xs_d = dram("xs_d", (NP, D), F32)
        x1_d = dram("x1_d", (NP, D), F32)
        ut_d = [dram(f"ut_d{k}", (P, NP), F32) for k in range(2)]
        y_d = dram("y_d", (NP, EXPERTS * D), F32)
        tab_d = dram("tab_d", (NP + 1, TABW), F32)
        bucket_d = {s.name: dram(f"bucket_{s.name}", (s.cols, P), BF16) for s in (gnn, gat)}
        rec_d = {s.name: dram(f"rec_{s.name}", (P * s.chunks, s.words), F32) for s in (gnn, gat)}

        pidx = keep("pidx", [P, 1], F32)
        iota_i = keep("iota_i", [P, P], I32)
        pidx_i = keep("pidx_i", [P, 1], I32)
        iota_f = keep("iota_f", [P, P], F32)
        iota_b = keep("iota_b", [P, P], BF16)
        ident = keep("ident", [P, P], F32)
        ident_b = keep("ident_b", [P, P], BF16)
        later = keep("later", [P, P], F32)
        ones_b = keep("ones_b", [P, 1], BF16)
        ones_f = keep("ones_f", [P, 1], F32)
        dis = keep("dis", [P, NT], F32)
        chunk_tile = {"gat": keep("chunk_tile_gat", [1, gat.chunks], I32)}

        chain = Chain(None, top.enter_context(nc.semaphore("chain")))
        constants(nc, chain, pidx, pidx_i, iota_i, iota_f, iota_b, ident, ident_b, later, ones_b, ones_f)
        C = dict(chain=chain, pidx=pidx, iota_f=iota_f, iota_b=iota_b, ident=ident, ident_b=ident_b, later=later,
                 ones_b=ones_b, ones_f=ones_f)
        gat_fields = keep("gat_fields", [P, gat.cols, gat.words], F32)
        count = {s.name: keep(f"count_{s.name}", [P, 4], F32) for s in (gnn, gat)}
        nodes = dict(own=keep("own", [P, NT, TABW], F32),
                     asd=keep("asd", [P, NT, HEADS], F32),
                     top=keep("top", [P, NT, HEADS], F32),
                     gate=keep("gate", [P, NT, EXPERTS], F32))
        with ExitStack() as graph:
            chunk_tile["gnn"] = graph.enter_context(nc.sbuf_tensor("chunk_tile_gnn", [1, gnn.chunks], I32))
            with ExitStack() as lists:
                fields = lists.enter_context(nc.sbuf_tensor("gnn_fields", [P, gnn.cols, gnn.words], F32))
                digits = lists.enter_context(nc.sbuf_tensor("gnn_digits", [P, 2, gnn.cols], BF16))
                tile_of_edge = lists.enter_context(nc.sbuf_tensor("gnn_tile_of_edge", [P, gnn.cols], BF16))
                prepare_sort(nc, gnn, src, dst, edge_weight, fields, tile_of_edge, digits, bucket_d["gnn"],
                             rec_d["gnn"], C)
                prepare_sort(nc, gat, edge_index[1], edge_index[0], None, gat_fields, None, None, bucket_d["gat"],
                             rec_d["gat"], C)
                count_edges(nc, gnn, tile_of_edge, count["gnn"], C)
                sort_and_degrees(nc, gnn, fields, digits, count["gnn"], bucket_d["gnn"], rec_d["gnn"], chunk_tile["gnn"],
                                 dis, gat, count["gat"], bucket_d["gat"], C)
            scaled_layernorm(nc, x, xs_d, dis, C)
            agg = graph.enter_context(nc.sbuf_tensor("agg", [P, NT, D], F32))
            neighbour_sum(nc, gnn, xs_d, rec_d["gnn"], chunk_tile["gnn"], agg, C)
            router_table(nc, x, agg, dis, x1_d, ut_d, W_gat, att_src, att_dst, tab_d, nodes, C)
        rec = keep("rec", [P, gat.chunks + AHEAD * GROUP, 2], F32)
        rows = keep("rows", [P, gat.chunks, TAB], F32)
        with ExitStack() as both:
            experts = Experts(nc, both, ut_d, y_d)
            done = sort_beside_experts(nc, gat, gat_fields, count["gat"], bucket_d["gat"], rec_d["gat"],
                                       chunk_tile["gat"], experts, (W1, b1, W2, b2),
                                       rows[:].rearrange("p c f -> p (c f)"), C)
            greatest_scores(nc, gat, tab_d, rec_d["gat"], chunk_tile["gat"], rec, rows, gat_fields, nodes, experts,
                            done, C)
        attention(nc, gat, rec, rows, chunk_tile["gat"], nodes, b_gat, ln_gamma, ln_beta, C)
        combine(nc, x1_d, y_d, nodes["gate"], out)


def constants(nc, the_chain, pidx, pidx_i, iota_i, iota_f, iota_b, ident, ident_b, later, ones_b, ones_f):
    with nc.semaphore("counted") as counted, nc.Block() as block:
        @block.gpsimd
        def _(pool):
            pool.iota(iota_i[:], pattern=[[1, P]], base=0, channel_multiplier=0).then_inc(counted, 1)
            pool.iota(pidx_i[:], pattern=[[0, 1]], base=0, channel_multiplier=1).then_inc(counted, 1)

        @block.vector
        def _(dve):
            chain = the_chain.on(dve)
            dve.memset(ones_b[:], 1.0)
            dve.memset(ones_f[:], 1.0)
            dve.wait_ge(counted, 2)
            chain.put(dve.tensor_copy(iota_f[:], iota_i[:]))
            chain.put(dve.tensor_copy(iota_b[:], iota_i[:]))
            chain.put(dve.tensor_copy(pidx[:], pidx_i[:]))
            chain.settle()
            dve.tensor_scalar(ident[:], iota_f[:], pidx[:, 0:1], None, ALU.is_equal)
            dve.tensor_scalar(ident_b[:], iota_f[:], pidx[:, 0:1], None, ALU.is_equal)
            dve.tensor_scalar(later[:], iota_f[:], pidx[:, 0:1], None, ALU.is_gt)


def load_edges(eng, s, tile, array, sem):
    full = s.edges // s.cols
    if full == P:
        eng.dma_start(tile[:, :], array.rearrange("(p c) -> p c", p=P)).then_inc(sem, 16)
        return 16
    assert full == P - 1
    eng.dma_start(tile[0:full, :], array[0:full * s.cols].rearrange("(p c) -> p c", p=full)).then_inc(sem, 16)
    rest = s.edges - full * s.cols
    eng.dma_start(tile[full:P, 0:rest], array[full * s.cols:s.edges].rearrange("(p c) -> p c", p=1)).then_inc(sem, 16)
    return 32


def layernorm_stats(dve, chain, tiles, stats, mv, k0=0):
    for k in range(tiles.shape[1]):
        chain.put(dve.bn_stats(stats[:, k], tiles[:, k]))
    chain.settle()
    dve.nop(nofuse=True)
    for k in range(tiles.shape[1]):
        chain.put(dve.bn_aggr(mv[:, k], stats[:, k]))
    chain.settle()


def node_rows(array, i):
    return array[bass.ds(i * TG * P, TG * P), :].rearrange("(t p) f -> p t f", p=P)


def load_nodes(sp, tile, x, i, last, sem):
    if not last:
        sp.dma_start(tile, node_rows(x, i)).then_inc(sem, 32)
    else:
        base = i * TG * P
        whole = base + (TG - 1) * P
        sp.dma_start(tile[:, 0:TG - 1], x[base:whole, :].rearrange("(t p) f -> p t f", p=P)).then_inc(sem, 16)
        sp.dma_start(tile[0:LAST, TG - 1], x[whole:N, :]).then_inc(sem, 16)


def scaled_layernorm(nc, x, xs_d, dis, C):
    steps = NT // TG
    with ExitStack() as ctx:
        sb = lambda n, sh, dt: ctx.enter_context(nc.sbuf_tensor(n, sh, dt))
        sem = lambda n: ctx.enter_context(nc.semaphore(n))
        xin = sb("sl_x", [P, 2, TG, D], F32)
        xout = sb("sl_out", [P, 2, TG, D], F32)
        stats = sb("sl_stats", [P, TG, 6], F32)
        mv = sb("sl_mv", [P, TG, 2], F32)
        var = sb("sl_var", [P, TG], F32)
        root = sb("sl_root", [P, TG], F32)
        scale = sb("sl_scale", [P, TG], F32)
        loaded = [sem("sl_loaded0"), sem("sl_loaded1")]
        stored = [sem("sl_stored0"), sem("sl_stored1")]
        ready, rooted, normed, cleared = (sem("sl_var_ready"), sem("sl_rooted"), sem("sl_normed"),
                                          sem("sl_cleared"))
        block = ctx.enter_context(nc.Block())

        @block.sync
        def _(sp):
            def one(i, slot, last=False):
                step = i * 2 + slot
                wait(sp, normed, TG * (step - 1))
                load_nodes(sp, xin[:, slot], x, step, last, loaded[slot])

            def body(i):
                one(i, 0)
                one(i, 1)
            peeled(sp, steps // 2 - 1, body)
            one(steps // 2 - 1, 0)
            sp.wait_ge(cleared, 1)
            one(steps // 2 - 1, 1, last=True)

        @block.vector
        def _(dve):
            chain = C["chain"].on(dve)

            def one(i, slot):
                step = i * 2 + slot
                dve.wait_ge(loaded[slot], i * 32 + 32)
                layernorm_stats(dve, chain, xin[:, slot], stats, mv)
                chain.put(dve.tensor_scalar(var[:], mv[:, :, 1], LN_EPS, None, ALU.add))
                chain.settle()
                dve.tensor_copy(var[:], var[:]).then_inc(ready, 1)
                dve.wait_ge(rooted, step + 1)
                chain.step(dve.reciprocal(scale[:], root[:]))
                chain.step(dve.tensor_tensor(scale[:], scale[:], dis[:, bass.ds(step * TG, TG)], ALU.mult))
                wait(dve, stored[slot], 16 * i)
                for k in range(TG):
                    dve.tensor_scalar(xout[:, slot, k], xin[:, slot, k], mv[:, k, 0:1], scale[:, k:k + 1],
                                      ALU.subtract, ALU.mult).then_inc(normed, 1)
                dve.wait_ge(normed, TG * step + TG)

            def body(i):
                one(i, 0)
                one(i, 1)
            chain.peeled(steps // 2 - 1, body)
            one(steps // 2 - 1, 0)
            dve.memset(xin[:, 1, TG - 1], 0.0).then_inc(cleared, 1)
            one(steps // 2 - 1, 1)

        @block.scalar
        def _(act):
            def body(i):
                for slot in range(2):
                    act.wait_ge(ready, i * 2 + slot + 1)
                    act.activation(root[:], var[:], ACT.Sqrt).then_inc(rooted, 1)
                    act.wait_ge(normed, TG * (i * 2 + slot + 1))
                    act.dma_start(node_rows(xs_d, i * 2 + slot), xout[:, slot]).then_inc(stored[slot], 16)
            peeled(act, steps // 2, body)
            for slot in range(2):
                act.wait_ge(stored[slot], 16 * (steps // 2))


def prepare_sort(nc, s, key_a, other_a, weight_a, fields, tile_of_edge, degree_digits, bucket_d, rec_d, C):
    NC = s.chunks
    blocks = s.cols // P
    with ExitStack() as c1:
        sb = lambda n, sh, dt: c1.enter_context(nc.sbuf_tensor(f"{s.name}_{n}", sh, dt))
        sem1 = lambda n: c1.enter_context(nc.semaphore(f"{s.name}_{n}"))
        empty = sb("empty", [P, NC, s.words], F32)
        key = sb("key", [P, s.cols], I32)
        other = sb("other", [P, s.cols], I32)
        weight = sb("weight", [P, s.cols], F32) if weight_a is not None else None
        digit = sb("digit", [P, s.cols], I32)
        hi = sb("hi", [P, s.cols], F32)
        hi_t = sb("hi_t", [P, blocks, P], BF16)
        pt = c1.enter_context(nc.psum_tensor(f"{s.name}_pt", [P, 2, 512], F32))
        filled, loaded, split_, turned, taken, saved, blank = (
            sem1("filled"), sem1("loaded"), sem1("split"), sem1("turned"), sem1("taken"),
            sem1("saved"), sem1("blank"))
        block = c1.enter_context(nc.Block())

        @block.sync
        def _(sp):
            sp.wait_ge(filled, s.words)
            load_edges(sp, s, key, key_a, loaded)
            load_edges(sp, s, other, other_a, loaded)
            if weight is not None:
                load_edges(sp, s, weight, weight_a, loaded)
            sp.wait_ge(blank, 2)
            sp.dma_start(rec_d.rearrange("(p c) w -> p (c w)", p=P),
                         empty[:, :, :].rearrange("p c w -> p (c w)")).then_inc(saved, 16)
            sp.wait_ge(taken, blocks)
            sp.dma_start(bucket_d.rearrange("(b t) p -> t b p", t=P), hi_t[:]).then_inc(saved, 16)
            sp.wait_ge(saved, 32)

        @block.gpsimd
        def _(pool):
            pool.memset(empty[:], 0.0).then_inc(blank, 1)
            pool.wait_ge(blank, 1)
            if weight is None:
                pool.memset(empty[:, :, 0], float(NP)).then_inc(blank, 1)
            else:
                pool.sem_inc(blank, 1)

        @block.vector
        def _(dve):
            chain = C["chain"].on(dve)
            dve.memset(key[:], NP).then_inc(filled, 1)
            dve.memset(other[:], NP).then_inc(filled, 1)
            if weight is not None:
                dve.memset(weight[:], 0.0).then_inc(filled, 1)
            per = 16 if s.edges == s.cols * P else 32
            dve.wait_ge(loaded, per * s.words)
            chain.step(dve.tensor_scalar(digit[:], key[:], LOG_P, None, ALU.logical_shift_right))
            dve.tensor_copy(hi[:], digit[:]).then_inc(split_, 1)
            dve.wait_ge(split_, 1)
            if tile_of_edge is not None:
                chain.step(dve.tensor_copy(tile_of_edge[:], digit[:]))
            chain.step(dve.tensor_scalar(digit[:], key[:], P - 1, None, ALU.bitwise_and))
            chain.put(dve.tensor_copy(fields[:, :, 1], digit[:]))
            chain.step(dve.tensor_scalar(fields[:, :, 0], other[:], float(NP - 1), None, ALU.min))
            if weight is not None:
                dve.tensor_copy(fields[:, :, 2], weight[:])
            if degree_digits is not None:
                chain.step(dve.tensor_scalar(digit[:], other[:], LOG_P, None, ALU.logical_shift_right))
                chain.step(dve.tensor_copy(degree_digits[:, 0], digit[:]))
                chain.step(dve.tensor_scalar(digit[:], other[:], P - 1, None, ALU.bitwise_and))
                chain.step(dve.tensor_copy(degree_digits[:, 1], digit[:]))
            for b in range(blocks):
                dve.wait_ge(turned, b + 1)
                dve.tensor_copy(hi_t[:, b], pt[:, b % 2, 0:P]).then_inc(taken, 1)

        @block.tensor
        def _(pe):
            pe.wait_ge(split_, 1)
            for b in range(blocks):
                wait(pe, taken, b - 1)
                pe.transpose(pt[:, b % 2, 0:P], hi[:, b * P:(b + 1) * P], C["ident"][:]).then_inc(turned, 1)


class EdgeCount:

    def __init__(self, nc, ctx, s, count, bucket_d, C):
        self.s, self.count, self.C = s, count, C
        self.flat = bucket_d.rearrange("c p -> (c p)")
        self.keys = ctx.enter_context(nc.sbuf_tensor(f"{s.name}_c_keys", [P, 2, SORT_EDGES], BF16))
        self.match = ctx.enter_context(nc.sbuf_tensor(f"{s.name}_c_match", [P, SORT_EDGES], BF16))
        sem = lambda n: ctx.enter_context(nc.semaphore(f"{s.name}_c_{n}"))
        self.keys_in = [sem("keys_in0"), sem("keys_in1")]
        self.keys_used, self.summed = sem("keys_used"), sem("summed")

    def load_keys(self, sp, step, slot):
        wait(sp, self.keys_used, step - 1)
        B = self.s.buckets
        sp.dma_start(self.keys[0:B, slot], self.flat[bass.ds(step * SORT_EDGES, SORT_EDGES)]
                     .partition_broadcast(B)).then_inc(self.keys_in[slot], 16)

    def add(self, dve, step, slot, i):
        B, count = self.s.buckets, self.count
        dve.wait_ge(self.keys_in[slot], i * 16 + 16)
        wait(dve, self.keys_used, step)
        dve.tensor_scalar(self.match[0:B, :], self.keys[0:B, slot], self.C["pidx"][0:B, 0:1], None,
                          ALU.is_equal, ALU.add, accum_out=count[0:B, slot:slot + 1]).then_inc(self.keys_used, 1)
        dve.wait_ge(self.keys_used, step + 1)
        wait(dve, self.summed, step)
        dve.tensor_tensor(count[0:B, 2:3], count[0:B, 2:3], count[0:B, slot:slot + 1], ALU.add).then_inc(self.summed, 1)


def count_edges(nc, s, tile_of_edge, count, C):
    B, RING = s.buckets, 4
    with ExitStack() as ctx:
        match = ctx.enter_context(nc.sbuf_tensor("count_match", [P, RING, s.cols], BF16))
        tally = ctx.enter_context(nc.sbuf_tensor("count_tally", [P, B], F32))
        total = ctx.enter_context(nc.psum_tensor("count_total", [P, 512], F32))
        tallied, summed = (ctx.enter_context(nc.semaphore(f"count_{n}")) for n in ("tallied", "summed"))
        block = ctx.enter_context(nc.Block())

        @block.vector
        def _(dve):
            def body(step, slot, i):
                wait(dve, tallied, step - RING + 1)
                dve.tensor_scalar(match[:, slot], tile_of_edge[:], C["iota_f"][:, bass.ds(step, 1)], None,
                                  ALU.is_equal, ALU.add, accum_out=tally[:, bass.ds(step, 1)]).then_inc(tallied, 1)
            run_steps(dve, B, body)
            dve.wait_ge(summed, 1)
            dve.tensor_copy(count[0:B, 2:3], total[0:B, 0:1])

        @block.tensor
        def _(pe):
            pe.wait_ge(tallied, B)
            pe.matmul(total[0:B, 0:1], tally[:], C["ones_f"][:], start=True, stop=True).then_inc(summed, 1)


class EdgeSort:

    def __init__(self, nc, ctx, s, fields, count, bucket_d, rec_d, chunk_tile, C, room=None):
        sb = lambda n, sh, dt: ctx.enter_context(nc.sbuf_tensor(f"{s.name}_{n}", sh, dt))
        ps = lambda n, sh, dt: ctx.enter_context(nc.psum_tensor(f"{s.name}_{n}", sh, dt))
        sem = lambda n: ctx.enter_context(nc.semaphore(f"{s.name}_{n}"))
        self.s, self.fields, self.rec_d, self.chunk_tile, self.C = s, fields, rec_d, chunk_tile, C
        self.flat = bucket_d.rearrange("c p -> (c p)")
        NC, W = s.chunks, s.words
        if room is None:
            room = sb("room", [P, 6 * SORT_EDGES], F32)
        two = lambda ap: ap.rearrange("p (k e) -> p k e", k=2)
        E = SORT_EDGES
        self.keys = two(room[:, 0:E].bitcast(BF16))
        self.match = two(room[:, E:2 * E].bitcast(BF16))
        self.run = two(room[:, 2 * E:4 * E])
        self.slots = two(room[:, 4 * E:6 * E])
        self.count = count
        self.small_i = sb("small_i", [P, 2], I32)
        self.need_f = sb("need_f", [P, 1], F32)
        self.end_f = sb("end_f", [P, 1], F32)
        self.chunk_no = sb("chunk_no", [P, NC], I32)
        self.past = sb("past", [P, NC], BF16)
        self.place = sb("place", [P, SORT_COLS], I32)
        self.lane = sb("lane", [P, SORT_COLS], I32)
        self.index = sb("index", [P, 2, SORT_COLS], I32)
        self.record = sb("record", [P, 2, SORT_COLS, W], F32)
        self.pos_ps = ps("pos_ps", [P, 2, 512], F32)
        self.keys_in = [sem("keys_in0"), sem("keys_in1")]
        self.scattered = [sem("scattered0"), sem("scattered1")]
        (self.keys_used, self.numbered, self.needed, self.started, self.pasted, self.tiled, self.tiles_read,
         self.masked, self.summed, self.placed, self.staged) = (
            sem(n) for n in ("keys_used", "numbered", "needed", "started", "pasted", "tiled", "tiles_read",
                             "masked", "summed", "placed", "staged"))

    def load_keys(self, sp, step, slot):
        wait(sp, self.keys_used, step - 1)
        B = self.s.buckets
        sp.dma_start(self.keys[0:B, slot], self.flat[bass.ds(step * SORT_EDGES, SORT_EDGES)]
                     .partition_broadcast(B)).then_inc(self.keys_in[slot], 16)

    def number_chunks(self, pool):
        pool.iota(self.chunk_no[:], pattern=[[1, self.s.chunks]], base=0, channel_multiplier=0).then_inc(self.numbered, 1)

    def scatter(self, pool, step, slot):
        pool.wait_ge(self.placed, step + 1)
        pool.wait_ge(self.staged, step + 1)
        pool.nop(nofuse=True)
        for c in range(SORT_COLS):
            pool.indirect_dma_start(self.rec_d, bass.IndirectOffsetOnAxis(ap=self.index[:, slot, c:c + 1], axis=0),
                                    self.record[:, slot, c], None).then_inc(self.scattered[slot], 16)

    def scattered_all(self, pool):
        for slot in range(2):
            pool.wait_ge(self.scattered[slot], 16 * SORT_COLS * (self.s.steps // 2))

    def stage(self, act, step, slot, i):
        wait(act, self.scattered[slot], 16 * SORT_COLS * i)
        act.activation(self.record[:, slot], self.fields[:, bass.ds(step * SORT_COLS, SORT_COLS), :],
                       ACT.Copy).then_inc(self.staged, 1)

    def start_pe(self, pe):
        B, NC = self.s.buckets, self.s.chunks
        pe.wait_ge(self.needed, 1)
        pe.matmul(self.pos_ps[0:B, 0, 0:1], self.C["later"][0:B, 0:B], self.need_f[0:B, :],
                  start=True, stop=True).then_inc(self.started, 1)
        pe.wait_ge(self.pasted, 1)
        for n, c in enumerate(range(0, NC, 512)):
            w = min(512, NC - c)
            wait(pe, self.tiles_read, n)
            pe.matmul(self.pos_ps[0:1, 0, 0:w], self.C["ones_b"][0:B, :], self.past[0:B, c:c + w],
                      start=True, stop=True).then_inc(self.tiled, 1)
        pe.wait_ge(self.tiles_read, -(-NC // 512))

    def sum_slots(self, pe, step, slot):
        B = self.s.buckets
        pe.wait_ge(self.masked, step + 1)
        for c in range(SORT_COLS):
            last = pe.matmul(self.pos_ps[:, slot, c:c + 1], self.slots[0:B, slot, c * P:(c + 1) * P],
                             self.C["ones_f"][0:B, :], start=True, stop=True)
        last.then_inc(self.summed, 1)

    def start_dve(self, dve, chain):
        s, B, NC, small_i = self.s, self.s.buckets, self.s.chunks, self.small_i
        chain.step(dve.tensor_scalar(small_i[0:B, 0:1], self.count[0:B, 2:3], float(P - 1), None, ALU.add))
        chain.step(dve.tensor_scalar(small_i[0:B, 1:2], small_i[0:B, 0:1], LOG_P, None, ALU.logical_shift_right))
        dve.tensor_copy(self.need_f[0:B, :], small_i[0:B, 1:2]).then_inc(self.needed, 1)
        dve.wait_ge(self.started, 1)
        chain.put(dve.tensor_scalar(self.run[0:B, 1, SORT_EDGES - 1:SORT_EDGES], self.pos_ps[0:B, 0, 0:1], float(P), -1.0,
                                    ALU.mult, ALU.add))
        chain.step(dve.tensor_tensor(self.end_f[0:B, :], self.pos_ps[0:B, 0, 0:1], self.need_f[0:B, :], ALU.add))
        dve.wait_ge(self.numbered, 1)
        dve.tensor_scalar(self.past[0:B, :], self.chunk_no[0:B, :], self.end_f[0:B, 0:1], None,
                          ALU.is_ge).then_inc(self.pasted, 1)
        for n, c in enumerate(range(0, NC, 512)):
            w = min(512, NC - c)
            dve.wait_ge(self.tiled, n + 1)
            dve.tensor_scalar(self.chunk_tile[:, c:c + w], self.pos_ps[0:1, 0, 0:w], float(NT - 1), None,
                              ALU.min).then_inc(self.tiles_read, 1)

    def rank(self, dve, chain, step, slot, i):
        B, s = self.s.buckets, self.s
        dve.wait_ge(self.keys_in[slot], i * 16 + 16)
        dve.tensor_scalar(self.match[0:B, slot], self.keys[0:B, slot], self.C["pidx"][0:B, 0:1], None,
                          ALU.is_equal).then_inc(self.keys_used, 1)
        dve.wait_ge(self.keys_used, step + 1)
        chain.step(dve.tensor_tensor_scan(self.run[0:B, slot], self.match[0:B, slot], self.match[0:B, slot],
                                          self.run[0:B, 1 - slot, SORT_EDGES - 1:SORT_EDGES], ALU.add, ALU.max))
        wait(dve, self.summed, step - 1)
        dve.tensor_tensor(self.slots[0:B, slot], self.run[0:B, slot], self.match[0:B, slot],
                          ALU.mult).then_inc(self.masked, 1)

    def address(self, dve, chain, step, slot, i):
        place, lane = self.place, self.lane
        dve.wait_ge(self.summed, step + 1)
        chain.step(dve.tensor_copy(place[:], self.pos_ps[:, slot, 0:SORT_COLS]))
        chain.step(dve.tensor_scalar(lane[:], place[:], P - 1, None, ALU.bitwise_and))
        chain.step(dve.tensor_scalar(place[:], place[:], LOG_P, None, ALU.logical_shift_right))
        wait(dve, self.scattered[slot], 16 * SORT_COLS * i)
        dve.scalar_tensor_tensor(out=self.index[:, slot], in0=lane[:], scalar=float(self.s.chunks), in1=place[:],
                                 op0=ALU.mult, op1=ALU.add).then_inc(self.placed, 1)
        dve.wait_ge(self.placed, step + 1)


def sort_and_degrees(nc, s, fields, digits, count, bucket_d, rec_d, chunk_tile, dis, later_list, later_count,
                     later_bucket_d, C):
    HALF = SORT_COLS // 2
    with ExitStack() as ctx:
        sb = lambda n, sh, dt: ctx.enter_context(nc.sbuf_tensor(f"deg_{n}", sh, dt))
        sem = lambda n: ctx.enter_context(nc.semaphore(f"deg_{n}"))
        one_hi = sb("one_hi", [P, 2, HALF, NT], BF16)
        one_lo = sb("one_lo", [P, 2, HALF, P], BF16)
        zeros = sb("zeros", [P, P], BF16)
        deg = sb("deg", [P, NT], F32)
        root = sb("root", [P, NT], F32)
        hist = ctx.enter_context(nc.psum_tensor("deg_hist", [P, 512], F32))[:, 0:NT]
        chain_sem, cleared, coded, counted, total, clipped, rooted = (
            sem("chain"), sem("cleared"), sem("coded"), sem("counted"), sem("total"), sem("clipped"), sem("rooted"))
        sort = EdgeSort(nc, ctx, s, fields, count, bucket_d, rec_d, chunk_tile, C)
        counting = EdgeCount(nc, ctx, later_list, later_count, later_bucket_d, C)
        block = ctx.enter_context(nc.Block())
        both, rounds = later_list.steps // 2, s.steps // 2
        assert both < rounds

        @block.sync
        def _(sp):
            def body(i, counts):
                for slot in range(2):
                    sort.load_keys(sp, i * 2 + slot, slot)
                    if counts:
                        counting.load_keys(sp, i * 2 + slot, slot)
            peeled(sp, both, lambda i: body(i, True))
            with sp.Fori(both, rounds) as i:
                body(i, False)

        @block.gpsimd
        def _(pool):
            sort.number_chunks(pool)

            def body(i):
                for slot in range(2):
                    sort.scatter(pool, i * 2 + slot, slot)
            peeled(pool, s.steps // 2, body)
            sort.scattered_all(pool)

        @block.scalar
        def _(act):
            def body(i):
                for slot in range(2):
                    sort.stage(act, i * 2 + slot, slot, i)
            peeled(act, s.steps // 2, body)
            act.wait_ge(clipped, 1)
            act.activation(root[:], deg[:], ACT.Sqrt).then_inc(rooted, 1)

        @block.tensor
        def _(pe):
            sort.start_pe(pe)
            pe.wait_ge(cleared, 1)
            pe.matmul(hist, zeros[:], zeros[:, 0:NT], start=True, stop=False)

            def body(i):
                for slot in range(2):
                    step = i * 2 + slot
                    sort.sum_slots(pe, step, slot)
                    for half in range(2):
                        pe.wait_ge(coded, 4 * step + 2 * half + 2)
                        for g in range(HALF):
                            last = pe.matmul(hist, one_lo[:, half, g], one_hi[:, half, g], start=False, stop=False)
                        last.then_inc(counted, 1)
            peeled(pe, s.steps // 2, body)
            pe.matmul(hist, zeros[:], zeros[:, 0:NT], start=False, stop=True).then_inc(total, 1)

        @block.vector
        def _(dve):
            chain = Chain(dve, chain_sem)
            dve.memset(zeros[:], 0.0).then_inc(cleared, 1)
            chain.step(dve.memset(later_count[:], 0.0))
            sort.start_dve(dve, chain)

            def body(i, counts):
                for slot in range(2):
                    step = i * 2 + slot
                    sort.rank(dve, chain, step, slot, i)
                    if counts:
                        counting.add(dve, step, slot, i)
                    for half in range(2):
                        cols = bass.ds(step * SORT_COLS + half * HALF, HALF)
                        wait(dve, counted, 2 * step + half - 1)
                        dve.tensor_tensor(one_hi[:, half], C["iota_b"][:, 0:NT].unsqueeze(1).to_broadcast([P, HALF, NT]),
                                          digits[:, 0, cols].unsqueeze(2).to_broadcast([P, HALF, NT]),
                                          ALU.is_equal).then_inc(coded, 1)
                        dve.tensor_tensor(one_lo[:, half], C["iota_b"][:, :].unsqueeze(1).to_broadcast([P, HALF, P]),
                                          digits[:, 1, cols].unsqueeze(2).to_broadcast([P, HALF, P]),
                                          ALU.is_equal).then_inc(coded, 1)
                    sort.address(dve, chain, step, slot, i)
            chain.peeled(both, lambda i: body(i, True))
            chain.rest(both, rounds, lambda i: body(i, False))
            dve.wait_ge(total, 1)
            dve.tensor_scalar(deg[:], hist, 1.0, None, ALU.max).then_inc(clipped, 1)
            dve.wait_ge(rooted, 1)
            dve.reciprocal(dis[:], root[:])


def neighbour_sum(nc, s, xs_d, rec_d, chunk_tile, agg, C):
    NC, W = s.chunks, s.words
    groups = NC // GROUP
    BANKS = 8
    with ExitStack() as ctx:
        sb = lambda n, sh, dt: ctx.enter_context(nc.sbuf_tensor(f"ns_{n}", sh, dt))
        sem = lambda n: ctx.enter_context(nc.semaphore(f"ns_{n}"))
        rec = sb("rec", [P, NC + AHEAD * GROUP, W], F32)
        got = sb("got", [P, SLOTS, GROUP, D], F32)
        spread = sb("spread", [P, 2, GROUP, P], F32)
        index = sb("index", [P, SLOTS, GROUP], I32)
        field = sb("field", [P, SLOTS, GROUP, 2], F32)
        part = ctx.enter_context(nc.psum_tensor("ns_part", [P, BANKS, 512], F32))
        rec_in, cleared, indexed, added, spreads, multiplied = (
            sem("rec_in"), sem("cleared"), sem("indexed"), sem("added"), sem("spreads"), sem("multiplied"))
        gathered = [sem(f"gathered{k}") for k in range(SLOTS)]
        block = ctx.enter_context(nc.Block())

        @block.sync
        def _(sp):
            sp.dma_start(rec[:, 0:NC, :].rearrange("p c w -> p (c w)"),
                         rec_d.rearrange("(p c) w -> p (c w)", p=P)).then_inc(rec_in, 16)

        @block.gpsimd
        def _(pool):
            def body(step, slot, i):
                wait(pool, multiplied, GROUP * (step - SLOTS + 1))
                pool.wait_ge(indexed, 2 * (step + 1))
                pool.nop(nofuse=True)
                for g in range(GROUP):
                    pool.indirect_dma_start(got[:, slot, g], None, xs_d,
                                            bass.IndirectOffsetOnAxis(ap=index[:, slot, g:g + 1], axis=0)
                                            ).then_inc(gathered[slot], 16)
            run_steps(pool, groups, body)

        @block.scalar
        def _(act):
            act.wait_ge(rec_in, 16)
            act.wait_ge(cleared, 1)

            def fields(step, slot, i):
                chunks = bass.ds(step * GROUP, GROUP)
                wait(act, gathered[slot], 16 * GROUP * i)
                act.activation(index[:, slot], rec[:, chunks, 0], ACT.Copy).then_inc(indexed, 1)
                wait(act, spreads, GROUP * (step - SLOTS + 1))
                act.activation(field[:, slot], rec[:, chunks, 1:3], ACT.Copy).then_inc(indexed, 1)
            run_steps(act, groups, fields)

        @block.tensor
        def _(pe):
            def body(step, slot, i):
                pe.wait_ge(gathered[slot], 16 * GROUP * (i + 1))
                for g in range(GROUP):
                    done = step * GROUP + g
                    pe.wait_ge(spreads, done + 1)
                    wait(pe, added, done + 1 - BANKS)
                    pe.matmul(part[:, g, 0:D], spread[:, slot % 2, g], got[:, slot, g],
                              start=True, stop=True).then_inc(multiplied, 1)
            run_steps(pe, groups, body)

        @block.vector
        def _(dve):
            dve.memset(rec[:, NC:, :], 0.0).then_inc(cleared, 1)
            dve.memset(agg[:], 0.0).then_inc(cleared, 1)
            dve.wait_ge(cleared, 2)

            def body(step, slot, i):
                if due(step, groups):
                    dve.wait_ge(indexed, 2 * (step + 1))
                    wait(dve, multiplied, GROUP * (step - 1))
                    for g in range(GROUP):
                        dve.tensor_scalar(spread[:, slot % 2, g], C["iota_f"][:], field[:, slot, g, 0:1],
                                          field[:, slot, g, 1:2], ALU.is_equal, ALU.mult).then_inc(spreads, 1)
                if due(step - 1, groups):
                    tiles = tiles_of(nc, dve, mybir.EngineType.DVE, chunk_tile, step - 1)
                    for g in range(GROUP):
                        dve.wait_ge(multiplied, (step - 1) * GROUP + g + 1)
                        wait(dve, added, (step - 1) * GROUP + g)
                        at = agg[:, bass.ds(tiles[g], 1), :].rearrange("p a f -> p (a f)")
                        dve.tensor_tensor(at, at, part[:, g, 0:D], ALU.add).then_inc(added, 1)
            run_steps(dve, groups, body, lag=1)
            dve.wait_ge(added, NC)


def split(dve, chain, parts, whole, left):
    w = whole.shape[-1]
    part = [parts[:, :, k * w:(k + 1) * w] for k in range(PARTS)]
    chain.step(dve.tensor_copy(part[0], whole))
    chain.step(dve.tensor_tensor(left, whole, part[0], ALU.subtract))
    chain.step(dve.tensor_copy(part[1], left))
    chain.step(dve.tensor_tensor(left, left, part[1], ALU.subtract))
    chain.step(dve.tensor_copy(part[2], left))


def router_table(nc, x, agg, dis, x1_d, ut_d, W_gat, att_src, att_dst, tab_d, nodes, C):
    steps = NT // TG
    with ExitStack() as ctx:
        sb = lambda n, sh, dt: ctx.enter_context(nc.sbuf_tensor(f"rt_{n}", sh, dt))
        sem = lambda n: ctx.enter_context(nc.semaphore(f"rt_{n}"))
        xin = sb("x", [P, 2, TG, D], F32)
        u = sb("u", [P, 2, TG, D], F32)
        ut = sb("ut", [P, 2, TG, 2, P], F32)
        wg = sb("wg", [P, 2, HE], F32)
        att = sb("att", [P, 2, HE], F32)
        stats = sb("stats", [P, TG, 6], F32)
        mv = sb("mv", [P, TG, 2], F32)
        var = sb("var", [P, TG], F32)
        root = sb("root", [P, TG], F32)
        scale = sb("scale", [P, TG], F32)
        prod = sb("prod", [P, NT, HE], F32)
        left = sb("left", [P, NT, HEADS], F32)
        blank = sb("blank", [1, TABW], F32)
        turned = ctx.enter_context(nc.psum_tensor("rt_turned", [P, 16, P], F32))
        h_ps = ctx.enter_context(nc.psum_tensor("rt_h", [P, TG, HE], F32))
        weights_in = sem("weights_in")
        x_in = [sem("x_in0"), sem("x_in1")]
        x_out = [sem("x_out0"), sem("x_out1")]
        cleared, summed = sem("cleared"), sem("summed")
        ut_out = [sem("ut_out0"), sem("ut_out1")]
        var_ready, rooted, normed, transposed, ut_ready, h_ready, h_taken, table_ready, table_out, blanked = (
            sem("var_ready"), sem("rooted"), sem("normed"), sem("transposed"), sem("ut_ready"),
            sem("h_ready"), sem("h_taken"), sem("table_ready"), sem("table_out"), sem("blanked"))
        block = ctx.enter_context(nc.Block())
        own = nodes["own"]

        @block.sync
        def _(sp):
            sp.dma_start(wg[:], W_gat.rearrange("(k p) n -> p k n", p=P)).then_inc(weights_in, 16)
            sp.dma_start(att[:, 0], att_src.rearrange("h e -> (h e)").partition_broadcast(P)).then_inc(weights_in, 16)
            sp.dma_start(att[:, 1], att_dst.rearrange("h e -> (h e)").partition_broadcast(P)).then_inc(weights_in, 16)

            sp.wait_ge(cleared, 1)

            def one(i, slot, last=False):
                wait(sp, normed, TG * (2 * i + slot - 1))
                sp.nop(nofuse=True)
                wait(sp, x_out[slot], 16 * i)
                load_nodes(sp, xin[:, slot], x, i * 2 + slot, last, x_in[slot])

            def body(i):
                one(i, 0)
                one(i, 1)
            peeled(sp, steps // 2 - 1, body)
            one(steps // 2 - 1, 0)
            one(steps // 2 - 1, 1, last=True)
            sp.wait_ge(table_ready, 3)
            sp.dma_start(tab_d[0:NP, :].rearrange("(t p) f -> p t f", p=P), own[:]).then_inc(table_out, 16)
            sp.wait_ge(blanked, 4)
            sp.dma_start(tab_d[NP:NP + 1, :], blank[:]).then_inc(table_out, 16)
            sp.wait_ge(table_out, 32)

        @block.vector
        def _(dve):
            chain = C["chain"].on(dve)
            dve.memset(blank[:, 0:HE], 0.0).then_inc(blanked, 1)
            dve.memset(blank[:, HE:TAB], NO_EDGE).then_inc(blanked, 1)
            blank_parts = blank[:, TAB:TABW].bitcast(BF16)
            dve.memset(blank_parts[:, 0:HEADS], NO_EDGE).then_inc(blanked, 1)
            dve.memset(blank_parts[:, HEADS:], 0.0).then_inc(blanked, 1)

            dve.memset(xin[:, 1, TG - 1], 0.0).then_inc(cleared, 1)

            def take_h(step):
                dve.wait_ge(h_ready, step + 1)
                dve.tensor_copy(own[:, bass.ds(step * TG, TG), 0:HE], h_ps[:]).then_inc(h_taken, 1)

            def body(i):
                for slot in range(2):
                    step = i * 2 + slot
                    dve.wait_ge(x_in[slot], i * 32 + 32)
                    for k in range(TG):
                        tile = step * TG + k
                        dve.scalar_tensor_tensor(
                            out=xin[:, slot, k], in0=agg[:, bass.ds(tile, 1), :].rearrange("p a f -> p (a f)"),
                            scalar=dis[:, bass.ds(tile, 1)], in1=xin[:, slot, k],
                            op0=ALU.mult, op1=ALU.add).then_inc(summed, 1)
                    dve.wait_ge(summed, TG * step + TG)
                    dve.nop(nofuse=True)
                    layernorm_stats(dve, chain, xin[:, slot], stats, mv)
                    dve.tensor_scalar(var[:], mv[:, :, 1], LN_EPS, None, ALU.add).then_inc(var_ready, 1)
                    dve.wait_ge(rooted, step + 1)
                    chain.step(dve.reciprocal(scale[:], root[:]))
                    wait(dve, transposed, step - 1)
                    for k in range(TG):
                        dve.tensor_scalar(u[:, slot, k], xin[:, slot, k], mv[:, k, 0:1], scale[:, k:k + 1],
                                          ALU.subtract, ALU.mult).then_inc(normed, 1)
                    dve.wait_ge(normed, TG * step + TG)
                    if due(step - 2, steps):
                        take_h(step - 2)
            chain.peeled(steps // 2, body)
            take_h(steps - 2)
            take_h(steps - 1)
            dve.wait_ge(h_taken, steps)
            dve.wait_ge(weights_in, 48)
            for k, target in ((0, own[:, :, HE:TAB]), (1, nodes["asd"][:])):
                chain.step(dve.tensor_tensor(prod[:], own[:, :, 0:HE],
                                             att[:, k].unsqueeze(1).to_broadcast([P, NT, HE]), ALU.mult))
                dve.tensor_reduce(target, prod[:, :, :].rearrange("p t (h e) -> p t h e", h=HEADS), AX.X,
                                  ALU.add).then_inc(table_ready, 1)
                dve.wait_ge(table_ready, k + 1)
            split(dve, chain, own[:, :, TAB:TABW].bitcast(BF16), own[:, :, HE:TAB], left[:])
            dve.sem_inc(table_ready, 1)

        @block.tensor
        def _(pe):
            pe.wait_ge(weights_in, 48)

            def project(step, slot):
                pe.wait_ge(ut_ready, step + 1)
                wait(pe, h_taken, step)
                for k in range(TG):
                    for half in range(2):
                        last = pe.matmul(h_ps[:, k], ut[:, slot, k, half], wg[:, half],
                                         start=(half == 0), stop=(half == 1))
                last.then_inc(h_ready, 1)

            def body(i):
                for slot in range(2):
                    step = i * 2 + slot
                    pe.wait_ge(normed, TG * step + TG)
                    wait(pe, ut_ready, step)
                    for k in range(TG):
                        for half in range(2):
                            last = pe.transpose(turned[:, 2 * k + half], u[:, slot, k, half * P:(half + 1) * P],
                                                C["ident"][:])
                    last.then_inc(transposed, 1)
                    if due(step - 1, steps):
                        project(step - 1, 1 - slot)
            peeled(pe, steps // 2, body)
            project(steps - 1, 1)

        @block.scalar
        def _(act):
            def body(i):
                for slot in range(2):
                    step = i * 2 + slot
                    act.wait_ge(summed, TG * step + TG)
                    act.dma_start(node_rows(x1_d, step), xin[:, slot]).then_inc(x_out[slot], 16)
                    act.wait_ge(var_ready, step + 1)
                    act.activation(root[:], var[:], ACT.Sqrt).then_inc(rooted, 1)
                    act.wait_ge(transposed, step + 1)
                    wait(act, h_ready, step - 1)
                    wait(act, ut_out[slot], 32 * i)
                    act.activation(ut[:, slot].rearrange("p k h q -> p (k h) q"), turned[:, 0:2 * TG],
                                   ACT.Copy).then_inc(ut_ready, 1)
                    act.wait_ge(ut_ready, step + 1)
                    for half in range(2):
                        act.dma_start(ut_d[half][:, bass.ds(step * TG * P, TG * P)].rearrange("p (k q) -> p k q", q=P),
                                      ut[:, slot, :, half]).then_inc(ut_out[slot], 16)
            peeled(act, steps // 2, body)
            for slot in range(2):
                act.wait_ge(ut_out[slot], 32 * (steps // 2))
                act.wait_ge(x_out[slot], 16 * (steps // 2))


def greatest_scores(nc, s, tab_d, rec_d, chunk_tile, rec, rows, fields, nodes, experts, done, C):
    NC = s.chunks
    groups = NC // GROUP
    HALF = GROUP // 2
    LOOP = 16
    PER = 8
    TURNS = 4
    HIGH, LOW = 8, 16
    top_, own = nodes["top"], nodes["own"]
    assert LOOP == 2 * PER and done % 2 == 0 and (experts.STEPS - done) * PER < groups

    def expert_step(slot, i):
        return 2 * i + (done + slot // PER)

    def expert_due(step, slot, i):
        return not isinstance(step, int) or 0 <= step < PER * (experts.STEPS - done)

    with ExitStack() as ctx:
        sb = lambda n, sh, dt: ctx.enter_context(nc.sbuf_tensor(f"am_{n}", sh, dt))
        ps = lambda n, sh, dt: ctx.enter_context(nc.psum_tensor(f"am_{n}", sh, dt))
        sem = lambda n: ctx.enter_context(nc.semaphore(f"am_{n}"))
        K = PARTS * HEADS + HIGH + LOW
        got = sb("got", [P, SLOTS, GROUP, TABW + (HIGH + LOW) // 2], F32)
        index = sb("index", [P, SLOTS, GROUP], I32)
        digit_room = fields[:].rearrange("p c w -> p (c w)").bitcast(BF16)
        high, low = digit_room[:, 0:NC], digit_room[:, NC:2 * NC]
        side_t = sb("side_t", [K, 2, GROUP * P], BF16)
        head_n = sb("head_n", [P, HEADS, K], BF16)
        head = sb("head", [K, HEADS, P], BF16)
        digit = sb("digit", [P, 2], F32)
        most = sb("most", [P, HEADS, GROUP], F32)
        other = sb("other", [P, LOW], F32)
        tops = sb("tops", [P, TURNS, NT, HEADS], F32)
        side_ps = ps("side_ps", [K, 2, GROUP * P], BF16)
        spread = ps("spread", [P, 2, HALF, P], F32)
        rec_in, ready, cleared = sem("rec_in"), sem("ready"), sem("cleared")
        indexed, coded, turned, copied_t, copied, spreads, reduced, topped = (
            sem("indexed"), sem("coded"), sem("turned"), sem("copied_t"), sem("copied"), sem("spreads"),
            sem("reduced"), sem("topped"))
        gathered = [sem(f"gathered{k}") for k in range(SLOTS)]
        block = ctx.enter_context(nc.Block())

        @block.sync
        def _(sp):
            sp.dma_start(rec[:, 0:NC, :].rearrange("p c w -> p (c w)"),
                         rec_d.rearrange("(p c) w -> p (c w)", p=P)).then_inc(rec_in, 16)
            with sp.Fori(done // 2, experts.STEPS // 2) as i:
                for slot in range(2):
                    experts.store(sp, i * 2 + slot, slot)
            assert experts.STEPS % 2
            experts.store(sp, experts.STEPS - 1, 0)
            experts.stored_all(sp)

        @block.gpsimd
        def _(pool):
            def body(step, slot, i):
                wait(pool, copied, step - SLOTS + 1)
                wait(pool, turned, step - SLOTS + 1)
                pool.wait_ge(indexed, step + 1)
                pool.nop(nofuse=True)
                for g in range(GROUP):
                    pool.indirect_dma_start(got[:, slot, g, 0:TABW], None, tab_d,
                                            bass.IndirectOffsetOnAxis(ap=index[:, slot, g:g + 1], axis=0)
                                            ).then_inc(gathered[slot], 16)
            run_steps(pool, groups, body)

        @block.scalar
        def _(act):
            act.wait_ge(rec_in, 16)
            act.wait_ge(cleared, 1)

            def fields(step, slot, i):
                turn = i * (LOOP // SLOTS) + slot // SLOTS
                wait(act, gathered[slot % SLOTS], 16 * GROUP * turn)
                act.activation(index[:, slot % SLOTS], rec[:, bass.ds(step * GROUP, GROUP), 0],
                               ACT.Copy).then_inc(indexed, 1)

            def body(step, slot, i):
                fields(step + AHEAD, slot + AHEAD, i)
                act.wait_ge(turned, step + 1)
                wait(act, spreads, 8 * (step - 1))
                act.activation(side_t[:, slot % 2], side_ps[:, slot % 2], ACT.Copy).then_inc(copied_t, 1)
                act.activation(rows[:, bass.ds(step * GROUP, GROUP), :], got[:, slot % SLOTS, :, 0:TAB],
                               ACT.Copy).then_inc(copied, 1)
                if expert_due(step, slot, i):
                    if slot % PER == 0 and not (isinstance(step, int) and expert_step(slot, i) == experts.STEPS - 1):
                        experts.load(act, expert_step(slot, i) + 1, (slot // PER + 1) % 2)
                    outputs, e = experts.UNITS[slot % PER]
                    if not outputs:
                        experts.activate(act, expert_step(slot, i), e)
            for k in range(AHEAD):
                fields(k, k, 0)
            run_steps(act, groups, body, unroll=LOOP)

        @block.tensor
        def _(pe):
            pe.wait_ge(ready, 1)
            for h in range(HEADS):
                last = pe.transpose(side_ps[:, 0, h * P:(h + 1) * P], head_n[:, h], C["ident_b"][:])
            last.then_inc(ready, 1)
            pe.wait_ge(ready, 3)

            def body(step, slot, i):
                if due(step, groups):
                    pe.wait_ge(gathered[slot % SLOTS], 16 * GROUP * (i * (LOOP // SLOTS) + slot // SLOTS + 1))
                    pe.wait_ge(coded, 2 * (step + 1))
                    wait(pe, copied_t, step - 1)
                    pe.nop(nofuse=True)
                    for g in range(GROUP):
                        last = pe.transpose(side_ps[:, slot % 2, g * P:(g + 1) * P],
                                            got[:, slot % SLOTS, g, TAB:].bitcast(BF16), C["ident_b"][:])
                    last.then_inc(turned, 1)
                for unit in range(8):
                    if due(step - 1, groups):
                        half, h = unit // HEADS, unit % HEADS
                        if unit == 0:
                            pe.wait_ge(copied_t, step)
                        wait(pe, reduced, 8 * (step - 1) + unit - 1)
                        pe.matmul(spread[:, unit % 2].rearrange("p c q -> p (c q)"), head[:, h],
                                  side_t[:, (slot + 1) % 2, half * HALF * P:(half + 1) * HALF * P],
                                  start=True, stop=True).then_inc(spreads, 1)
                    if expert_due(step, slot, i):
                        experts.product(pe, expert_step(slot, i), slot // PER, i + done // 2, slot % PER, unit)
            run_steps(pe, groups, body, lag=1, unroll=LOOP)

        @block.vector
        def _(dve):
            chain = C["chain"].on(dve)
            dve.memset(rec[:, NC:, :], 0.0).then_inc(cleared, 1)

            def digits(hi, lo, number):
                chain.step(dve.tensor_scalar(hi, number, float(LOW), None, ALU.is_ge))
                for k in range(2, HIGH):
                    chain.step(dve.scalar_tensor_tensor(out=hi, in0=number, scalar=float(k * LOW), in1=hi,
                                                        op0=ALU.is_ge, op1=ALU.add))
                chain.step(dve.scalar_tensor_tensor(out=lo, in0=hi, scalar=-float(LOW), in1=number,
                                                    op0=ALU.mult, op1=ALU.add))
            chain.put(dve.memset(head_n[:], 0.0))
            digits(digit[:, 0:1], digit[:, 1:2], C["pidx"][:, 0:1])
            for h in range(HEADS):
                for k in range(PARTS):
                    chain.put(dve.memset(head_n[:, h, k * HEADS + h:k * HEADS + h + 1], 1.0))
            at = PARTS * HEADS
            for k, width in enumerate((HIGH, LOW)):
                chain.step(dve.tensor_scalar(other[:, 0:width], C["iota_f"][:, 0:width], digit[:, k:k + 1], None, ALU.is_equal))
                chain.step(dve.tensor_scalar(other[:, 0:width], other[:, 0:width], -NO_EDGE, NO_EDGE, ALU.mult, ALU.add))
                chain.step(dve.tensor_copy(head_n[:, :, at:at + width], other[:, 0:width].unsqueeze(1).to_broadcast([P, HEADS, width])))
                at += width
            dve.memset(most[:], 0.0).then_inc(ready, 1)
            dve.wait_ge(ready, 2)
            dve.tensor_copy(head[:].rearrange("k h n -> k (h n)"), side_ps[:, 0, 0:HEADS * P]).then_inc(ready, 1)
            dve.wait_ge(rec_in, 16)
            digits(high, low, rec[:, 0:NC, 1])
            for g in range(TURNS):
                chain.put(dve.tensor_copy(tops[:, g], own[:, :, HE:TAB]))
            chain.settle()

            def body(step, slot, i):
                if due(step, groups):
                    wait(dve, turned, step - SLOTS + 1)
                    chunks = bass.ds(step * GROUP, GROUP)
                    for number, first, width in ((high, TABW, HIGH), (low, TABW + HIGH // 2, LOW)):
                        dve.tensor_tensor(got[:, slot % SLOTS, :, first:first + width // 2].bitcast(BF16),
                                          C["iota_b"][:, 0:width].unsqueeze(1).to_broadcast([P, GROUP, width]),
                                          number[:, chunks].unsqueeze(2).to_broadcast([P, GROUP, width]),
                                          ALU.is_equal).then_inc(coded, 1)
                if due(step - 2, groups):
                    tiles = tiles_of(nc, dve, mybir.EngineType.DVE, chunk_tile, step - 2)
                    wait(dve, topped, GROUP * (step - 2))
                    for unit in range(8):
                        half, h = unit // HEADS, unit % HEADS
                        dve.wait_ge(spreads, 8 * (step - 2) + unit + 1)
                        dve.tensor_reduce(most[:, h, half * HALF:(half + 1) * HALF], spread[:, unit % 2],
                                          AX.X, ALU.max).then_inc(reduced, 1)
                last_slot, turn = (slot - 1, i) if slot else (LOOP - 1, i - 1)
                if expert_due(step - 1, last_slot, turn):
                    outputs, e = experts.UNITS[last_slot % PER]
                    if outputs:
                        experts.take(dve, expert_step(last_slot, turn), last_slot // PER, turn + done // 2, e)
                if due(step - 2, groups):
                    dve.wait_ge(reduced, 8 * (step - 1))
                    for g in range(GROUP):
                        if g == TURNS:
                            dve.wait_ge(topped, GROUP * (step - 2) + TURNS)
                        at = tops[:, g % TURNS, bass.ds(tiles[g], 1), :].rearrange("p a f -> p (a f)")
                        dve.tensor_tensor(at, at, most[:, :, g], ALU.max).then_inc(topped, 1)
            run_steps(dve, groups, body, lag=2, unroll=LOOP)
            dve.wait_ge(topped, NC)
            dve.tensor_reduce(top_[:], tops[:].rearrange("p g t h -> p t h g"), AX.X, ALU.max)


def attention(nc, s, rec, rows, chunk_tile, nodes, b_gat, ln_gamma, ln_beta, C):
    NC = s.chunks
    groups = NC // GROUP
    TURNS = 4
    LOOP = 8
    KEYS = 2 * HEADS
    top_, own, asd = nodes["top"], nodes["own"], nodes["asd"]
    with ExitStack() as ctx:
        sb = lambda n, sh, dt: ctx.enter_context(nc.sbuf_tensor(f"as_{n}", sh, dt))
        ps = lambda n, sh, dt: ctx.enter_context(nc.psum_tensor(f"as_{n}", sh, dt))
        sem = lambda n: ctx.enter_context(nc.semaphore(f"as_{n}"))
        RING = 4
        one = sb("one", [P, LOOP, GROUP, P], BF16)
        one_t = sb("one_t", [P, 2, GROUP, P], BF16)
        T = sb("T", [P, NT, KEYS], F32)
        T_parts = sb("T_parts", [P, NT, PARTS * KEYS], BF16)
        keys = sb("keys", [P, GROUP, KEYS], F32)
        z = sb("z", [P, GROUP, HEADS], F32)
        zz = sb("zz", [P, 2, GROUP, HEADS], F32)
        msg = sb("msg", [P, RING, GROUP, TAB], F32)
        left = sb("left", [P, RING, GROUP, TAB], F32)
        msg_parts = sb("msg_parts", [P, RING, GROUP, PARTS, TAB], BF16)
        sums = sb("sums", [P, 2, GROUP, TAB], F32)
        accs = sb("accs", [P, TURNS, NT, TAB], F32)
        acc = accs[:, 0]
        self_z = sb("self_z", [P, NT, HEADS], F32)
        vec = sb("vec", [P, 3, HE], F32)
        flat = one[:].rearrange("p s g q -> p (s g q)").bitcast(F32)
        t16 = flat[:, 0:NT * HE].rearrange("p (t f) -> p t f", t=NT)
        score = flat[:, 2048:2048 + NT * EXPERTS].rearrange("p (t f) -> p t f", t=NT)
        beaten = flat[:, 3072:3072 + NT * EXPERTS].rearrange("p (t f) -> p t f", t=NT)
        win = flat[:, 3488:3488 + NT]
        t1 = flat[:, 3616:3616 + 2 * NT].rearrange("p (k t) -> p k t", k=2)
        T_left = flat[:, 0:NT * KEYS].rearrange("p (t f) -> p t f", t=NT)
        one_ps = ps("one_ps", [P, 2, GROUP, P], BF16)
        edge_ps = ps("edge_ps", [P, 2, GROUP, 64], F32)
        sum_ps = ps("sum_ps", [P, 2, GROUP, 64], F32)
        vec_in, asked, answered = sem("vec_in"), sem("asked"), sem("answered")
        coded, coded_t, copied_t, fetched, read, shifted, exped, messaged, summed, added = (
            sem("coded"), sem("coded_t"), sem("copied_t"), sem("fetched"), sem("read"),
            sem("shifted"), sem("exped"), sem("messaged"), sem("summed"), sem("added"))
        headed, lefted, middled, lowed, taken = sem("headed"), sem("lefted"), sem("middled"), sem("lowed"), sem("taken")
        chained, started = sem("chained"), sem("started")
        block = ctx.enter_context(nc.Block())
        heads = lambda ap: ap.rearrange("p t (h e) -> p t h e", h=HEADS)

        @block.sync
        def _(sp):
            for k, v in enumerate((b_gat, ln_gamma, ln_beta)):
                sp.dma_start(vec[:, k], v.partition_broadcast(P)).then_inc(vec_in, 16)

        @block.gpsimd
        def _(pool):
            pool.wait_ge(started, 1)

            def body(step, slot, i):
                j, k = step - 6, slot - 6
                if due(j, groups):
                    pool.wait_ge(middled, j + 1)
                    pool.tensor_tensor(msg_parts[:, k % RING, :, 2, :], left[:, k % RING],
                                       msg_parts[:, k % RING, :, 1, :], ALU.subtract).then_inc(lowed, 1)
                j, k = step - 8, slot - 8
                if due(j, groups):
                    tiles = tiles_of(nc, pool, mybir.EngineType.Pool, chunk_tile, j)
                    pool.wait_ge(taken, j + 1)
                    for g in range(GROUP):
                        if g % TURNS == 0:
                            wait(pool, added, GROUP * j + g)
                        at = accs[:, g % TURNS, bass.ds(tiles[g], 1), :].rearrange("p a f -> p (a f)")
                        pool.tensor_tensor(at, at, sums[:, k % 2, g], ALU.add).then_inc(added, 1)
            run_steps(pool, groups, body, lag=8, unroll=LOOP)

        @block.scalar
        def _(act):
            act.wait_ge(asked, 1)
            act.activation(acc[:, :, HE:TAB], self_z[:], ACT.Exp).then_inc(answered, 1)

            def body(step, slot, i):
                if due(step, groups):
                    act.wait_ge(coded_t, step + 1)
                    wait(act, fetched, step - 1)
                    act.activation(one_t[:, slot % 2], one_ps[:, slot % 2], ACT.Copy).then_inc(copied_t, 1)
                j, k = step - 3, slot - 3
                if due(j, groups):
                    act.wait_ge(shifted, j + 1)
                    wait(act, lefted, j + 1 - RING)
                    act.activation(msg[:, k % RING, :, HE:TAB], zz[:, k % 2], ACT.Exp).then_inc(exped, 1)
                j, k = step - 4, slot - 4
                if due(j, groups):
                    act.wait_ge(messaged, j + 1)
                    wait(act, summed, j + 1 - RING)
                    act.activation(msg_parts[:, k % RING, :, 0, :], msg[:, k % RING], ACT.Copy).then_inc(headed, 1)
                j, k = step - 5, slot - 5
                if due(j, groups):
                    act.wait_ge(lefted, j + 1)
                    act.activation(msg_parts[:, k % RING, :, 1, :], left[:, k % RING], ACT.Copy).then_inc(middled, 1)
                j, k = step - 7, slot - 7
                if due(j, groups):
                    act.wait_ge(summed, j + 1)
                    wait(act, added, GROUP * (j - 1))
                    act.activation(sums[:, k % 2], sum_ps[:, k % 2, :, 0:TAB], ACT.Copy).then_inc(taken, 1)
            run_steps(act, groups, body, lag=7, unroll=LOOP)
            act.wait_ge(asked, 2)
            act.activation(t1[:, 1], t1[:, 0], ACT.Sqrt).then_inc(answered, 1)
            act.wait_ge(asked, 3)
            act.activation(score[:], score[:], ACT.Exp).then_inc(answered, 1)

        @block.tensor
        def _(pe):
            pe.wait_ge(asked, 1)

            def body(step, slot, i):
                j, k = step - 2, slot - 2
                if due(j, groups):
                    tiles = tiles_of(nc, pe, mybir.EngineType.PE, chunk_tile, j)
                    pe.wait_ge(copied_t, j + 1)
                    wait(pe, read, j - 1)
                    for g in range(GROUP):
                        last = pe.matmul(edge_ps[:, k % 2, g, 0:PARTS * KEYS], one_t[:, k % 2, g],
                                         T_parts[:, bass.ds(tiles[g], 1), :].rearrange("p a f -> p (a f)"),
                                         start=True, stop=True)
                    last.then_inc(fetched, 1)
                j, k = step - 7, slot - 7
                if due(j, groups):
                    pe.wait_ge(lowed, j + 1)
                    wait(pe, taken, j - 1)
                    for g in range(GROUP):
                        for part in range(PARTS):
                            last = pe.matmul(sum_ps[:, k % 2, g, 0:TAB], one[:, k % LOOP, g],
                                             msg_parts[:, k % RING, g, part], start=(part == 0),
                                             stop=(part == PARTS - 1))
                    last.then_inc(summed, 1)
                if due(step, groups):
                    pe.wait_ge(coded, step + 1)
                    wait(pe, copied_t, step - 1)
                    for g in range(GROUP):
                        last = pe.transpose(one_ps[:, slot % 2, g], one[:, slot, g], C["ident_b"][:])
                    last.then_inc(coded_t, 1)
            run_steps(pe, groups, body, lag=7, unroll=LOOP)

        @block.vector
        def _(dve):
            chain = C["chain"].on(dve)
            chain.put(dve.memset(accs[:, 1:], 0.0))
            chain.put(dve.tensor_copy(T[:, :, 0:HEADS], asd[:]))
            chain.step(dve.tensor_tensor(self_z[:], top_[:], asd[:], ALU.add))
            chain.step(dve.scalar_tensor_tensor(out=T[:, :, HEADS:KEYS], in0=self_z[:], scalar=0.2,
                                                in1=self_z[:], op0=ALU.mult, op1=ALU.max))
            split(dve, chain, T_parts[:], T[:], T_left[:])
            chain.step(dve.tensor_tensor(self_z[:], own[:, :, HE:TAB], asd[:], ALU.add))
            chain.step(dve.scalar_tensor_tensor(out=self_z[:], in0=self_z[:], scalar=0.2, in1=self_z[:],
                                                op0=ALU.mult, op1=ALU.max))
            dve.tensor_tensor(self_z[:], self_z[:], T[:, :, HEADS:KEYS], ALU.subtract).then_inc(asked, 1)
            dve.wait_ge(answered, 1)
            dve.tensor_tensor(heads(acc[:, :, 0:HE]), heads(own[:, :, 0:HE]),
                              acc[:, :, HE:TAB].unsqueeze(3).to_broadcast([P, NT, HEADS, EXPERTS]),
                              ALU.mult).then_inc(started, 1)

            def body(step, slot, i):
                at, turn = step - 3, (slot - 3) % 2
                if due(at, groups):
                    parts = edge_ps[:, turn, :, 0:PARTS * KEYS].rearrange("p g (k w) -> p g w k", k=PARTS)
                    dve.wait_ge(fetched, at + 1)
                    wait(dve, shifted, at)
                    dve.tensor_reduce(keys[:], parts, AX.X, ALU.add).then_inc(read, 1)
                if due(step, groups):
                    wait(dve, summed, step - LOOP + 1)
                    dve.tensor_tensor(one[:, slot], C["iota_b"][:, :].unsqueeze(1).to_broadcast([P, GROUP, P]),
                                      rec[:, bass.ds(step * GROUP, GROUP), 1].unsqueeze(2).to_broadcast([P, GROUP, P]),
                                      ALU.is_equal).then_inc(coded, 1)
                if due(at, groups):
                    dve.wait_ge(read, at + 1)
                    dve.tensor_tensor(z[:], rows[:, bass.ds(at * GROUP, GROUP), HE:TAB], keys[:, :, 0:HEADS],
                                      ALU.add).then_inc(chained, 1)
                j, k = step - 5, slot - 5
                if due(j, groups):
                    dve.wait_ge(headed, j + 1)
                    wait(dve, lowed, j + 1 - RING)
                    dve.tensor_tensor(left[:, k % RING], msg[:, k % RING], msg_parts[:, k % RING, :, 0, :],
                                      ALU.subtract).then_inc(lefted, 1)
                if due(at, groups):
                    dve.wait_ge(chained, 2 * at + 1)
                    dve.scalar_tensor_tensor(out=z[:], in0=z[:], scalar=0.2, in1=z[:],
                                             op0=ALU.mult, op1=ALU.max).then_inc(chained, 1)
                j, k = step - 4, slot - 4
                if due(j, groups):
                    dve.wait_ge(exped, j + 1)
                    dve.tensor_tensor(msg[:, k % RING, :, 0:HE].rearrange("p g (h e) -> p g h e", h=HEADS),
                                      rows[:, bass.ds(j * GROUP, GROUP), 0:HE].rearrange("p g (h e) -> p g h e", h=HEADS),
                                      msg[:, k % RING, :, HE:TAB].unsqueeze(3).to_broadcast([P, GROUP, HEADS, EXPERTS]),
                                      ALU.mult).then_inc(messaged, 1)
                if due(at, groups):
                    dve.wait_ge(chained, 2 * at + 2)
                    dve.tensor_tensor(zz[:, turn], z[:], keys[:, :, HEADS:KEYS], ALU.subtract).then_inc(shifted, 1)
            run_steps(dve, groups, body, lag=5, unroll=LOOP)
            dve.wait_ge(added, NC)
            chain.put(dve.tensor_tensor(accs[:, 0], accs[:, 0], accs[:, 1], ALU.add))
            chain.step(dve.tensor_tensor(accs[:, 2], accs[:, 2], accs[:, 3], ALU.add))
            chain.step(dve.tensor_tensor(accs[:, 0], accs[:, 0], accs[:, 2], ALU.add))
            tt, ts, red = dve.tensor_tensor, dve.tensor_scalar, dve.tensor_reduce
            wide = lambda ap: ap.unsqueeze(2).to_broadcast([P, NT, HE])
            row = lambda k: vec[:, k].unsqueeze(1).to_broadcast([P, NT, HE])
            dve.wait_ge(vec_in, 48)
            chain.step(ts(self_z[:], acc[:, :, HE:TAB], 1e-16, None, ALU.add))
            chain.step(dve.reciprocal(self_z[:], self_z[:]))
            chain.step(tt(heads(t16[:]), heads(acc[:, :, 0:HE]),
                          self_z[:].unsqueeze(3).to_broadcast([P, NT, HEADS, EXPERTS]), ALU.mult))
            chain.step(tt(t16[:], t16[:], row(0), ALU.add))
            chain.step(red(t1[:, 0], t16[:], AX.X, ALU.add))
            chain.step(ts(t1[:, 0], t1[:, 0], 1.0 / HE, None, ALU.mult))
            chain.step(tt(t16[:], t16[:], wide(t1[:, 0]), ALU.subtract))
            chain.step(tt(acc[:, :, 0:HE], t16[:], t16[:], ALU.mult))
            chain.step(red(t1[:, 0], acc[:, :, 0:HE], AX.X, ALU.add))
            ts(t1[:, 0], t1[:, 0], 1.0 / HE, LN_EPS, ALU.mult, ALU.add).then_inc(asked, 1)
            dve.wait_ge(answered, 2)
            chain.step(dve.reciprocal(t1[:, 1], t1[:, 1]))
            chain.step(tt(t16[:], t16[:], wide(t1[:, 1]), ALU.mult))
            chain.step(tt(t16[:], t16[:], row(1), ALU.mult))
            chain.step(tt(t16[:], t16[:], row(2), ALU.add))
            chain.step(red(score[:], t16[:].rearrange("p t (h e) -> p t e h", h=HEADS), AX.X, ALU.add))
            chain.step(ts(score[:], score[:], 1.0 / HEADS, None, ALU.mult))
            chain.step(dve.memset(beaten[:], 0.0))
            for a in range(EXPERTS):
                for b in range(a + 1, EXPERTS):
                    chain.step(tt(win[:], score[:, :, a], score[:, :, b], ALU.is_ge))
                    chain.put(tt(beaten[:, :, b], beaten[:, :, b], win[:], ALU.add))
                    chain.step(dve.scalar_tensor_tensor(out=beaten[:, :, a], in0=beaten[:, :, a], scalar=1.0,
                                                        in1=win[:], op0=ALU.add, op1=ALU.subtract))
            chain.put(ts(beaten[:], beaten[:], 1.5, None, ALU.is_lt))
            chain.step(red(t1[:, 0], score[:], AX.X, ALU.max))
            four = lambda ap: ap.unsqueeze(2).to_broadcast([P, NT, EXPERTS])
            tt(score[:], score[:], four(t1[:, 0]), ALU.subtract).then_inc(asked, 1)
            dve.wait_ge(answered, 3)
            chain.step(tt(score[:], score[:], beaten[:], ALU.mult))
            chain.step(red(t1[:, 0], score[:], AX.X, ALU.add))
            chain.step(dve.reciprocal(t1[:, 0], t1[:, 0]))
            chain.step(tt(nodes["gate"][:], score[:], four(t1[:, 0]), ALU.mult))


class Experts:
    PAIR = 2
    TOK = PAIR * P
    FO = FF // P
    HID = EXPERTS * FF // P
    STEPS = NT // PAIR
    UNITS = ((0, 0), (0, 1), (1, 0), (0, 2), (1, 1), (0, 3), (1, 2), (1, 3))

    def __init__(self, nc, ctx, ut_d, y_d):
        sb = lambda n, sh, dt: ctx.enter_context(nc.sbuf_tensor(f"ex_{n}", sh, dt))
        ps = lambda n, sh, dt: ctx.enter_context(nc.psum_tensor(f"ex_{n}", sh, dt))
        sem = lambda n: ctx.enter_context(nc.semaphore(f"ex_{n}"))
        self.ut_d, self.y_d = ut_d, y_d
        self.w1 = sb("w1", [P, EXPERTS, 2, FF], F32)
        self.w2 = sb("w2", [P, EXPERTS, self.FO, D], F32)
        self.b1c = sb("b1c", [P, self.HID], F32)
        self.b2r = sb("b2r", [P, EXPERTS, D], F32)
        self.ut = sb("ut", [P, 2, 2, self.TOK], F32)
        self.y = sb("y", [P, 2, self.PAIR, EXPERTS * D], F32)
        self.hid = sb("hid", [P, 2, self.FO, self.TOK], F32)
        self.h_ps = ps("h_ps", [P, 2, 2, self.TOK], F32)
        self.y_ps = ps("y_ps", [P, 2, self.PAIR, D], F32)
        self.w_in = sem("w_in")
        self.ut_in = [sem("ut_in0"), sem("ut_in1")]
        self.stored = [sem("stored0"), sem("stored1")]
        self.hidden, self.active, self.mixed, self.taken = sem("hidden"), sem("active"), sem("mixed"), sem("taken")

    def load_weights(self, nc, sp, W1, b1, W2, b2):
        for e in range(EXPERTS):
            sp.dma_start(self.w1[:, e], W1[e].rearrange("(k p) n -> p k n", p=P)).then_inc(self.w_in, 16)
            sp.dma_start(self.w2[:, e], W2[e].rearrange("(f p) n -> p f n", p=P)).then_inc(self.w_in, 16)
            sp.dma_start(self.b2r[:, e], b2[e].partition_broadcast(P)).then_inc(self.w_in, 16)
        with nc.allow_non_contiguous_dma(reason="a bias per partition"):
            sp.dma_start(self.b1c[:], b1.rearrange("e (f p) -> p (e f)", p=P)).then_inc(self.w_in, 16)

    def weights_loaded(self, eng):
        eng.wait_ge(self.w_in, 16 * (3 * EXPERTS + 1))

    def load(self, act, step, slot):
        wait(act, self.mixed, EXPERTS * (step - 1))
        for half in range(2):
            act.dma_start(self.ut[:, slot, half], self.ut_d[half][:, bass.ds(step * self.TOK, self.TOK)]
                          ).then_inc(self.ut_in[slot], 16)

    def product(self, pe, step, slot, i, unit, n):
        outputs, e = self.UNITS[unit]
        if outputs:
            t, f = n // self.FO, n % self.FO
            if n == 0:
                pe.wait_ge(self.active, step * self.HID + (e + 1) * self.FO)
                wait(pe, self.taken, step * EXPERTS + e - 1)
            last = pe.matmul(self.y_ps[:, e % 2, t], self.hid[:, e % 2, f, t * P:(t + 1) * P], self.w2[:, e, f],
                             start=(f == 0), stop=(f == self.FO - 1))
            if n == 7:
                last.then_inc(self.mixed, 1)
        else:
            f, half = n // 2, n % 2
            if unit == 0 and n == 0:
                pe.wait_ge(self.ut_in[slot], 32 * (i + 1))
            if n % 4 == 0:
                wait(pe, self.active, step * self.HID + (e - 1) * self.FO + f + 2)
            last = pe.matmul(self.h_ps[:, f // 2, f % 2], self.w1[:, e, half, f * P:(f + 1) * P],
                             self.ut[:, slot, half], start=(half == 0), stop=(half == 1))
            if n % 4 == 3:
                last.then_inc(self.hidden, 2)

    def activate(self, act, step, e):
        wait(act, self.mixed, step * EXPERTS + e - 1)
        for f in range(self.FO):
            act.wait_ge(self.hidden, step * self.HID + e * self.FO + 2 * (f // 2 + 1))
            act.activation(self.hid[:, e % 2, f], self.h_ps[:, f // 2, f % 2], ACT.Gelu,
                           bias=self.b1c[:, e * self.FO + f:e * self.FO + f + 1]).then_inc(self.active, 1)

    def take(self, dve, step, slot, i, e):
        if e == 0:
            wait(dve, self.stored[slot], 16 * i)
        dve.wait_ge(self.mixed, step * EXPERTS + e + 1)
        dve.tensor_tensor(self.y[:, slot, :, e * D:(e + 1) * D], self.y_ps[:, e % 2],
                          self.b2r[:, e].unsqueeze(1).to_broadcast([P, self.PAIR, D]), ALU.add).then_inc(self.taken, 1)

    def store(self, sp, step, slot):
        sp.wait_ge(self.taken, EXPERTS * (step + 1))
        sp.dma_start(self.y_d[bass.ds(step * self.TOK, self.TOK), :].rearrange("(t p) f -> p t f", p=P),
                     self.y[:, slot]).then_inc(self.stored[slot], 16)

    def stored_all(self, sp):
        for slot in range(2):
            sp.wait_ge(self.stored[slot], 16 * ((self.STEPS + 1 - slot) // 2))


def sort_beside_experts(nc, s, fields, count, bucket_d, rec_d, chunk_tile, experts, weights, room, C):
    MLP, SORT = 2, 4
    rounds = s.steps // SORT
    assert s.steps % SORT == 0 and rounds * MLP < experts.STEPS
    with ExitStack() as ctx:
        sort = EdgeSort(nc, ctx, s, fields, count, bucket_d, rec_d, chunk_tile, C, room)
        block = ctx.enter_context(nc.Block())

        def in_rounds(eng, one_round):
            one_round(0, False)
            with eng.Fori(1, rounds - 1) as i:
                one_round(i, False)
            one_round(rounds - 1, True)

        @block.sync
        def _(sp):
            experts.load_weights(nc, sp, *weights)
            sort.load_keys(sp, 0, 0)

            def one_round(i, last):
                for k in range(SORT):
                    if not (last and k == SORT - 1):
                        sort.load_keys(sp, i * SORT + k + 1, (k + 1) % 2)
                    if k % 2:
                        experts.store(sp, i * MLP + k // 2, k // 2)
            in_rounds(sp, one_round)

        @block.gpsimd
        def _(pool):
            sort.number_chunks(pool)

            def body(i):
                for slot in range(2):
                    sort.scatter(pool, i * 2 + slot, slot)
            peeled(pool, s.steps // 2, body)
            sort.scattered_all(pool)

        @block.tensor
        def _(pe):
            sort.start_pe(pe)
            experts.weights_loaded(pe)

            def one_round(i, last):
                for k in range(SORT):
                    for unit in range(k % 2 * 4, k % 2 * 4 + 4):
                        for n in range(8):
                            experts.product(pe, i * MLP + k // 2, k // 2, i, unit, n)
                    sort.sum_slots(pe, i * SORT + k, k % 2)
            in_rounds(pe, one_round)

        @block.scalar
        def _(act):
            experts.weights_loaded(act)
            experts.load(act, 0, 0)

            def one_round(i, last):
                for k in range(SORT):
                    if k % 2 == 0:
                        experts.load(act, i * MLP + k // 2 + 1, (k // 2 + 1) % 2)
                    for unit in range(k % 2 * 4, k % 2 * 4 + 4):
                        outputs, e = experts.UNITS[unit]
                        if not outputs:
                            experts.activate(act, i * MLP + k // 2, e)
                    sort.stage(act, i * SORT + k, k % 2, i * 2 + k // 2)
            in_rounds(act, one_round)

        @block.vector
        def _(dve):
            chain = C["chain"].on(dve)
            sort.start_dve(dve, chain)

            def take(step, k, i):
                for unit in range(k % 2 * 4, k % 2 * 4 + 4):
                    outputs, e = experts.UNITS[unit]
                    if outputs:
                        experts.take(dve, step, k // 2, i, e)

            def one_round(i, last):
                for k in range(SORT):
                    take(i * MLP + k // 2, k, i)
                    if not (last and k == SORT - 1):
                        nxt = k + 1
                        sort.rank(dve, chain, i * SORT + nxt, nxt % 2, i * 2 + nxt // 2)
                    sort.address(dve, chain, i * SORT + k, k % 2, i * 2 + k // 2)
            experts.weights_loaded(dve)
            sort.rank(dve, chain, 0, 0, 0)
            start = chain.count
            one_round(0, False)
            per = chain.count - start
            with dve.Fori(1, rounds - 1) as i:
                chain.loop = i * per - per
                one_round(i, False)
            chain.count, chain.loop = start + per * (rounds - 1), 0
            one_round(rounds - 1, True)
    return rounds * MLP


def combine(nc, x1_d, y_d, gate, out):
    steps = NT // TG
    with ExitStack() as ctx:
        sb = lambda n, sh, dt: ctx.enter_context(nc.sbuf_tensor(f"co_{n}", sh, dt))
        sem = lambda n: ctx.enter_context(nc.semaphore(f"co_{n}"))
        res = sb("res", [P, 2, TG, D], F32)
        y = sb("y", [P, 2, TG, EXPERTS * D], F32)
        g = sb("g", [P, 2, TG, EXPERTS], F32)
        loaded = [sem("loaded0"), sem("loaded1")]
        stored = [sem("stored0"), sem("stored1")]
        picked, added = sem("picked"), sem("added")
        PER = TG * EXPERTS
        block = ctx.enter_context(nc.Block())

        @block.sync
        def _(sp):
            def body(i):
                for slot in range(2):
                    step = i * 2 + slot
                    wait(sp, added, PER * (step - 1))
                    sp.dma_start(y[:, slot], node_rows(y_d, step)).then_inc(loaded[slot], 16)
                    wait(sp, stored[slot], 16 * i)
                    sp.dma_start(res[:, slot], node_rows(x1_d, step)).then_inc(loaded[slot], 16)
            peeled(sp, steps // 2, body)

        @block.vector
        def _(dve):
            def body(i):
                for slot in range(2):
                    step = i * 2 + slot
                    wait(dve, added, PER * (step - 1))
                    dve.tensor_copy(g[:, slot], gate[:, bass.ds(step * TG, TG), :]).then_inc(picked, 1)
                    dve.wait_ge(picked, step + 1)
                    dve.wait_ge(loaded[slot], 32 * (i + 1))
                    for e in range(EXPERTS):
                        if e:
                            dve.wait_ge(added, PER * step + TG * e)
                        for k in range(TG):
                            dve.scalar_tensor_tensor(out=res[:, slot, k], in0=y[:, slot, k, e * D:(e + 1) * D],
                                                     scalar=g[:, slot, k, e:e + 1], in1=res[:, slot, k],
                                                     op0=ALU.mult, op1=ALU.add).then_inc(added, 1)
            peeled(dve, steps // 2, body)

        @block.scalar
        def _(act):
            def store(step, slot):
                act.wait_ge(added, PER * (step + 1))
                act.dma_start(node_rows(out, step), res[:, slot]).then_inc(stored[slot], 16)

            def body(i):
                store(i * 2, 0)
                store(i * 2 + 1, 1)
            peeled(act, steps // 2 - 1, body)
            store(steps - 2, 0)
            act.wait_ge(added, PER * steps)
            whole = N - LAST
            act.dma_start(out[(steps - 1) * TG * P:whole, :].rearrange("(t p) f -> p t f", p=P),
                          res[:, 1, 0:TG - 1]).then_inc(stored[1], 16)
            act.dma_start(out[whole:N, :], res[0:LAST, 1, TG - 1]).then_inc(stored[1], 16)
            act.wait_ge(stored[0], 16 * (steps // 2))
            act.wait_ge(stored[1], 16 * (steps // 2) + 16)


_INS = ['x', 'src', 'dst', 'edge_weight', 'L0_ffn_W_gat', 'L0_ffn_att_src', 'L0_ffn_att_dst', 'L0_ffn_b_gat',
        'L0_ffn_ln_gamma', 'L0_ffn_ln_beta', 'L0_ffn_W1', 'L0_ffn_b1', 'L0_ffn_W2', 'L0_ffn_b2', 'L0_ffn_edge_index']
_OUTS = [((12500, 256), 'float32')]


def kernel(**inputs):
    import numpy as _np
    import concourse.bacc as _bacc
    from concourse import mybir as _mybir
    from concourse.bass_utils import run_bass_kernel_spmd as _run

    nc = _bacc.Bacc("TRN2", target_bir_lowering=False, num_devices=1)
    arrays, args = {}, []
    for name in _INS:
        a = _np.ascontiguousarray(inputs[name])
        arrays[f"in_{name}_dram"] = a
        args.append(nc.dram_tensor(f"in_{name}_dram", a.shape, _mybir.dt.from_np(a.dtype), kind="ExternalInput").ap())
    for i, (shape, dtype) in enumerate(_OUTS):
        dt = _mybir.dt.from_np(_np.dtype(dtype))
        args.append(nc.dram_tensor(f"out_{i}_dram", shape, dt, kind="ExternalOutput").ap())
    build(nc, *args)
    r = _run(nc, [arrays], core_ids=[0])
    return r.results[0]["out_0_dram"]
```
